# Optimizing a Trainium2 kernel written in Bass

```python
import numpy as np
import jax
import jax.numpy as jnp

def _softmax(x, axis=-1):
    return jax.nn.softmax(x, axis=axis)

def _gelu(x):
    return jax.nn.gelu(x, approximate=True)

def _silu(x):
    return jax.nn.silu(x)

def _sigmoid(x):
    return jax.nn.sigmoid(x)

def _layernorm(x, axis=-1, eps=1e-05):
    m = jnp.mean(x, axis=axis, keepdims=True)
    v = jnp.var(x, axis=axis, keepdims=True)
    return (x - m) / jnp.sqrt(v + eps)

def _scatter_add(tgt, idx, src, axis=0):
    return tgt.at[idx].add(src)

def _segment_sum(src, seg, n):
    return jax.ops.segment_sum(src, seg, n)
kernel_name = 'mk_gps_d2_gnn_r8_fb703a'

def setup_inputs(seed: int=0):
    np.random.seed(seed)
    _w = jnp.asarray

    def _rec_inputs():
        import jax
        import jax.numpy as jnp
        _gk = jax.random.key(seed)
        x = -0.0002117 + 1 * jax.random.normal(jax.random.fold_in(_gk, 1), (6250, 256), jnp.float32)
        _s = jax.random.randint(jax.random.fold_in(_gk, 2), (50000,), 0, 6250, jnp.int32)
        _d = jax.random.randint(jax.random.fold_in(_gk, 3), (50000,), 0, 6250, jnp.int32)
        _loop = jnp.arange(6250, dtype=jnp.int32)
        src = jnp.concatenate([_s, _d, _loop])
        dst = jnp.concatenate([_d, _s, _loop])
        _o = jnp.argsort(dst, stable=True)
        src = src[_o]
        dst = dst[_o]
        return (x, src, dst)
    x, src, dst = _rec_inputs()

    def _L0_gnn_setup():
        import jax, jax.numpy as jnp
        import numpy as np
        NEG_SLOPE = 0.2
        EPS = 1e-16

        def _one_head(x, e0, e1, W_h, a_h, n):
            d = W_h.shape[1]
            h = x @ W_h
            s_dst = h @ a_h[:d]
            s_src = h @ a_h[d:]
            logits = jax.nn.leaky_relu(s_dst[e0] + s_src[e1], NEG_SLOPE)
            m = jax.ops.segment_max(logits, e0, num_segments=n)
            ex = jnp.exp(logits - m[e0])
            denom = jax.ops.segment_sum(ex, e0, num_segments=n) + EPS
            alpha = ex / denom[e0]
            return jax.ops.segment_sum(alpha[:, None] * h[e1], e0, num_segments=n)
        key = jax.random.key(seed)
        k1, k2, k3, k4 = jax.random.split(key, 4)
        N, F_IN, HEADS, D = (12500, 256, 8, 32)
        E = 200000
        x = jax.random.normal(k1, (N, F_IN), dtype=jnp.float32)
        adj = jax.random.randint(k2, (2, E), 0, N, dtype=jnp.int32)
        W = jax.random.normal(k3, (HEADS, F_IN, D), dtype=jnp.float32) / np.sqrt(F_IN)
        a = jax.random.normal(k4, (HEADS, 2 * D), dtype=jnp.float32) / np.sqrt(2 * D)
        return {'input': x, 'adj': adj, 'W': W, 'a': a}
    _L0_gnn_all = _L0_gnn_setup()
    _L0_gnn_in = {k: v for k, v in _L0_gnn_all.items() if k in ('W', 'a')}
    del _L0_gnn_all

    def _L0_mix_setup():
        import jax, jax.numpy as jnp
        import numpy as np
        BN_EPS = 1e-05
        key = jax.random.key(seed)
        ks = jax.random.split(key, 4)
        B, N, D = (8, 1024, 256)
        outD = 256
        s = 1.0 / np.sqrt(D)
        return {'feature': jax.random.normal(ks[0], (B, N, D), dtype=jnp.float32), 'W_qk': jax.random.normal(ks[1], (2, D, D), dtype=jnp.float32) * s, 'b_qk': jnp.zeros((2, D), dtype=jnp.float32), 'W_v': jax.random.normal(ks[2], (D, outD), dtype=jnp.float32) * s, 'b_v': jnp.zeros((outD,), dtype=jnp.float32), 'gamma': jnp.ones((D,), dtype=jnp.float32), 'beta': jnp.zeros((D,), dtype=jnp.float32)}
    _L0_mix_all = _L0_mix_setup()
    _L0_mix_in = {k: v for k, v in _L0_mix_all.items() if k in ('W_qk', 'b_qk', 'W_v', 'b_v', 'gamma', 'beta')}
    del _L0_mix_all

    def _L0_ffn_setup():
        import math
        import jax, jax.numpy as jnp
        import numpy as np
        CAPACITY_FACTOR = 1.25
        key = jax.random.key(seed)
        ks = jax.random.split(key, 5)
        B, L, D, F, E = (8, 1024, 256, 1024, 8)
        h = jax.random.normal(ks[0], (B, L, D), dtype=jnp.float32)
        gate_w = jax.random.normal(ks[1], (D, E), dtype=jnp.float32) * 0.02
        gate_b = jnp.zeros((E,), dtype=jnp.float32)
        w1 = jax.random.normal(ks[2], (E, D, F), dtype=jnp.float32) * (1.0 / math.sqrt(D))
        b1 = jnp.zeros((E, F), dtype=jnp.float32)
        w2 = jax.random.normal(ks[3], (E, F, D), dtype=jnp.float32) * (1.0 / math.sqrt(F))
        b2 = jnp.zeros((E, D), dtype=jnp.float32)
        return {'h': h, 'gate_w': gate_w, 'gate_b': gate_b, 'w1': w1, 'b1': b1, 'w2': w2, 'b2': b2}
    _L0_ffn_all = _L0_ffn_setup()
    _L0_ffn_in = {k: v for k, v in _L0_ffn_all.items() if k in ('gate_w', 'gate_b', 'w1', 'b1', 'w2', 'b2')}
    del _L0_ffn_all

    def _L1_gnn_setup():
        import jax, jax.numpy as jnp
        import numpy as np
        N_NODES = 12500

        def add_self_loops(edge_index, num_nodes):
            loops = jnp.arange(num_nodes, dtype=edge_index.dtype)
            src = jnp.concatenate([edge_index[0], loops])
            dst = jnp.concatenate([edge_index[1], loops])
            return (src, dst)

        def gcn_conv(x, src, dst, W, b, num_nodes):
            ones = jnp.ones(dst.shape[0], dtype=x.dtype)
            deg = jax.ops.segment_sum(ones, dst, num_segments=num_nodes)
            dinv = jnp.where(deg > 0, jax.lax.rsqrt(deg), 0.0)
            norm = dinv[src] * dinv[dst]
            h = x @ W
            msg = h[src] * norm[:, None]
            out = jax.ops.segment_sum(msg, dst, num_segments=num_nodes)
            return out + b
        key = jax.random.key(seed)
        k1, k2, k3, k4 = jax.random.split(key, 4)
        N, C, H, E = (N_NODES, 256, 64, 200000)
        x = jax.random.normal(k1, (N, C), dtype=jnp.float32)
        edge_index = jax.random.randint(k2, (2, E), 0, N, dtype=jnp.int64)
        lim1 = float(np.sqrt(6.0 / (C + H)))
        lim2 = float(np.sqrt(6.0 / (H + C)))
        W1 = jax.random.uniform(k3, (C, H), dtype=jnp.float32, minval=-lim1, maxval=lim1)
        W2 = jax.random.uniform(k4, (H, C), dtype=jnp.float32, minval=-lim2, maxval=lim2)
        b1 = jnp.zeros((H,), dtype=jnp.float32)
        b2 = jnp.zeros((C,), dtype=jnp.float32)
        return {'x': x, 'edge_index': edge_index, 'W1': W1, 'b1': b1, 'W2': W2, 'b2': b2}
    _L1_gnn_all = _L1_gnn_setup()
    _L1_gnn_in = {k: v for k, v in _L1_gnn_all.items() if k in ('W1', 'b1', 'W2', 'b2')}
    del _L1_gnn_all

    def _L1_mix_setup():
        import jax, jax.numpy as jnp
        import numpy as np
        HEADS = 4
        DIM_HEAD = 32
        key = jax.random.key(seed)
        k1, k2, k3 = jax.random.split(key, 3)
        B, L, D = (16, 1024, 256)
        hidden = HEADS * DIM_HEAD
        x = jax.random.normal(k1, (B, L, D), dtype=jnp.float32)
        W_qkv = jax.random.normal(k2, (D, 3 * hidden), dtype=jnp.float32) * D ** (-0.5)
        W_out = jax.random.normal(k3, (hidden, D), dtype=jnp.float32) * hidden ** (-0.5)
        b_out = jnp.zeros((D,), dtype=jnp.float32)
        return {'x': x, 'W_qkv': W_qkv, 'W_out': W_out, 'b_out': b_out}
    _L1_mix_all = _L1_mix_setup()
    _L1_mix_in = {k: v for k, v in _L1_mix_all.items() if k in ('W_qkv', 'W_out', 'b_out')}
    del _L1_mix_all

    def _L1_ffn_setup():
        import jax, jax.numpy as jnp
        import numpy as np
        B, S, D = (8, 512, 256)
        H = 4 * D
        CAPACITY = 0.5
        key = jax.random.key(seed)
        ks = jax.random.split(key, 6)
        x = jax.random.normal(ks[0], (B, S, D), dtype=jnp.float32)
        attention_mask = jnp.zeros((B, 1, 1, S), dtype=jnp.float32)
        wr = jax.random.normal(ks[1], (D, 1), dtype=jnp.float32) * 0.02
        br = jnp.zeros((1,), dtype=jnp.float32)
        w1 = jax.random.normal(ks[2], (D, H), dtype=jnp.float32) * 0.02
        b1 = jnp.zeros((H,), dtype=jnp.float32)
        w2 = jax.random.normal(ks[3], (H, D), dtype=jnp.float32) * 0.02
        b2 = jnp.zeros((D,), dtype=jnp.float32)
        return {'x': x, 'attention_mask': attention_mask, 'wr': wr, 'br': br, 'w1': w1, 'b1': b1, 'w2': w2, 'b2': b2}
    _L1_ffn_all = _L1_ffn_setup()
    _L1_ffn_in = {k: v for k, v in _L1_ffn_all.items() if k in ('attention_mask', 'wr', 'br', 'w1', 'b1', 'w2', 'b2')}
    del _L1_ffn_all
    return {'x': x, 'src': src, 'dst': dst, 'L0_gnn_W': _L0_gnn_in['W'], 'L0_gnn_a': _L0_gnn_in['a'], 'L0_mix_W_qk': _L0_mix_in['W_qk'], 'L0_mix_b_qk': _L0_mix_in['b_qk'], 'L0_mix_W_v': _L0_mix_in['W_v'], 'L0_mix_b_v': _L0_mix_in['b_v'], 'L0_mix_gamma': _L0_mix_in['gamma'], 'L0_mix_beta': _L0_mix_in['beta'], 'L0_ffn_gate_w': _L0_ffn_in['gate_w'], 'L0_ffn_gate_b': _L0_ffn_in['gate_b'], 'L0_ffn_w1': _L0_ffn_in['w1'], 'L0_ffn_b1': _L0_ffn_in['b1'], 'L0_ffn_w2': _L0_ffn_in['w2'], 'L0_ffn_b2': _L0_ffn_in['b2'], 'L1_gnn_W1': _L1_gnn_in['W1'], 'L1_gnn_b1': _L1_gnn_in['b1'], 'L1_gnn_W2': _L1_gnn_in['W2'], 'L1_gnn_b2': _L1_gnn_in['b2'], 'L1_mix_W_qkv': _L1_mix_in['W_qkv'], 'L1_mix_W_out': _L1_mix_in['W_out'], 'L1_mix_b_out': _L1_mix_in['b_out'], 'L1_ffn_attention_mask': _L1_ffn_in['attention_mask'], 'L1_ffn_wr': _L1_ffn_in['wr'], 'L1_ffn_br': _L1_ffn_in['br'], 'L1_ffn_w1': _L1_ffn_in['w1'], 'L1_ffn_b1': _L1_ffn_in['b1'], 'L1_ffn_w2': _L1_ffn_in['w2'], 'L1_ffn_b2': _L1_ffn_in['b2']}

def reference(x, src, dst, L0_gnn_W, L0_gnn_a, L0_mix_W_qk, L0_mix_b_qk, L0_mix_W_v, L0_mix_b_v, L0_mix_gamma, L0_mix_beta, L0_ffn_gate_w, L0_ffn_gate_b, L0_ffn_w1, L0_ffn_b1, L0_ffn_w2, L0_ffn_b2, L1_gnn_W1, L1_gnn_b1, L1_gnn_W2, L1_gnn_b2, L1_mix_W_qkv, L1_mix_W_out, L1_mix_b_out, L1_ffn_attention_mask, L1_ffn_wr, L1_ffn_br, L1_ffn_w1, L1_ffn_b1, L1_ffn_w2, L1_ffn_b2):
    import jax
    import jax.numpy as jnp

    def _L0_gnn_ref(input, adj, W, a):
        import jax, jax.numpy as jnp
        import numpy as np
        NEG_SLOPE = 0.2
        EPS = 1e-16

        def _one_head(x, e0, e1, W_h, a_h, n):
            d = W_h.shape[1]
            h = x @ W_h
            s_dst = h @ a_h[:d]
            s_src = h @ a_h[d:]
            logits = jax.nn.leaky_relu(s_dst[e0] + s_src[e1], NEG_SLOPE)
            m = jax.ops.segment_max(logits, e0, num_segments=n)
            ex = jnp.exp(logits - m[e0])
            denom = jax.ops.segment_sum(ex, e0, num_segments=n) + EPS
            alpha = ex / denom[e0]
            return jax.ops.segment_sum(alpha[:, None] * h[e1], e0, num_segments=n)
        n = input.shape[0]
        e0, e1 = (adj[0], adj[1])
        heads = W.shape[0]
        outs = [_one_head(input, e0, e1, W[h], a[h], n) for h in range(heads)]
        return jnp.concatenate(outs, axis=1)

    def _L0_mix_ref(feature, W_qk, b_qk, W_v, b_v, gamma, beta):
        import jax, jax.numpy as jnp
        import numpy as np
        BN_EPS = 1e-05
        QK = jnp.einsum('bnd,kde->bkne', feature, W_qk) + b_qk[None, :, None, :]
        value = jnp.einsum('bnd,de->bne', feature, W_v) + b_v
        query = QK[:, 0]
        key = QK[:, 1]
        sm = jax.nn.softmax(key, axis=1)
        lam = jnp.einsum('bnd,bne->bde', sm, value)
        mean = jnp.mean(lam, axis=(0, 2), keepdims=True)
        var = jnp.var(lam, axis=(0, 2), keepdims=True)
        bn = (lam - mean) * jax.lax.rsqrt(var + BN_EPS)
        bn = bn * gamma[None, :, None] + beta[None, :, None]
        return jnp.einsum('bnd,bde->bne', query, bn)

    def _L0_ffn_ref(h, gate_w, gate_b, w1, b1, w2, b2):
        import math
        import jax, jax.numpy as jnp
        import numpy as np
        CAPACITY_FACTOR = 1.25
        B, L, D = h.shape
        E = gate_w.shape[1]
        T = B * L
        C = max(1, math.ceil(CAPACITY_FACTOR * T / E))
        x = h.reshape(T, D)
        logits = x @ gate_w + gate_b
        probs = jax.nn.softmax(logits, axis=-1)
        idx = jnp.argmax(probs, axis=-1)
        prb = jnp.take_along_axis(probs, idx[:, None], axis=1)[:, 0]
        one_hot = jax.nn.one_hot(idx, E, dtype=jnp.float32)
        pos = (jnp.cumsum(one_hot, axis=0) * one_hot).sum(-1).astype(jnp.int32) - 1
        kept = pos < C
        pos_safe = jnp.where(kept, pos, C)
        buf = jnp.zeros((E, C, D), dtype=h.dtype).at[idx, pos_safe].set(x, mode='drop')
        hmid = jax.nn.relu(jnp.einsum('ecd,edf->ecf', buf, w1) + b1[:, None, :])
        ybuf = jnp.einsum('ecf,efd->ecd', hmid, w2) + b2[:, None, :]
        pos_g = jnp.minimum(pos, C - 1)
        y_tok = ybuf[idx, pos_g] * (prb * kept)[:, None]
        y = y_tok.reshape(B, L, D)
        y = jnp.nan_to_num(y, nan=0.0, posinf=10000.0, neginf=-10000.0)
        return y

    def _L1_gnn_ref(x, edge_index, W1, b1, W2, b2):
        import jax, jax.numpy as jnp
        import numpy as np
        N_NODES = 12500

        def add_self_loops(edge_index, num_nodes):
            loops = jnp.arange(num_nodes, dtype=edge_index.dtype)
            src = jnp.concatenate([edge_index[0], loops])
            dst = jnp.concatenate([edge_index[1], loops])
            return (src, dst)

        def gcn_conv(x, src, dst, W, b, num_nodes):
            ones = jnp.ones(dst.shape[0], dtype=x.dtype)
            deg = jax.ops.segment_sum(ones, dst, num_segments=num_nodes)
            dinv = jnp.where(deg > 0, jax.lax.rsqrt(deg), 0.0)
            norm = dinv[src] * dinv[dst]
            h = x @ W
            msg = h[src] * norm[:, None]
            out = jax.ops.segment_sum(msg, dst, num_segments=num_nodes)
            return out + b
        N = x.shape[0]
        src, dst = add_self_loops(edge_index, N)
        h = gcn_conv(x, src, dst, W1, b1, N)
        h = jax.nn.relu(h)
        h = gcn_conv(h, src, dst, W2, b2, N)
        return jnp.tanh(h)

    def _L1_mix_ref(x, W_qkv, W_out, b_out):
        import jax, jax.numpy as jnp
        import numpy as np
        HEADS = 4
        DIM_HEAD = 32
        B, L, D = x.shape
        scale = DIM_HEAD ** (-0.5)
        qkv = jnp.einsum('bld,df->blf', x, W_qkv)
        qkv = qkv.reshape(B, L, 3, HEADS, DIM_HEAD)
        q = jnp.transpose(qkv[:, :, 0], (0, 2, 1, 3)) * scale
        k = jax.nn.softmax(jnp.transpose(qkv[:, :, 1], (0, 2, 1, 3)), axis=2)
        v = jnp.transpose(qkv[:, :, 2], (0, 2, 1, 3))
        context = jnp.einsum('bhld,bhle->bhde', k, v)
        out = jnp.einsum('bhde,bhld->bhle', context, q)
        out = jnp.transpose(out, (0, 2, 1, 3)).reshape(B, L, HEADS * DIM_HEAD)
        return jnp.einsum('blf,fd->bld', out, W_out) + b_out

    def _L1_ffn_ref(x, attention_mask, wr, br, w1, b1, w2, b2):
        import jax, jax.numpy as jnp
        import numpy as np
        B, S, D = (8, 512, 256)
        H = 4 * D
        CAPACITY = 0.5
        b, s, d = x.shape
        weights = (jnp.einsum('bsd,do->bso', x, wr) + br)[..., 0]
        k = max(1, int(CAPACITY * s))
        kk = k - 1 if k > 1 else 1
        _, idx = jax.lax.top_k(weights, k)
        sel_idx = idx[:, :kk]
        sel = jnp.take_along_axis(x, sel_idx[:, :, None], axis=1)
        h = jax.nn.gelu(jnp.einsum('bkd,dh->bkh', sel, w1) + b1)
        y = jnp.einsum('bkh,hd->bkd', h, w2) + b2
        w_sel = jnp.take_along_axis(weights, sel_idx, axis=1)
        y = y * w_sel[..., None]
        batch_idx = jnp.arange(b)[:, None]
        processed = jnp.zeros_like(x).at[batch_idx, sel_idx].set(y)
        return processed + x
    edge_index = jnp.stack([src, dst])
    xn = _layernorm(x, axis=-1)
    x = x + _L0_gnn_ref(xn, edge_index, L0_gnn_W, L0_gnn_a) + _L0_mix_ref(xn[None], L0_mix_W_qk, L0_mix_b_qk, L0_mix_W_v, L0_mix_b_v, L0_mix_gamma, L0_mix_beta)[0]
    x = x + _L0_ffn_ref(_layernorm(x, axis=-1)[None], L0_ffn_gate_w, L0_ffn_gate_b, L0_ffn_w1, L0_ffn_b1, L0_ffn_w2, L0_ffn_b2)[0]
    xn = _layernorm(x, axis=-1)
    x = x + _L1_gnn_ref(xn, edge_index, L1_gnn_W1, L1_gnn_b1, L1_gnn_W2, L1_gnn_b2) + _L1_mix_ref(xn[None], L1_mix_W_qkv, L1_mix_W_out, L1_mix_b_out)[0]
    x = x + _L1_ffn_ref(_layernorm(x, axis=-1)[None], L1_ffn_attention_mask, L1_ffn_wr, L1_ffn_br, L1_ffn_w1, L1_ffn_b1, L1_ffn_w2, L1_ffn_b2)[0]
    return x

_drawn_inputs = setup_inputs


def setup_inputs(seed=0):
    import zlib

    import numpy as np

    out = dict(_drawn_inputs(seed))
    spreads = {'L0_mix_b_qk': (0.0, 0.1),
     'L0_mix_b_v': (0.0, 0.1),
     'L0_mix_gamma': (1.0, 0.2),
     'L0_mix_beta': (0.0, 0.1),
     'L0_ffn_gate_b': (0.0, 0.8),
     'L0_ffn_b1': (0.0, 0.8),
     'L0_ffn_b2': (0.0, 2.0),
     'L1_gnn_b1': (0.0, 2.0),
     'L1_gnn_b2': (0.0, 2.0),
     'L1_mix_b_out': (0.0, 2.0),
     'L1_ffn_b1': (0.0, 0.8),
     'L1_ffn_b2': (0.0, 0.8)}
    factors = {'L0_gnn_W': 3.324,
     'L0_gnn_a': 6.229,
     'L0_ffn_gate_w': 8.0,
     'L0_ffn_w1': 8.0,
     'L0_ffn_w2': 8.0,
     'L1_gnn_W1': 8.0,
     'L1_gnn_W2': 7.978,
     'L1_mix_W_qkv': 2.67,
     'L1_ffn_wr': 8.0,
     'L1_ffn_w1': 8.0,
     'L1_ffn_w2': 8.0}
    for name, (base, spread) in spreads.items():
        noise = np.random.default_rng([zlib.crc32(name.encode()), seed]).standard_normal(out[name].shape)
        drawn = base * np.exp(spread * noise) if base else spread * noise
        out[name] = jnp.asarray(drawn.astype(out[name].dtype))
    for name, factor in factors.items():
        out[name] = (out[name] * factor).astype(out[name].dtype)
    return out
```

```python
from contextlib import ExitStack

import concourse.bass as bass
from concourse import mybir

ALU = mybir.AluOpType
ACT = mybir.ActivationFunctionType
AX = mybir.AxisListType
F32 = mybir.dt.float32
BF16 = mybir.dt.bfloat16
I32 = mybir.dt.int32

P = 128
N, D = 6250, 256
NB = -(-N // P)
LAST = N - (NB - 1) * P
PAIRS = (NB - 1) // 2
DC = D // P
E_ALL = 106250
EP, ET = 125, 850
GRP = 5
LOOPS = ET // (2 * GRP)
RING = 5
GROUPS = ET // GRP
TILES = 880
SLOTS = TILES * P
TGRP = 4
TRING = 5
TGROUPS = TILES // TGRP
assert TGROUPS % TRING == 0 and GROUPS % RING == 0
HEADS, HD = 8, 32
ROW = D + HEADS
GH = 64
EXPERTS, FF = 8, 1024
FC = FF // P
CAP = 977
EGROUP = 489
EROWS = 2 * EGROUP
TOPK = N // 2 - 1
CGROUP = 448
CROWS = 7 * CGROUP
BIG = 1.0e30
LN_EPS = 1e-05


class Buffers:
    pass


class Graph:

    def __init__(self, table, other, local, block, count, last):
        self.table, self.other, self.local = table, other, local
        self.block, self.count, self.last = block, count, last


class Chain:

    def __init__(self, eng, sem, base=0):
        self.eng, self.sem, self.base, self.n = eng, sem, base, 0

    def __call__(self, ins):
        self.n += 1
        ins.then_inc(self.sem, 1)
        self.eng.wait_ge(self.sem, self.base + self.n)


def rounds(eng, groups, width, step):
    for j in range(width):
        step(j, j)
    with eng.Fori(1, groups // width, 1) as i:
        for j in range(width):
            step(i * width + j, j)


def has(g, groups):
    return not isinstance(g, int) or 0 <= g < groups


def staged(eng, groups, width, step, drain=0):
    for b in range(width):
        step(b, b, 0)
    with eng.Fori(1, groups // width - 1, 1) as i:
        for b in range(width):
            step(i * width + b, b, i)
    for b in range(width + drain):
        step(groups - width + b, b % width, groups // width - 1 + b // width)




def wait_past(eng, sem, value):
    if not isinstance(value, int) or value > 0:
        eng.wait_ge(sem, value)


class Phase:

    def __init__(self, nc, name):
        self.nc, self.name, self.stack, self.sems = nc, name, ExitStack(), []

    def sb(self, name, shape, dt=F32):
        return self.stack.enter_context(self.nc.sbuf_tensor(f"{self.name}_{name}", shape, dt))

    def ps(self, name, shape, dt=F32):
        return self.stack.enter_context(self.nc.psum_tensor(f"{self.name}_{name}", shape, dt))

    def sem(self, name):
        s = self.nc.alloc_semaphore(f"{self.name}_{name}")
        self.sems.append(s)
        return s

    def __enter__(self):
        return self

    def __exit__(self, *error):
        if error[0] is None:
            self.nc.clear_and_free_semaphores(self.sems)
            self.nc.all_engine_barrier()
        self.stack.close()


def constants(nc, k):
    with Phase(nc, "const") as ph:
        made, ramp = ph.sem("made"), ph.sem("ramp")
        valid_set = ph.sem("valid_set")
        token_i = ph.sb("token_i", [P, NB], I32)
        ramp_i = ph.sb("ramp_i", [P, TILES], I32)
        with nc.Block() as block:

            @block.gpsimd
            def _(pool):
                pool.memset(k.ident[:, :], 0.0).then_inc(made, 1)
                pool.memset(k.upper[:, :], 1.0).then_inc(made, 1)
                pool.memset(k.ones[:, :], 1.0).then_inc(made, 1)
                pool.memset(k.valid[:, :], 1.0).then_inc(valid_set, 1)
                pool.wait_ge(valid_set, 1)
                pool.affine_select(out=k.valid[:, NB - 1:NB], in_=k.valid[:, NB - 1:NB], compare_op=ALU.is_ge, fill=0.0,
                                   base=LAST - 1, pattern=[[0, 1]], channel_multiplier=-1).then_inc(valid_set, 1)
                pool.iota(token_i[:, :], [[P, NB]], base=0, channel_multiplier=1).then_inc(valid_set, 1)
                pool.iota(ramp_i[:, :], [[1, TILES]], base=0, channel_multiplier=0).then_inc(ramp, 1)
                pool.wait_ge(made, 3)
                pool.affine_select(out=k.ident[:, :], in_=k.ident[:, :], compare_op=ALU.not_equal, fill=1.0,
                                   base=0, pattern=[[-1, P]], channel_multiplier=1).then_inc(made, 1)
                pool.affine_select(out=k.upper[:, :], in_=k.upper[:, :], compare_op=ALU.is_gt, fill=0.0,
                                   base=0, pattern=[[1, P]], channel_multiplier=-1).then_inc(made, 1)

            @block.vector
            def _(dve):
                dve.wait_ge(ramp, 1)
                nc.vector.tensor_copy(k.ramp[:, :], ramp_i[:, :])
                dve.wait_ge(valid_set, 3)
                nc.vector.tensor_copy(k.token[:, :], token_i[:, :])
                nc.vector.memset(k.eps[:, :], LN_EPS)
                nc.vector.memset(k.zeros_b[:, :], 0.0)
                nc.vector.memset(k.eps16[:, :], 1e-16)
                dve.wait_ge(made, 5)
                nc.vector.tensor_copy(k.ident_b[:, :], k.ident[:, :])


def load_x(nc, k):
    with Phase(nc, "load") as ph:
        zeroed, loaded = ph.sem("zeroed"), ph.sem("loaded")
        with nc.Block() as block:

            @block.vector
            def _(dve):
                nc.vector.memset(k.X[:, NB - 1, :], 0.0).then_inc(zeroed, 1)

            @block.sync
            def _(sp):
                sp.dma_start(k.X[:, 0:NB - 1, :],
                             k.x[0:(NB - 1) * P, :].rearrange("(t p) d -> p t d", p=P)).then_inc(loaded, 16)
                sp.wait_ge(zeroed, 1)
                sp.dma_start(k.X[0:LAST, NB - 1, :], k.x[(NB - 1) * P:N, :]).then_inc(loaded, 16)
                sp.wait_ge(loaded, 32)


def flat(ap):
    return ap.rearrange("p a d -> p (a d)")


class Tokens:

    def __init__(self, nc, k, ph, norm=True):
        self.nc, self.k, self.norm = nc, k, norm
        self.xn = [ph.sb(f"xn{b}", [P, D]) for b in range(2)]
        self.xnT = [ph.sb(f"xnT{b}", [P, DC, P]) for b in range(2)]
        self.stats = [ph.sb(f"stats{b}", [P, 6]) for b in range(2)]
        self.meanvar = [ph.sb(f"meanvar{b}", [P, 2]) for b in range(2)]
        self.std = [ph.sb(f"std{b}", [P, 2]) for b in range(2)]
        self.ps_turn = [ph.ps(f"ps_turn{b}", [P, 512]) for b in range(2)]
        self.var_ok = [ph.sem(f"var_ok{b}") for b in range(2)]
        self.std_ok = [ph.sem(f"std_ok{b}") for b in range(2)]
        self.xn_ok = [ph.sem(f"xn_ok{b}") for b in range(2)]
        self.xn_saved = [ph.sem(f"xn_saved{b}") for b in range(2)]
        self.turned = [ph.sem(f"turned{b}") for b in range(2)]
        self.xnT_ok = [ph.sem(f"xnT_ok{b}") for b in range(2)]
        self.projected = [ph.sem(f"projected{b}") for b in range(2)]
        self.dve_done = [ph.sem(f"dve_done{b}") for b in range(2)]
        self.act_done = [ph.sem(f"act_done{b}") for b in range(2)]
        self.stats_ok = ph.sem("stats_ok")
        self.dve_going = ph.sem("dve_going")

    def blocks(self, eng, step):
        with eng.Fori(0, PAIRS, 1) as i:
            for b in range(2):
                step(i, i * 2 + b, b, P)
        step(PAIRS, NB - 1, 0, LAST)

    def skewed(self, eng, first, second):
        first(0, 0, 0, P)
        with eng.Fori(0, PAIRS, 1) as i:
            first(i, i * 2 + 1, 1, P)
            second(i, i * 2, 0, P)
            first(i + 1, i * 2 + 2, 0, P)
            second(i, i * 2 + 1, 1, P)
        second(PAIRS, NB - 1, 0, LAST)

    def vector(self, dve, post, before=None):
        nc, k = self.nc, self.k

        def normalise(i, t, b, rows):
            if before:
                before(i, t, b, rows)
            if not self.norm:
                return
            x = flat(k.X[:, bass.ds(t, 1), :])
            dve.wait_ge(self.xn_saved[b], i)
            dve.wait_ge(self.turned[b], i)
            link = Chain(dve, self.stats_ok, t * 2)
            dve.sem_inc(self.dve_going, 1)
            link(nc.vector.bn_stats(self.stats[b][:, :], x))
            dve.sem_inc(self.dve_going, 1)
            nc.vector.bn_aggr(self.meanvar[b][:, :], self.stats[b][:, :]).then_inc(self.var_ok[b], 1)
            dve.wait_ge(self.std_ok[b], i + 1)
            link(nc.vector.reciprocal(self.std[b][:, 1:2], self.std[b][:, 0:1]))
            nc.vector.tensor_scalar(self.xn[b][:, :], x, self.meanvar[b][:, 0:1], self.std[b][:, 1:2],
                                    ALU.subtract, ALU.mult).then_inc(self.xn_ok[b], 1)

        def after(i, t, b, rows):
            dve.wait_ge(self.projected[b], i + 1)
            post(i, t, b, rows).then_inc(self.dve_done[b], 1)

        self.skewed(dve, normalise, after)

    def scalar(self, act, post=None):
        nc, k = self.nc, self.k

        def root(i, t, b, rows):
            if self.norm:
                act.wait_ge(self.var_ok[b], i + 1)
                act.wait_ge(self.xn_ok[b], i)
                nc.scalar.activation(self.std[b][:, 0:1], self.meanvar[b][:, 1:2], ACT.Sqrt,
                                     bias=k.eps[:, 0:1]).then_inc(self.std_ok[b], 1)

        def copies(i, t, b, rows):
            saved = flat(k.XN[:, bass.ds(t, 1), :])
            if self.norm:
                act.wait_ge(self.xn_ok[b], i + 1)
                nc.scalar.copy(saved, self.xn[b][:, :]).then_inc(self.xn_saved[b], 1)
            else:
                act.wait_ge(self.turned[b], i)
                nc.scalar.copy(self.xn[b][:, :], saved).then_inc(self.xn_ok[b], 1)
            act.wait_ge(self.turned[b], i + 1)
            act.wait_ge(self.projected[b], i)
            nc.scalar.copy(self.xnT[b][:, :, :].rearrange("p c n -> p (c n)"),
                           self.ps_turn[b][:, 0:D]).then_inc(self.xnT_ok[b], 1)
            if post:
                act.wait_ge(self.projected[b], i + 1)
                post(i, t, b, rows).then_inc(self.act_done[b], 1)

        self.skewed(act, root, copies)

    def tensor(self, pe, project, act_posts=False):
        nc, k = self.nc, self.k

        def turn(i, t, b, rows):
            pe.wait_ge(self.xn_ok[b], i + 1)
            pe.wait_ge(self.xnT_ok[b], i)
            for c in range(DC):
                last = nc.tensor.transpose(self.ps_turn[b][:, c * P:(c + 1) * P],
                                           self.xn[b][:, c * P:(c + 1) * P], k.ident[:, :])
            last.then_inc(self.turned[b], 1)

        def products(i, t, b, rows):
            pe.wait_ge(self.xnT_ok[b], i + 1)
            pe.wait_ge(self.dve_done[b], i)
            if act_posts:
                pe.wait_ge(self.act_done[b], i)
            project(i, t, b, rows).then_inc(self.projected[b], 1)

        self.skewed(pe, turn, products)


def load_columns(sp, sem, dst, src):
    for c in range(DC):
        sp.dma_start(dst[:, c:c + 1], src[c * P:(c + 1) * P].rearrange("(p a) -> p a", a=1)).then_inc(sem, 16)


def load_matrix(sp, sem, dst, src):
    sp.dma_start(dst, src.rearrange("(c p) n -> p c n", p=P)).then_inc(sem, 16)


def sort_edges(nc, k, name, keys, others, out):
    HI, LO = NB, P
    with Phase(nc, name) as ph:
        key_i, other_i = ph.sb("key_i", [EP, ET], I32), ph.sb("other_i", [EP, ET], I32)
        hi_i, lo_i = ph.sb("hi_i", [EP, ET], I32), ph.sb("lo_i", [EP, ET], I32)
        hi, lo = ph.sb("hi", [EP, ET]), ph.sb("lo", [EP, ET])
        pairs = ph.sb("pairs", [EP, ET, 2])
        free = ph.sb("free", [P, TILES, 2])
        is_hi = [ph.sb(f"is_hi{b}", [EP, GRP, HI], BF16) for b in range(RING)]
        is_lo = [ph.sb(f"is_lo{b}", [EP, GRP, LO], BF16) for b in range(RING)]
        counts = ph.sb("counts", [HI, LO])
        starts = ph.sb("starts", [HI, LO])
        upto = ph.sb("upto", [HI, LO])
        ones_row = ph.sb("ones_row", [HI, LO])
        tiles_i = ph.sb("tiles_i", [HI, 1], I32)
        tiles = ph.sb("tiles", [HI, 4])
        past = ph.sb("past", [HI, TILES])
        block_f = ph.sb("block_f", [P, TILES])
        ps_h = ph.ps("ps_h", [P, 512])
        ps_a = [ph.ps(f"ps_a{q}", [P, 512]) for q in range(2)]
        ps_p = [ph.ps(f"ps_p{q}", [P, 512]) for q in range(2)]
        ps_t = ph.ps("ps_t", [P, 1024], BF16)

        loaded, filled, free_set, split, chain = (ph.sem(s) for s in ("loaded", "filled", "free_set", "split", "chain"))
        onehot = [ph.sem(f"onehot{b}") for b in range(2)]
        counted = [ph.sem(f"counted{b}") for b in range(2)]
        mid_pe, mid_dve = ph.sem("mid_pe"), ph.sem("mid_dve")

        def one_hots(g, b):
            cols = bass.ds(g * GRP, GRP)
            nc.vector.tensor_tensor(is_hi[b][:, :, :], k.ramp[0:EP, 0:HI].unsqueeze(1).to_broadcast([EP, GRP, HI]),
                                    hi[:, cols].unsqueeze(2).to_broadcast([EP, GRP, HI]), ALU.is_equal)
            return nc.vector.tensor_tensor(is_lo[b][:, :, :], k.ramp[0:EP, 0:LO].unsqueeze(1).to_broadcast([EP, GRP, LO]),
                                           lo[:, cols].unsqueeze(2).to_broadcast([EP, GRP, LO]), ALU.is_equal)

        with nc.Block() as block:

            @block.sync
            def _(sp):
                sp.dma_start(key_i[:, :], keys.rearrange("(p t) -> p t", p=EP)).then_inc(loaded, 16)
                sp.dma_start(other_i[:, :], others.rearrange("(p t) -> p t", p=EP)).then_inc(loaded, 16)
                sp.wait_ge(free_set, 2)
                sp.dma_start(out.table.rearrange("(p t) a -> p t a", p=P), free[:, :, :]).then_inc(filled, 16)
                sp.wait_ge(filled, 16)

            @block.vector
            def _(dve):
                nc.vector.memset(free[:, :, 0], 0.0).then_inc(free_set, 1)
                nc.vector.memset(free[:, :, 1], -1.0).then_inc(free_set, 1)
                nc.vector.memset(ones_row[:, :], 1.0)
                nc.vector.memset(out.local[:, TILES:], -1.0)
                dve.wait_ge(loaded, 32)
                nc.vector.tensor_single_scalar(hi_i[:, :], key_i[:, :], 7, ALU.arith_shift_right).then_inc(split, 1)
                nc.vector.tensor_single_scalar(lo_i[:, :], key_i[:, :], LO - 1, ALU.bitwise_and).then_inc(split, 1)
                nc.vector.tensor_copy(pairs[:, :, 0], other_i[:, :]).then_inc(split, 1)
                nc.vector.tensor_copy(pairs[:, :, 1], key_i[:, :]).then_inc(split, 1)
                dve.wait_ge(split, 4)
                nc.vector.tensor_copy(hi[:, :], hi_i[:, :]).then_inc(split, 1)
                nc.vector.tensor_copy(lo[:, :], lo_i[:, :]).then_inc(split, 1)
                dve.wait_ge(split, 6)
                with dve.Fori(0, LOOPS, 1) as i:
                    for b in range(2):
                        dve.wait_ge(counted[b], i)
                        one_hots(i * 2 + b, b).then_inc(onehot[b], 1)

                link = Chain(dve, chain)
                for b in range(2):
                    dve.wait_ge(counted[b], LOOPS)
                link(nc.vector.tensor_copy(counts[:, :], ps_h[0:HI, 0:LO]))
                link(nc.vector.tensor_tensor_scan(upto[:, :], ones_row[:, :], counts[:, :], 0.0, ALU.mult, ALU.add))
                link(nc.vector.tensor_scalar(tiles_i[:, :], upto[:, LO - 1:LO], 127.0, None, ALU.add))
                link(nc.vector.tensor_single_scalar(tiles_i[:, :], tiles_i[:, :], 7, ALU.arith_shift_right))
                nc.vector.tensor_copy(tiles[:, 0:1], tiles_i[:, :]).then_inc(mid_dve, 1)
                dve.wait_ge(mid_dve, 1)
                dve.wait_ge(mid_pe, 1)
                link(nc.vector.tensor_tensor(tiles[:, 1:2], ps_h[0:HI, 256:257], tiles[:, 0:1], ALU.add))
                link(nc.vector.tensor_scalar(tiles[:, 2:3], ps_h[0:HI, 256:257], float(P), None, ALU.mult))
                nc.vector.tensor_scalar(past[:, :], k.ramp[0:HI, :], tiles[:, 1:2], None, ALU.is_ge).then_inc(mid_dve, 1)
                link(nc.vector.tensor_scalar(upto[:, :], upto[:, :], tiles[:, 2:3], None, ALU.add))
                link(nc.vector.tensor_tensor(starts[:, :], upto[:, :], counts[:, :], ALU.subtract))
                link(nc.vector.tensor_scalar(upto[:, :], upto[:, :], -1.0, 0.0, ALU.add, ALU.max))
                nc.vector.tensor_copy(tiles[:, 3:4], tiles[:, 2:3]).then_inc(mid_dve, 1)
                dve.wait_ge(mid_pe, 2)
                for q in range(2):
                    w = min(512, TILES - 512 * q)
                    nc.vector.tensor_copy(block_f[:, 512 * q:512 * q + w], ps_a[q][:, 0:w])
                    nc.vector.tensor_copy(out.block[0:1, 512 * q:512 * q + w], ps_a[q][0:1, 0:w])
                nc.vector.tensor_copy(out.count[:, :], ps_p[0][:, 0:HI])
                nc.vector.tensor_copy(out.last[:, :], ps_p[0][:, 64:64 + HI])

            @block.tensor
            def _(pe):
                nc.tensor.matmul(ps_h[0:HI, 0:LO], k.zeros_b[:, 0:HI], k.ident_b[:, :], start=True, stop=False,
                                 skip_group_check=True)
                with pe.Fori(0, LOOPS, 1) as i:
                    for b in range(2):
                        pe.wait_ge(onehot[b], i + 1)
                        for j in range(GRP):
                            last = nc.tensor.matmul(ps_h[0:HI, 0:LO], is_hi[b][:, j, :], is_lo[b][:, j, :],
                                                    start=False, stop=False, skip_group_check=True)
                        last.then_inc(counted[b], 1)
                pe.wait_ge(mid_dve, 1)
                nc.tensor.matmul(ps_h[0:HI, 256:257], k.upper[0:HI, 0:HI], tiles[:, 0:1], start=True, stop=True,
                                 skip_group_check=True).then_inc(mid_pe, 1)
                pe.wait_ge(mid_dve, 3)
                for q in range(2):
                    w = min(512, TILES - 512 * q)
                    nc.tensor.matmul(ps_a[q][:, 0:w], k.ones[0:HI, :], past[:, 512 * q:512 * q + w], start=True, stop=True)
                nc.tensor.transpose(ps_p[0][:, 0:HI], counts[:, :], k.ident[0:HI, 0:HI])
                nc.tensor.transpose(ps_p[0][:, 64:64 + HI], upto[:, :], k.ident[0:HI, 0:HI]).then_inc(mid_pe, 1)

        hots, turned, turn_ok = ph.sem("hots"), ph.sem("turned"), ph.sem("turn_ok")
        same_ok, earlier_ok = ph.sem("same_ok"), ph.sem("earlier_ok")
        state_new, state_ok = ph.sem("state_new"), ph.sem("state_ok")
        looked, placed, step = ph.sem("looked"), ph.sem("placed"), ph.sem("step")
        picked_ok = ph.sem("picked_ok")
        scattered = [[ph.sem(f"scattered{b}_{j}") for j in range(GRP)] for b in range(RING)]
        hiT = [ph.sb(f"hiT{b}", [HI, GRP, EP]) for b in range(RING)]
        hiT_b = [ph.sb(f"hiT_b{b}", [HI, GRP, EP], BF16) for b in range(RING)]
        state = [ph.sb(f"state{b}", [HI, GRP, LO]) for b in range(RING)]
        earlier = [ph.sb(f"earlier{b}", [EP, GRP, EP], BF16) for b in range(RING)]
        picked = ph.sb("picked", [EP, GRP, LO])
        place_f = ph.sb("place_f", [EP, GRP])
        place = [ph.sb(f"place{b}", [EP, GRP], I32) for b in range(RING)]
        row = [ph.sb(f"row{b}", [EP, GRP, 2]) for b in range(RING)]
        pe_going, pool_going = ph.sem("pe_going"), ph.sem("pool_going")
        HALF = 4

        with nc.Block() as block:

            @block.vector
            def _(dve):
                def compare(g, b):
                    dve.wait_ge(same_ok, g + 1)
                    for q, n in ((0, HALF), (1, GRP - HALF)):
                        last = nc.vector.tensor_tensor(
                            earlier[b][:, q * HALF:q * HALF + n, :],
                            ps_a[q][0:EP, 0:n * P].rearrange("p (n e) -> p n e", n=n)[:, :, 0:EP],
                            k.upper[0:EP, 0:EP].unsqueeze(1).to_broadcast([EP, n, EP]), ALU.mult)
                    last.then_inc(earlier_ok, 1)

                def pick(g, b):
                    dve.wait_ge(looked, g + 1)
                    wait_past(dve, step, g)
                    for q, n in ((0, HALF), (1, GRP - HALF)):
                        last = nc.vector.tensor_tensor(
                            picked[:, q * HALF:q * HALF + n, :],
                            ps_p[q][0:EP, 0:n * LO].rearrange("p (n e) -> p n e", n=n),
                            is_lo[b][:, q * HALF:q * HALF + n, :], ALU.mult)
                    last.then_inc(picked_ok, 1)

                def places(g, b, i):
                    dve.wait_ge(picked_ok, g + 1)
                    wait_past(dve, placed, g)
                    nc.vector.tensor_reduce(place_f[:, :], picked[:, :, :], AX.X, ALU.add).then_inc(step, 1)
                    if not isinstance(g, int) or g >= RING:
                        for j in range(GRP):
                            dve.wait_ge(scattered[b][j], i * 16)
                    nc.vector.tensor_copy(row[b][:, :, :], pairs[:, bass.ds(g * GRP, GRP), :])
                    dve.wait_ge(step, g + 1)
                    nc.vector.tensor_copy(place[b][:, :], place_f[:, :]).then_inc(placed, 1)

                def group(g, b, i):
                    written = (g - 2, (b - 2) % RING, i + (b - 2) // RING)
                    if has(g - 2, GROUPS):
                        pick(written[0], written[1])
                    if has(g, GROUPS):
                        compare(g, b)
                    if has(g - 2, GROUPS):
                        places(*written)
                    if has(g + 2, GROUPS):
                        one_hots(g + 2, (b + 2) % RING).then_inc(hots, 1)

                for g in range(2):
                    one_hots(g, g).then_inc(hots, 1)
                staged(dve, GROUPS, RING, group, drain=2)

            @block.scalar
            def _(act):
                def turn(g, b):
                    act.wait_ge(turned, g + 1)
                    hot = ps_t[0:HI, 0:GRP * P].rearrange("p (n e) -> p n e", n=GRP)[:, :, 0:EP]
                    nc.scalar.copy(hiT_b[b][:, :, :], hot)
                    nc.scalar.copy(hiT[b][:, :, :], hot).then_inc(turn_ok, 1)

                def group(g, b, i):
                    for j in range(GRP):
                        act.wait_ge(state_new, g * GRP + j + 1)
                        nc.scalar.copy(state[b][:, j, :], ps_h[0:HI, 0:LO]).then_inc(state_ok, 1)
                        if j == 0 and has(g + 1, GROUPS):
                            turn(g + 1, (b + 1) % RING)

                turn(0, 0)
                staged(act, GROUPS, RING, group)

            @block.tensor
            def _(pe):
                nc.tensor.matmul(ps_h[0:HI, 0:LO], k.ident[0:HI, 0:HI], starts[:, :], start=True, stop=False,
                                 skip_group_check=True).then_inc(state_new, 1)

                def turn(g, b):
                    pe.wait_ge(hots, g + 1)
                    wait_past(pe, turn_ok, g)
                    pe.sem_inc(pe_going, 1)
                    for j in range(GRP):
                        last = nc.tensor.transpose(ps_t[0:HI, j * P:j * P + EP], is_hi[b][:, j, :], k.ident_b[0:EP, 0:EP])
                    last.then_inc(turned, 1)

                def compare(g, b, tiles):
                    if tiles[0] == 0:
                        pe.wait_ge(turn_ok, g + 1)
                        wait_past(pe, earlier_ok, g)
                    for j in tiles:
                        q, r = j // HALF, j % HALF
                        last = nc.tensor.matmul(ps_a[q][0:EP, r * P:r * P + EP], hiT_b[b][:, j, :], hiT_b[b][:, j, :],
                                                start=True, stop=True)
                    if tiles[-1] == GRP - 1:
                        last.then_inc(same_ok, 1)

                def count(g, b, j):
                    pe.wait_ge(state_ok, g * GRP + j + 1)
                    nc.tensor.matmul(ps_h[0:HI, 0:LO], is_hi[b][:, j, :], is_lo[b][:, j, :], start=False, stop=False,
                                     skip_group_check=True).then_inc(state_new, 1)

                def lookup(g, b, tiles):
                    if tiles[0] == 0:
                        pe.wait_ge(earlier_ok, g + 1)
                        wait_past(pe, picked_ok, g)
                    for j in tiles:
                        q, r = j // HALF, j % HALF
                        cols = ps_p[q][0:EP, r * LO:(r + 1) * LO]
                        nc.tensor.matmul(cols, hiT[b][:, j, :], state[b][:, j, :], start=True, stop=False)
                        last = nc.tensor.matmul(cols, earlier[b][:, j, :], is_lo[b][:, j, :], start=False, stop=True)
                    if tiles[-1] == GRP - 1:
                        last.then_inc(looked, 1)

                def group(g, b, i):
                    here, ahead, behind = has(g, GROUPS), has(g + 1, GROUPS), has(g - 1, GROUPS)
                    nxt, prev = (b + 1) % RING, (b - 1) % RING
                    if ahead:
                        turn(g + 1, nxt)
                    if here:
                        count(g, b, 0)
                    if behind:
                        lookup(g - 1, prev, [0, 1])
                    if here:
                        count(g, b, 1)
                    if behind:
                        lookup(g - 1, prev, [2, 3, 4])
                    if here:
                        count(g, b, 2)
                    if ahead:
                        compare(g + 1, nxt, [0, 1, 2])
                    if here:
                        count(g, b, 3)
                    if ahead:
                        compare(g + 1, nxt, [3, 4])
                    if here:
                        count(g, b, 4)

                turn(0, 0)
                compare(0, 0, list(range(GRP)))
                staged(pe, GROUPS, RING, group, drain=1)

            @block.gpsimd
            def _(pool):
                def group(g, b):
                    pool.wait_ge(placed, g + 1)
                    pool.sem_inc(pool_going, 1)
                    for j in range(GRP):
                        pool.indirect_dma_start(out=out.table, out_offset=bass.IndirectOffsetOnAxis(ap=place[b][:, j:j + 1], axis=0),
                                                in_=row[b][:, j, :], in_offset=None).then_inc(scattered[b][j], 16)

                rounds(pool, GROUPS, RING, group)
                for b in range(RING):
                    for j in range(GRP):
                        pool.wait_ge(scattered[b][j], GROUPS // RING * 16)

        CH = -(-TILES // P)
        tab = ph.sb("tab", [P, CH, 2 * P])
        reloaded, turned2, moved = ph.sem("reloaded"), ph.sem("turned2"), ph.sem("moved")
        with nc.Block() as block:

            @block.sync
            def _(sp):
                t = out.table.rearrange("(t p) a -> t (p a)", p=P)
                for c in range(CH):
                    n = min(P, TILES - c * P)
                    sp.dma_start(tab[0:n, c, :], t[c * P:c * P + n, :]).then_inc(reloaded, 16)

            @block.tensor
            def _(pe):
                pe.wait_ge(reloaded, 16 * CH)
                for c in range(CH):
                    n = min(P, TILES - c * P)
                    pe.wait_ge(moved, c)
                    for a in range(2):
                        last = nc.tensor.transpose(ps_a[0][:, a * P:a * P + n],
                                                   tab[0:n, c, :].rearrange("t (p a) -> t a p", a=2)[:, a, :], k.ident[0:n, 0:n])
                    last.then_inc(turned2, 1)

            @block.vector
            def _(dve):
                nc.vector.tensor_scalar(block_f[:, :], block_f[:, :], float(P), None, ALU.mult).then_inc(mid_dve, 1)
                dve.wait_ge(mid_dve, 4)
                for c in range(CH):
                    n = min(P, TILES - c * P)
                    dve.wait_ge(turned2, c + 1)
                    nc.vector.tensor_copy(out.other[:, c * P:c * P + n], ps_a[0][:, 0:n])
                    nc.vector.tensor_tensor(out.local[:, c * P:c * P + n], ps_a[0][:, P:P + n],
                                            block_f[:, c * P:c * P + n], ALU.subtract).then_inc(moved, 1)


def attention_tables(nc, k):
    with Phase(nc, "l0") as ph:
        wcat = ph.sb("wcat", [P, DC, D + 16])
        wh = ph.sb("wh", [P, DC, D])
        whT = ph.sb("whT", [P, DC, D])
        amat = ph.sb("amat", [P, DC, 16])
        bias_k = ph.sb("bias_k", [1, D + 16])
        bias_q = ph.sb("bias_q", [P, DC])
        bias_v = ph.sb("bias_v", [1, D])
        gamma = ph.sb("gamma", [P, DC])
        beta = ph.sb("beta", [P, DC])
        wq = ph.sb("wq", [P, DC, D])
        wqT = ph.sb("wqT", [P, DC, D])
        wv = ph.sb("wv", [P, DC, D])
        keys = ph.sb("keys", [P, NB, D])
        kmax = ph.sb("kmax", [P, D])
        rows_out = [ph.sb(f"rows{b}", [P, ROW]) for b in range(2)]
        ps_k = [ph.ps(f"ps_k{b}", [P, 512]) for b in range(2)]
        ps_h = [ph.ps(f"ps_h{b}", [P, 512]) for b in range(2)]
        ps_m = ph.ps("ps_m", [P, 2, 512])
        tok = Tokens(nc, k, ph)

        loaded, cleared = ph.sem("loaded"), ph.sem("cleared")
        w_products, w_copied, score_w = ph.sem("w_products"), ph.sem("w_copied"), ph.sem("score_w")
        row_out = [ph.sem(f"row_out{b}") for b in range(2)]
        n_loads = 3 + DC + 2 + 3 * DC + 2 * HEADS

        with nc.Block() as block:

            @block.sync
            def _(sp):
                sp.wait_ge(cleared, 1)
                load_matrix(sp, loaded, wcat[:, :, 0:D], k.W_qk[1])
                load_matrix(sp, loaded, wq[:, :, :], k.W_qk[0])
                load_matrix(sp, loaded, wv[:, :, :], k.W_v)
                for c in range(DC):
                    sp.dma_start(wh[:, c, :].rearrange("p (h d) -> p h d", h=HEADS),
                                 k.gnn_W[:, c * P:(c + 1) * P, :].rearrange("h p d -> p h d")).then_inc(loaded, 16)
                sp.dma_start(bias_k[:, 0:D], k.b_qk[1:2, :]).then_inc(loaded, 16)
                sp.dma_start(bias_v[:, :], k.b_v.rearrange("(a n) -> a n", a=1)).then_inc(loaded, 16)
                load_columns(sp, loaded, bias_q, k.b_qk[0])
                load_columns(sp, loaded, gamma, k.gamma)
                load_columns(sp, loaded, beta, k.beta)
                for h in range(HEADS):
                    for s in range(2):
                        r = (h * HD) % P
                        sp.dma_start(amat[r:r + HD, h * HD // P, s * HEADS + h:s * HEADS + h + 1],
                                     k.gnn_a[h, s * HD:(s + 1) * HD].rearrange("(p a) -> p a", a=1)).then_inc(loaded, 16)

                def store(i, t, b, rows):
                    sp.wait_ge(tok.act_done[b], i + 1)
                    sp.wait_ge(tok.dve_done[b], i + 1)
                    sp.dma_start(k.hs[bass.ds(t * P, rows), :], rows_out[b][0:rows, :]).then_inc(row_out[b], 16)
                    sp.dma_start(k.scores_table[bass.ds(t * P, rows), :], rows_out[b][0:rows, D:ROW]).then_inc(row_out[b], 16)

                tok.blocks(sp, store)
                sp.wait_ge(row_out[0], 32 * (PAIRS + 1))
                sp.wait_ge(row_out[1], 32 * PAIRS)

            @block.vector
            def _(dve):
                nc.vector.memset(bias_k[:, :], 0.0)
                nc.vector.memset(kmax[:, :], -BIG)
                nc.vector.memset(amat[:, :, :], 0.0).then_inc(cleared, 1)
                dve.wait_ge(w_products, 1)
                nc.vector.tensor_copy(whT[:, :, :].rearrange("p c n -> p (c n)"), ps_m[:, 0, :]).then_inc(w_copied, 1)
                dve.wait_ge(w_products, 2)
                dve.wait_ge(loaded, 16 * n_loads)
                for c in range(DC):
                    nc.vector.tensor_copy(wcat[:, c, D:D + 16], ps_m[:, 1, c * 16:(c + 1) * 16]).then_inc(score_w, 1)

                def post(i, t, b, rows):
                    dve.wait_ge(row_out[b], i * 32)
                    nc.vector.tensor_copy(rows_out[b][:, D:ROW], ps_k[b][:, D + 8:D + 16])
                    nc.vector.tensor_copy(flat(k.sdm[:, bass.ds(t, 1), 0:HEADS]), ps_k[b][:, D:D + 8])
                    nc.vector.tensor_copy(flat(keys[:, bass.ds(t, 1), :]), ps_k[b][:, 0:D])
                    dve.wait_ge(tok.dve_done[1 - b], i + b)
                    return nc.vector.tensor_tensor(kmax[0:rows, :], kmax[0:rows, :], ps_k[b][0:rows, 0:D], ALU.max)

                tok.vector(dve, post)

            @block.scalar
            def _(act):
                def post(i, t, b, rows):
                    act.wait_ge(row_out[b], i * 32)
                    return nc.scalar.copy(rows_out[b][:, 0:D], ps_h[b][:, 0:D])

                tok.scalar(act, post)

            @block.tensor
            def _(pe):
                pe.wait_ge(loaded, 16 * n_loads)
                for c in range(DC):
                    for d in range(DC):
                        last = nc.tensor.transpose(ps_m[:, 0, d * D + c * P:d * D + (c + 1) * P],
                                                   wh[:, c, d * P:(d + 1) * P], k.ident[:, :])
                last.then_inc(w_products, 1)
                pe.wait_ge(w_copied, 1)
                for c in range(DC):
                    for d in range(DC):
                        last = nc.tensor.matmul(ps_m[:, 1, c * 16:(c + 1) * 16], whT[:, d, c * P:(c + 1) * P],
                                                amat[:, d, :], start=(d == 0), stop=(d == DC - 1))
                last.then_inc(w_products, 1)
                pe.wait_ge(score_w, DC)

                def project(i, t, b, rows):
                    for c in range(DC):
                        nc.tensor.matmul(ps_k[b][:, 0:D + 16], tok.xnT[b][:, c, :], wcat[:, c, :], start=(c == 0), stop=False)
                    nc.tensor.matmul(ps_k[b][:, 0:D + 16], k.ones[0:1, :], bias_k[:, :], start=False, stop=True)
                    for c in range(DC):
                        last = nc.tensor.matmul(ps_h[b][:, 0:D], tok.xnT[b][:, c, :], wh[:, c, :],
                                                start=(c == 0), stop=(c == DC - 1))
                    return last

                tok.tensor(pe, project, act_posts=True)

        chain, pe_step, diag_ok = ph.sem("chain"), ph.sem("pe_step"), ph.sem("diag_ok")
        shifted = [ph.sem(f"shifted{b}") for b in range(2)]
        exp_ok = [ph.sem(f"exp_ok{b}") for b in range(2)]
        exp_used = [ph.sem(f"exp_used{b}") for b in range(2)]
        max_ok, copied, std_done, m_ok = ph.sem("max_ok"), ph.sem("copied"), ph.sem("std_done"), ph.sem("m_ok")
        kd, ek = tok.xn, [rows_out[b][:, 0:D] for b in range(2)]
        peak, diag, peaks = ph.sb("peak", [P, DC]), tok.xnT[0], kmax
        grams, lam = whT, wh
        gramsT = ph.sb("gramsT", [P, DC, D])
        rden, st6, mv2, std2 = ph.sb("rden", [P, DC]), ph.sb("st6", [P, DC, 6]), ph.sb("mv2", [P, DC, 2]), ph.sb("std2", [P, DC, 2])
        ps_g = ps_k
        ps_x = ps_h

        with nc.Block() as block:

            @block.tensor
            def _(pe):
                for c in range(DC):
                    last = nc.tensor.transpose(ps_m[:, 0, c * P:(c + 1) * P], kmax[:, c * P:(c + 1) * P], k.ident[:, :])
                last.then_inc(pe_step, 1)
                pe.wait_ge(diag_ok, DC)
                nc.tensor.matmul(ps_m[:, 1, 0:D], k.ones[:, :], diag[:, :, :].rearrange("p c n -> p (c n)"),
                                 start=True, stop=True).then_inc(pe_step, 1)

                def gram(i, t, b, rows, start, stop):
                    pe.wait_ge(exp_ok[b], i + 1)
                    for c in range(DC):
                        nc.tensor.matmul(ps_g[c][:, 0:D], ek[b][0:rows, c * P:(c + 1) * P],
                                         flat(k.XN[0:rows, bass.ds(t, 1), :]), start=start, stop=stop, skip_group_check=True)
                        last = nc.tensor.matmul(ps_x[c][:, 0:1], ek[b][0:rows, c * P:(c + 1) * P],
                                                k.ones[0:rows, 0:1], start=start, stop=stop, skip_group_check=True)
                    last.then_inc(exp_used[b], 1)

                gram(0, NB - 1, 0, LAST, True, False)
                with pe.Fori(0, PAIRS, 1) as i:
                    gram(i, i * 2, 1, P, False, False)
                    gram(i + 1, i * 2 + 1, 0, P, False, False)
                pe.wait_ge(copied, 1)
                for src, q in ((grams, 0), (wq, 1)):
                    for c in range(DC):
                        for d in range(DC):
                            last = nc.tensor.transpose(ps_m[:, q, d * D + c * P:d * D + (c + 1) * P],
                                                       src[:, c, d * P:(d + 1) * P], k.ident[:, :])
                last.then_inc(pe_step, 1)
                pe.wait_ge(copied, 3)
                for m in range(DC):
                    for c in range(DC):
                        nc.tensor.matmul(tok.ps_turn[m][:, 0:D], gramsT[:, c, m * P:(m + 1) * P], wv[:, c, :],
                                         start=(c == 0), stop=False)
                    last = nc.tensor.matmul(tok.ps_turn[m][:, 0:D], k.ones[0:1, :], bias_v[:, :], start=False, stop=True)
                last.then_inc(pe_step, 1)
                pe.wait_ge(m_ok, 1)
                for m in range(DC):
                    for d in range(DC):
                        nc.tensor.matmul(ps_g[m][:, 0:D], wqT[:, d, m * P:(m + 1) * P], lam[:, d, :],
                                         start=(d == 0), stop=(d == DC - 1))
                for d in range(DC):
                    last = nc.tensor.matmul(ps_x[0][0:1, 0:D], bias_q[:, d:d + 1], lam[:, d, :],
                                            start=(d == 0), stop=(d == DC - 1))
                last.then_inc(pe_step, 1)

            @block.vector
            def _(dve):
                link = Chain(dve, chain)
                dve.wait_ge(pe_step, 1)
                for c in range(DC):
                    link(nc.vector.tensor_reduce(peak[:, c:c + 1], ps_m[:, 0, c * P:(c + 1) * P], AX.X, ALU.max))
                    nc.vector.tensor_scalar(diag[:, c, :], k.ident[:, :], peak[:, c:c + 1], None, ALU.mult).then_inc(diag_ok, 1)
                dve.wait_ge(pe_step, 2)
                link(nc.vector.tensor_copy(peaks[:, :], ps_m[:, 1, 0:D]))

                def shift(i, t, b, rows):
                    dve.wait_ge(exp_ok[b], i)
                    nc.vector.tensor_tensor(kd[b][0:rows, :], flat(keys[0:rows, bass.ds(t, 1), :]),
                                            peaks[0:rows, :], ALU.subtract).then_inc(shifted[b], 1)

                shift(0, NB - 1, 0, LAST)
                with dve.Fori(0, PAIRS, 1) as i:
                    shift(i, i * 2, 1, P)
                    shift(i + 1, i * 2 + 1, 0, P)
                dve.wait_ge(exp_used[0], PAIRS + 1)
                dve.wait_ge(exp_used[1], PAIRS)
                for c in range(DC):
                    link(nc.vector.reciprocal(rden[:, c:c + 1], ps_x[c][:, 0:1]))
                    link(nc.vector.tensor_scalar(grams[:, c, :], ps_g[c][:, 0:D], rden[:, c:c + 1], None, ALU.mult))
                nc.vector.tensor_copy(std2[:, 0, :], k.ones[:, 0:2]).then_inc(copied, 1)
                dve.wait_ge(pe_step, 3)
                nc.vector.tensor_copy(gramsT[:, :, :].rearrange("p c n -> p (c n)"), ps_m[:, 0, :]).then_inc(copied, 1)
                nc.vector.tensor_copy(wqT[:, :, :].rearrange("p c n -> p (c n)"), ps_m[:, 1, :]).then_inc(copied, 1)
                dve.wait_ge(pe_step, 4)
                for m in range(DC):
                    link(nc.vector.bn_stats(st6[:, m, :], tok.ps_turn[m][:, 0:D]))
                    last = nc.vector.bn_aggr(mv2[:, m, :], st6[:, m, :])
                    link(last)
                nc.vector.tensor_copy(std2[:, 0, 0:1], k.ones[:, 0:1]).then_inc(max_ok, 1)
                dve.wait_ge(std_done, 1)
                for m in range(DC):
                    link(nc.vector.reciprocal(std2[:, m, 1:2], std2[:, m, 0:1]))
                    link(nc.vector.tensor_scalar(lam[:, m, :], tok.ps_turn[m][:, 0:D], mv2[:, m, 0:1], std2[:, m, 1:2],
                                                 ALU.subtract, ALU.mult))
                    link(nc.vector.tensor_scalar(lam[:, m, :], lam[:, m, :], gamma[:, m:m + 1], beta[:, m:m + 1],
                                                 ALU.mult, ALU.add))
                nc.vector.tensor_copy(peak[:, 0:1], k.ones[:, 0:1]).then_inc(m_ok, 1)
                dve.wait_ge(pe_step, 5)
                for m in range(DC):
                    nc.vector.tensor_copy(k.mixw[:, m, :], ps_g[m][:, 0:D])
                nc.vector.tensor_copy(k.mixb[:, :], ps_x[0][0:1, 0:D])

            @block.scalar
            def _(act):
                def exps(i, b, rows):
                    act.wait_ge(shifted[b], i + 1)
                    act.wait_ge(exp_used[b], i)
                    nc.scalar.activation(ek[b][0:rows, :], kd[b][0:rows, :], ACT.Exp).then_inc(exp_ok[b], 1)

                exps(0, 0, LAST)
                with act.Fori(0, PAIRS, 1) as i:
                    exps(i, 1, P)
                    exps(i + 1, 0, P)
                act.wait_ge(max_ok, 1)
                for m in range(DC):
                    last = nc.scalar.activation(std2[:, m, 0:1], mv2[:, m, 1:2], ACT.Sqrt, bias=k.eps[:, 0:1])
                last.then_inc(std_done, 1)

    add_mix(nc, k, "l0mix")


def add_mix(nc, k, name):
    with Phase(nc, name) as ph:
        tok = Tokens(nc, k, ph, norm=False)
        ps_y = [ph.ps(f"ps_y{b}", [P, 512]) for b in range(2)]
        with nc.Block() as block:

            @block.vector
            def _(dve):
                def post(i, t, b, rows):
                    x = flat(k.X[:, bass.ds(t, 1), :])
                    return nc.vector.tensor_tensor(x, x, ps_y[b][:, 0:D], ALU.add)

                tok.vector(dve, post)

            @block.scalar
            def _(act):
                tok.scalar(act)

            @block.tensor
            def _(pe):
                def project(i, t, b, rows):
                    for c in range(DC):
                        nc.tensor.matmul(ps_y[b][:, 0:D], tok.xnT[b][:, c, :], k.mixw[:, c, :], start=(c == 0), stop=False)
                    return nc.tensor.matmul(ps_y[b][:, 0:D], k.ones[0:1, :], k.mixb[:, :], start=False, stop=True)

                tok.tensor(pe, project)


def segment_peaks(nc, k):
    g = k.graph[0]
    FOLD = SLOTS // P
    with Phase(nc, "peaks") as ph:
        tab = ph.sb("tab", [P, FOLD, 2])
        other = ph.sb("other", [P, FOLD], I32)
        slot = [ph.sb(f"slot{b}", [P, TGRP], I32) for b in range(TRING)]
        got = [ph.sb(f"got{b}", [P, TGRP, HEADS]) for b in range(TRING)]
        scores = ph.sb("scores", [P, HEADS, FOLD])
        fresh = ph.sb("fresh", [P, FOLD])
        first = ph.sb("first", [P, FOLD])
        edge_keys = ph.sb("edge_keys", [P, 8])
        keyT = ph.sb("keyT", [8, P])
        tails = ph.sb("tails", [P, 16])
        tailsT = ph.sb("tailsT", [8, P])
        pen = ph.sb("pen", [8, P])
        carry = ph.sb("carry", [8, P + 1])
        carried = ph.sb("carried", [P, 8])
        cand = ph.sb("cand", [P, FOLD])
        flip = k.XN[:, :, :].rearrange("p a d -> p (a d)")[:, 0:FOLD * HEADS].rearrange("p (t h) -> p t h", h=HEADS)
        z = ph.sb("z", [P, NB, HEADS])
        peak = ph.sb("peak", [P, NB, HEADS])
        ps = ph.ps("ps", [P, 512])

        loaded, ready, chain = ph.sem("loaded"), ph.sem("ready"), ph.sem("chain")
        slots_ok, fetched = ph.sem("slots_ok"), [[ph.sem(f"fetched{b}_{j}") for j in range(TGRP)] for b in range(TRING)]
        kept, pe_ok, pe_go, stored, node_got = ph.sem("kept"), ph.sem("pe_ok"), ph.sem("pe_go"), ph.sem("stored"), ph.sem("node_got")
        pool_going = ph.sem("pool_going")
        with nc.Block() as block:

            @block.sync
            def _(sp):
                sp.dma_start(tab[:, :, :], g.table.rearrange("(p t) a -> p t a", p=P)).then_inc(loaded, 16)
                sp.wait_ge(ready, 2)
                sp.dma_start(k.peak_table.rearrange("(p t) a -> p t a", p=P), flip).then_inc(stored, 16)
                sp.wait_ge(stored, 16)

            @block.gpsimd
            def _(pool):
                def fetch(g_, b):
                    pool.wait_ge(slots_ok, g_ + 1)
                    wait_past(pool, kept, g_ - (TRING - 1))
                    pool.sem_inc(pool_going, 1)
                    for j in range(TGRP):
                        pool.indirect_dma_start(out=got[b][:, j, :], out_offset=None, in_=k.scores_table,
                                                in_offset=bass.IndirectOffsetOnAxis(ap=slot[b][:, j:j + 1], axis=0)).then_inc(fetched[b][j], 16)

                rounds(pool, TGROUPS, TRING, fetch)
                pool.wait_ge(stored, 16)
                for t in range(NB):
                    pool.indirect_dma_start(out=peak[:, t, :], out_offset=None, in_=k.peak_table,
                                            in_offset=bass.IndirectOffsetOnAxis(ap=g.last[:, t:t + 1], axis=0)).then_inc(node_got, 16)

            @block.scalar
            def _(act):
                act.wait_ge(ready, 1)

                def indices(g_, b, i):
                    if i is not None:
                        for j in range(TGRP):
                            act.wait_ge(fetched[b][j], i * 16)
                    nc.scalar.copy(slot[b][:, :], other[:, bass.ds(g_ * TGRP, TGRP)]).then_inc(slots_ok, 1)

                for b in range(TRING):
                    indices(b, b, None)
                with act.Fori(1, TGROUPS // TRING, 1) as i:
                    for b in range(TRING):
                        indices(i * TRING + b, b, i)

            @block.vector
            def _(dve):
                link = Chain(dve, chain)
                dve.wait_ge(loaded, 16)
                nc.vector.tensor_copy(other[:, :], tab[:, :, 0]).then_inc(ready, 1)
                link(nc.vector.tensor_tensor(fresh[:, 1:FOLD], tab[:, 1:FOLD, 1], tab[:, 0:FOLD - 1, 1], ALU.not_equal))
                link(nc.vector.memset(fresh[:, 0:1], 1.0))
                link(nc.vector.tensor_scalar(fresh[:, :], fresh[:, :], -BIG, None, ALU.mult))
                link(nc.vector.tensor_scalar(first[:, :], tab[:, :, 1], tab[:, 0, 1:2], -BIG, ALU.not_equal, ALU.mult))
                link(nc.vector.tensor_copy(edge_keys[:, 0:1], tab[:, 0, 1:2]))
                link(nc.vector.tensor_copy(edge_keys[:, 1:2], tab[:, FOLD - 1, 1:2]))

                def keep(g_, b, i):
                    for j in range(TGRP):
                        dve.wait_ge(fetched[b][j], i * 16 + 16)
                    nc.vector.tensor_copy(scores[:, :, bass.ds(g_ * TGRP, TGRP)], got[b][:, :, :].rearrange("p t h -> p h t")).then_inc(kept, 1)

                with dve.Fori(0, TGROUPS // TRING, 1) as i:
                    for b in range(TRING):
                        keep(i * TRING + b, b, i)
                dve.wait_ge(kept, TGROUPS)
                for h in range(HEADS):
                    link(nc.vector.tensor_tensor_scan(cand[:, :], fresh[:, :], scores[:, h, :], -BIG, ALU.add, ALU.max))
                    link(nc.vector.tensor_copy(scores[:, h, :], cand[:, :]))
                for c in range(2):
                    link(nc.vector.tensor_copy(tails[:, c * 8:c * 8 + 8], (edge_keys[:, c:c + 1] if c else edge_keys[:, 0:1]).to_broadcast([P, 8])))
                pe_go_ins = nc.vector.tensor_copy(tails[:, 0:1], edge_keys[:, 0:1])
                link(pe_go_ins)
                nc.vector.tensor_copy(carried[:, :], scores[:, :, FOLD - 1]).then_inc(pe_go, 1)
                dve.wait_ge(pe_ok, 1)
                link(nc.vector.tensor_copy(tailsT[:, :], ps[0:8, 2 * P:3 * P]))
                link(nc.vector.tensor_copy(keyT[:, :], ps[0:8, 0:P]))
                link(nc.vector.memset(pen[:, :], 1.0))
                link(nc.vector.tensor_tensor(pen[:, 1:P], keyT[:, 1:P], ps[0:8, P:2 * P - 1], ALU.not_equal))
                link(nc.vector.tensor_scalar(pen[:, :], pen[:, :], -BIG, None, ALU.mult))
                link(nc.vector.tensor_tensor(keyT[:, :], keyT[:, :], ps[0:8, P:2 * P], ALU.not_equal))
                link(nc.vector.tensor_scalar(keyT[:, :], keyT[:, :], -BIG, None, ALU.mult))
                link(nc.vector.tensor_tensor(keyT[:, :], keyT[:, :], pen[:, :], ALU.min))
                link(nc.vector.memset(carry[:, :], -BIG))
                link(nc.vector.tensor_tensor_scan(carry[:, 1:P + 1], keyT[:, :], tailsT[:, :], -BIG, ALU.add, ALU.max))
                nc.vector.tensor_tensor(tailsT[:, :], carry[:, 0:P], pen[:, :], ALU.add).then_inc(pe_go, 1)
                dve.wait_ge(pe_ok, 2)
                link(nc.vector.tensor_copy(carried[:, :], ps[:, 0:8]))
                for h in range(HEADS):
                    link(nc.vector.tensor_scalar(cand[:, :], first[:, :], carried[:, h:h + 1], None, ALU.add))
                    last = nc.vector.tensor_tensor(flip[:, :, h], scores[:, h, :], cand[:, :], ALU.max)
                    link(last)
                nc.vector.tensor_copy(tails[:, 0:1], tails[:, 1:2]).then_inc(ready, 1)
                dve.wait_ge(node_got, 16 * NB)
                link(nc.vector.tensor_tensor(z[:, :, :], k.sdm[:, 0:NB, 0:HEADS], peak[:, :, :], ALU.add))
                link(nc.vector.scalar_tensor_tensor(out=peak[:, :, :], in0=z[:, :, :], scalar=0.2, in1=z[:, :, :],
                                                    op0=ALU.mult, op1=ALU.max))
                nc.vector.tensor_copy(k.sdm[:, 0:NB, HEADS:2 * HEADS], peak[:, :, :])
                nc.vector.memset(k.sdm[:, NB, :], 0.0)

            @block.tensor
            def _(pe):
                pe.wait_ge(pe_go, 1)
                nc.tensor.transpose(ps[0:8, 0:P], tails[:, 0:8], k.ident[:, :])
                nc.tensor.transpose(ps[0:8, P:2 * P], tails[:, 8:16], k.ident[:, :])
                nc.tensor.transpose(ps[0:8, 2 * P:3 * P], carried[:, :], k.ident[:, :]).then_inc(pe_ok, 1)
                pe.wait_ge(pe_go, 2)
                nc.tensor.transpose(ps[:, 0:8], tailsT[:, :], k.ident[0:8, 0:8]).then_inc(pe_ok, 1)


class Gather:

    def __init__(self, nc, k, ph, graph, table, width):
        self.nc, self.graph, self.table, self.width = nc, graph, table, width
        self.k = k
        self.slot = [ph.sb(f"slot{b}", [P, TGRP], I32) for b in range(TRING)]
        self.got = [ph.sb(f"got{b}", [P, TGRP, width]) for b in range(TRING)]
        self.member = [ph.sb(f"member{b}", [P, TGRP, P]) for b in range(TRING)]
        self.slots_ok, self.adding = ph.sem("slots_ok"), ph.sem("adding")
        self.members_ok, self.summed = ph.sem("members_ok"), ph.sem("summed")
        self.pool_going = ph.sem("pool_going")
        self.fetched = [[ph.sem(f"fetched{b}_{j}") for j in range(TGRP)] for b in range(TRING)]

    def fetch(self, pool):
        def group(g, b):
            pool.wait_ge(self.slots_ok, g + 1)
            wait_past(pool, self.summed, g - (TRING - 1))
            pool.sem_inc(self.pool_going, 1)
            for j in range(TGRP):
                pool.indirect_dma_start(out=self.got[b][:, j, :], out_offset=None, in_=self.table,
                                        in_offset=bass.IndirectOffsetOnAxis(ap=self.slot[b][:, j:j + 1], axis=0)).then_inc(self.fetched[b][j], 16)

        rounds(pool, TGROUPS, TRING, group)

    def arrived(self, eng, b, i):
        for j in range(TGRP):
            eng.wait_ge(self.fetched[b][j], i * 16 + 16)

    def indices(self, act, g, b, i):
        if not isinstance(i, int) or i:
            for j in range(TGRP):
                act.wait_ge(self.fetched[b][j], i * 16)
        self.nc.scalar.copy(self.slot[b][:, :], self.graph.other[:, bass.ds(g * TGRP, TGRP)]).then_inc(self.slots_ok, 1)

    def members(self, g, b):
        return self.nc.vector.tensor_tensor(
            self.member[b][:, :, :], self.k.ramp[:, 0:P].unsqueeze(1).to_broadcast([P, TGRP, P]),
            self.graph.local[:, bass.ds(g * TGRP, TGRP)].unsqueeze(2).to_broadcast([P, TGRP, P]), ALU.is_equal)

    def total(self, g, b, ps_sum):
        for j in range(TGRP):
            wait_past(self.nc.tensor, self.adding, (g - 1) * TGRP + j + 1)
            last = self.nc.tensor.matmul(ps_sum[j][:, 0:self.width], self.member[b][:, j, :], self.got[b][:, j, :],
                                         start=True, stop=True)
        last.then_inc(self.summed, 1)

    def blocks(self, eng, g):
        return [eng.value_load(self.graph.block[0:1, bass.ds(g * TGRP + j, 1)], min_val=0, max_val=NB)
                for j in range(TGRP)]

    def add(self, dve, g, j, sums, blocks, ps_sum):
        wait_past(dve, self.adding, g * TGRP + j)
        into = flat(sums[:, bass.ds(blocks[j], 1), :])
        self.nc.vector.tensor_tensor(into, into, ps_sum[j][:, 0:self.width], ALU.add).then_inc(self.adding, 1)


def ring_steps(eng, step, drain=0):
    staged(eng, TGROUPS, TRING, step, drain)


def attend(nc, k):
    graph = k.graph[0]
    with Phase(nc, "attend") as ph:
        io = Gather(nc, k, ph, graph, k.hs, ROW)
        nodeT = [ph.sb(f"nodeT{b}", [P, TGRP, P]) for b in range(TRING)]
        z = [ph.sb(f"z{b}", [P, TGRP, HEADS]) for b in range(TRING)]
        ps_n = ph.ps("ps_n", [P, 512])
        ps_s = ph.ps("ps_s", [P, 512])
        ps_sum = [ph.ps(f"ps_sum{j}", [P, 512]) for j in range(TGRP)]
        turned, nodeT_ok, looked, z_ok, exp_ok, step = (ph.sem(s) for s in ("turned", "nodeT_ok", "looked", "z_ok", "exp_ok", "step"))
        weighed = ph.sem("weighed")
        cleared = ph.sem("cleared")

        with nc.Block() as block:

            @block.gpsimd
            def _(pool):
                io.fetch(pool)

            @block.scalar
            def _(act):
                def turn(g, b):
                    act.wait_ge(turned, g + 1)
                    nc.scalar.copy(nodeT[b][:, :, :].rearrange("p t n -> p (t n)"), ps_n[:, :]).then_inc(nodeT_ok, 1)

                def group(g, b, i):
                    if has(g + 1, TGROUPS):
                        turn(g + 1, (b + 1) % TRING)
                    if has(g + 3, TGROUPS):
                        io.indices(act, g + 3, (b + 3) % TRING, i + (b + 3) // TRING)
                    act.wait_ge(z_ok, g + 1)
                    nc.scalar.activation(io.got[b][:, :, D:ROW], z[b][:, :, :], ACT.Exp).then_inc(exp_ok, 1)

                for b in range(3):
                    io.indices(act, b, b, 0)
                turn(0, 0)
                ring_steps(act, group)

            @block.tensor
            def _(pe):
                def turn(g, b):
                    pe.wait_ge(io.members_ok, g + 1)
                    wait_past(pe, nodeT_ok, g)
                    for j in range(TGRP):
                        last = nc.tensor.transpose(ps_n[:, j * P:(j + 1) * P], io.member[b][:, j, :], k.ident[:, :])
                    last.then_inc(turned, 1)

                def look(g, b):
                    blocks = io.blocks(pe, g)
                    pe.wait_ge(nodeT_ok, g + 1)
                    wait_past(pe, z_ok, g)
                    for j in range(TGRP):
                        last = nc.tensor.matmul(ps_s[:, j * 16:(j + 1) * 16], nodeT[b][:, j, :],
                                                flat(k.sdm[:, bass.ds(blocks[j], 1), :]), start=True, stop=True)
                    last.then_inc(looked, 1)

                def group(g, b, i):
                    if has(g + 1, TGROUPS):
                        turn(g + 1, (b + 1) % TRING)
                    if has(g - 2, TGROUPS):
                        pe.wait_ge(weighed, g - 1)
                        io.total(g - 2, (b - 2) % TRING, ps_sum)
                    if has(g + 1, TGROUPS):
                        look(g + 1, (b + 1) % TRING)

                turn(0, 0)
                look(0, 0)
                ring_steps(pe, group, drain=2)

            @block.vector
            def _(dve):
                nc.vector.memset(k.sums[:, :, :], 0.0).then_inc(cleared, 1)
                dve.wait_ge(cleared, 1)

                def group(g, b, i):
                    here, before, adds = has(g, TGROUPS), has(g - 1, TGROUPS), has(g - 3, TGROUPS)
                    s = ps_s[:, 0:TGRP * 16].rearrange("p (t a h) -> p t a h", t=TGRP, a=2)
                    if adds:
                        blocks = io.blocks(dve, g - 3)
                        dve.wait_ge(io.summed, g - 2)
                        io.add(dve, g - 3, 0, k.sums, blocks, ps_sum)
                    if has(g + 2, TGROUPS):
                        io.members(g + 2, (b + 2) % TRING).then_inc(io.members_ok, 1)
                    if adds:
                        io.add(dve, g - 3, 1, k.sums, blocks, ps_sum)
                    if here:
                        io.arrived(dve, b, i)
                        dve.wait_ge(looked, g + 1)
                        first = nc.vector.tensor_tensor(z[b][:, :, :], s[:, :, 0, :], io.got[b][:, :, D:ROW], ALU.add)
                        first.then_inc(step, 1)
                    if adds:
                        io.add(dve, g - 3, 2, k.sums, blocks, ps_sum)
                    if here:
                        dve.wait_ge(step, g * 2 + 1)
                        second = nc.vector.scalar_tensor_tensor(out=z[b][:, :, :], in0=z[b][:, :, :], scalar=0.2, in1=z[b][:, :, :],
                                                                op0=ALU.mult, op1=ALU.max)
                        second.then_inc(step, 1)
                    if adds:
                        io.add(dve, g - 3, 3, k.sums, blocks, ps_sum)
                    if here:
                        dve.wait_ge(step, g * 2 + 2)
                        nc.vector.tensor_tensor(z[b][:, :, :], z[b][:, :, :], s[:, :, 1, :], ALU.subtract).then_inc(z_ok, 1)
                    if before:
                        c = (b - 1) % TRING
                        dve.wait_ge(exp_ok, g)
                        rows = io.got[c][:, :, 0:D].rearrange("p t (h d) -> p t h d", h=HEADS)
                        nc.vector.tensor_tensor(rows, rows, io.got[c][:, :, D:ROW].unsqueeze(3).to_broadcast([P, TGRP, HEADS, HD]),
                                                ALU.mult).then_inc(weighed, 1)

                for g in range(2):
                    io.members(g, g).then_inc(io.members_ok, 1)
                ring_steps(dve, group, drain=3)


def route(nc, k):
    with Phase(nc, "route") as ph:
        gate = ph.sb("gate", [P, DC, EXPERTS])
        gate_b = ph.sb("gate_b", [1, EXPERTS])
        inv = [ph.sb(f"inv{b}", [P, HEADS]) for b in range(2)]
        share = [ph.sb(f"share{b}", [P, D]) for b in range(2)]
        zero = ph.sb("zero", [P, D])
        logits = ph.sb("logits", [P, NB, EXPERTS])
        tok = Tokens(nc, k, ph)
        ps_l = [ph.ps(f"ps_l{b}", [P, 512]) for b in range(2)]
        loaded, attn, zeroed, cleared = ph.sem("loaded"), ph.sem("attn"), ph.sem("zeroed"), ph.sem("cleared")
        with nc.Block() as block:

            @block.sync
            def _(sp):
                load_matrix(sp, loaded, gate[:, :, :], k.gate_w)
                sp.dma_start(gate_b[:, :], k.gate_b.rearrange("(a n) -> a n", a=1)).then_inc(loaded, 16)
                sp.wait_ge(zeroed, 1)
                full = EXPERTS * EROWS // P
                sp.dma_start(k.expert_rows[0:full * P, :].rearrange("(t p) d -> p t d", p=P),
                             zero[:, :].unsqueeze(1).to_broadcast([P, full, D])).then_inc(cleared, 16)
                rest = EXPERTS * EROWS - full * P
                if rest:
                    sp.dma_start(k.expert_rows[full * P:full * P + rest, :], zero[0:rest, :]).then_inc(cleared, 16)
                sp.wait_ge(cleared, 32 if rest else 16)

            @block.vector
            def _(dve):
                nc.vector.memset(zero[:, :], 0.0).then_inc(zeroed, 1)

                def attended(i, t, b, rows):
                    link = Chain(dve, attn, t * 4)
                    s = flat(k.sums[:, bass.ds(t, 1), :])
                    x = flat(k.X[:, bass.ds(t, 1), :])
                    link(nc.vector.tensor_scalar(inv[b][:, :], s[:, D:ROW], 1e-16, None, ALU.add))
                    link(nc.vector.reciprocal(inv[b][:, :], inv[b][:, :]))
                    link(nc.vector.tensor_tensor(share[b][:, :].rearrange("p (h d) -> p h d", h=HEADS),
                                                 s[:, 0:D].rearrange("p (h d) -> p h d", h=HEADS),
                                                 inv[b][:, :].unsqueeze(2).to_broadcast([P, HEADS, HD]), ALU.mult))
                    link(nc.vector.tensor_tensor(x, x, share[b][:, :], ALU.add))

                def post(i, t, b, rows):
                    return nc.vector.tensor_copy(flat(logits[:, bass.ds(t, 1), :]), ps_l[b][:, 0:EXPERTS])

                tok.vector(dve, post, attended)

            @block.scalar
            def _(act):
                tok.scalar(act)

            @block.tensor
            def _(pe):
                pe.wait_ge(loaded, 32)

                def project(i, t, b, rows):
                    for c in range(DC):
                        nc.tensor.matmul(ps_l[b][:, 0:EXPERTS], tok.xnT[b][:, c, :], gate[:, c, :], start=(c == 0), stop=False)
                    return nc.tensor.matmul(ps_l[b][:, 0:EXPERTS], k.ones[0:1, :], gate_b[:, :], start=False, stop=True)

                tok.tensor(pe, project)

        chain, shifted, exp_ok, marks_ok, counted = (ph.sem(s) for s in ("chain", "shifted", "exp_ok", "marks_ok", "counted"))
        places_ok, spread = ph.sem("places_ok"), ph.sem("spread")
        E3 = [P, NB, EXPERTS]
        top, total, expert, pos, kept, a, c = (ph.sb(s, [P, NB]) for s in ("top", "total", "expert", "pos", "kept", "a", "c"))
        prob, marks, tot, scan = (ph.sb(s, E3) for s in ("prob", "marks", "tot", "scan"))
        place = ph.sb("place", [P, NB], I32)
        ramp8 = k.ramp[:, 0:EXPERTS].unsqueeze(1).to_broadcast(E3)

        def wide(v):
            return v[:, :].unsqueeze(2).to_broadcast(E3)

        with nc.Block() as block:

            @block.scalar
            def _(act):
                act.wait_ge(shifted, 1)
                nc.scalar.activation(prob[:, :, :], logits[:, :, :], ACT.Exp).then_inc(exp_ok, 1)

            @block.tensor
            def _(pe):
                pe.wait_ge(marks_ok, 1)
                m = marks[:, :, :].rearrange("p t e -> p (t e)")
                nc.tensor.matmul(ps_l[0][:, 0:NB * EXPERTS], k.upper[:, :], m, start=True, stop=True)
                nc.tensor.matmul(ps_l[1][:, 0:NB * EXPERTS], k.ones[:, :], m, start=True, stop=True).then_inc(counted, 1)

            @block.vector
            def _(dve):
                link = Chain(dve, chain)
                v = nc.vector
                link(v.tensor_reduce(top[:, :], logits[:, :, :], AX.X, ALU.max))
                v.tensor_tensor(logits[:, :, :], logits[:, :, :], wide(top), ALU.subtract).then_inc(shifted, 1)
                dve.wait_ge(exp_ok, 1)
                link(v.tensor_reduce(total[:, :], prob[:, :, :], AX.X, ALU.add))
                link(v.tensor_reduce(top[:, :], prob[:, :, :], AX.X, ALU.max))
                link(v.tensor_tensor(marks[:, :, :], prob[:, :, :], wide(top), ALU.is_equal))
                link(v.scalar_tensor_tensor(out=marks[:, :, :], in0=marks[:, :, :], scalar=-float(EXPERTS), in1=ramp8,
                                            op0=ALU.mult, op1=ALU.add))
                link(v.tensor_reduce(expert[:, :], marks[:, :, :], AX.X, ALU.min))
                link(v.tensor_scalar(expert[:, :], expert[:, :], float(EXPERTS), None, ALU.add))
                link(v.tensor_tensor(marks[:, :, :], ramp8, wide(expert), ALU.is_equal))
                v.tensor_tensor(marks[:, :, :], marks[:, :, :], wide(k.valid), ALU.mult).then_inc(marks_ok, 1)
                link(v.reciprocal(total[:, :], total[:, :]))
                link(v.tensor_tensor(top[:, :], top[:, :], total[:, :], ALU.mult))
                dve.wait_ge(counted, 1)
                link(v.tensor_copy(tot[:, :, :].rearrange("p t e -> p (t e)"), ps_l[1][:, 0:NB * EXPERTS]))
                for e in range(EXPERTS):
                    v.tensor_tensor_scan(scan[:, :, e], k.ones[:, 0:NB], tot[:, :, e], 0.0, ALU.mult, ALU.add)
                link(v.tensor_copy(a[:, :], k.ones[:, 0:NB]))
                link(v.tensor_tensor(scan[:, :, :], scan[:, :, :], tot[:, :, :], ALU.subtract))
                link(v.tensor_tensor(scan[:, :, :].rearrange("p t e -> p (t e)"), scan[:, :, :].rearrange("p t e -> p (t e)"),
                                     ps_l[0][:, 0:NB * EXPERTS], ALU.add))
                link(v.tensor_tensor(scan[:, :, :], scan[:, :, :], marks[:, :, :], ALU.mult))
                link(v.tensor_reduce(pos[:, :], scan[:, :, :], AX.X, ALU.add))
                link(v.tensor_scalar(kept[:, :], pos[:, :], float(CAP), None, ALU.is_lt))
                link(v.tensor_tensor(k.weight[:, :], top[:, :], kept[:, :], ALU.mult))
                link(v.scalar_tensor_tensor(out=a[:, :], in0=expert[:, :], scalar=float(EROWS), in1=pos[:, :], op0=ALU.mult, op1=ALU.add))
                link(v.tensor_scalar(c[:, :], k.token[:, :], float(EXPERTS * EROWS), None, ALU.add))
                link(v.tensor_tensor(a[:, :], a[:, :], c[:, :], ALU.subtract))
                link(v.tensor_tensor(a[:, :], a[:, :], kept[:, :], ALU.mult))
                link(v.tensor_tensor(a[:, :], a[:, :], c[:, :], ALU.add))
                v.tensor_copy(place[:, :], a[:, :]).then_inc(places_ok, 1)
                link(v.tensor_scalar(pos[:, :], pos[:, :], float(CAP - 1), None, ALU.min))
                link(v.scalar_tensor_tensor(out=pos[:, :], in0=expert[:, :], scalar=float(EROWS), in1=pos[:, :], op0=ALU.mult, op1=ALU.add))
                v.tensor_copy(k.source[:, :], pos[:, :])

            @block.gpsimd
            def _(pool):
                pool.wait_ge(places_ok, 1)
                spread_rows(pool, k, k.expert_rows, place, spread)


def spread_rows(pool, k, table, place, sem):
    for t in range(NB):
        rows = P if t < NB - 1 else LAST
        pool.indirect_dma_start(out=table, out_offset=bass.IndirectOffsetOnAxis(ap=place[0:rows, t:t + 1], axis=0),
                                in_=k.XN[0:rows, t, :], in_offset=None).then_inc(sem, 16)
    pool.wait_ge(sem, 16 * NB)


def feed_forward(nc, k, name, rows_in, rows_out, width, experts, per_expert, func, w1, b1, w2, b2):
    TOKS = [(m * P, min(P, width - m * P)) for m in range(-(-width // P))]
    NT = len(TOKS)
    sets = min(2, experts)
    turns = experts // sets
    LOADS = 32 if width % P else 16
    GI = sets * per_expert
    with Phase(nc, name) as ph:
        sw1 = [ph.sb(f"w1_{s}", [P, DC, FF]) for s in range(sets)]
        sw2 = [ph.sb(f"w2_{s}", [P, FC, D]) for s in range(sets)]
        sb1 = [ph.sb(f"b1_{s}", [P, FC]) for s in range(sets)]
        sb2 = [ph.sb(f"b2_{s}", [P, D]) for s in range(sets)]
        x = ph.sb("x", [P, NT, D])
        xT = ph.sb("xT", [P, DC, width])
        hT = ph.sb("hT", [P, FC, width])
        y = ph.sb("y", [P, NT, D])
        ps_x = [ph.ps(f"ps_x{c}", [P, 512]) for c in range(DC)]
        ps_h = [ph.ps(f"ps_h{q}", [P, 512]) for q in range(2)]
        ps_y = [ph.ps(f"ps_y{q}", [P, 512]) for q in range(2)]
        weights = [ph.sem(f"weights{s}") for s in range(sets)]
        x_in, turned, xT_ok, hid, relu_ok, y_ps, y_ok, y_out = (
            ph.sem(s) for s in ("x_in", "turned", "xT_ok", "hid", "relu_ok", "y_ps", "y_ok", "y_out"))

        def loop(eng, step, head=None):
            for s in range(sets):
                if head:
                    head(0, s)
                for h in range(per_expert):
                    step(s * per_expert + h, 0, s)
            if turns > 1:
                with eng.Fori(1, turns, 1) as i:
                    for s in range(sets):
                        if head:
                            head(i, s)
                        for h in range(per_expert):
                            step(i * GI + (s * per_expert + h), i, s)

        with nc.Block() as block:

            @block.sync
            def _(sp):
                def load_weights(i, s):
                    if not isinstance(i, int):
                        sp.wait_ge(y_ok, (i - 1) * (GI * NT) + (s + 1) * per_expert * NT)
                    e = i * sets + s
                    sp.dma_start(sw1[s][:, :, :], w1(e).rearrange("(c p) n -> p c n", p=P)).then_inc(weights[s], 16)
                    sp.dma_start(sw2[s][:, :, :], w2(e).rearrange("(c p) n -> p c n", p=P)).then_inc(weights[s], 16)
                    sp.dma_start(sb1[s][:, :], b1(e).rearrange("(f p) -> p f", p=P), allow_slow_non_contiguous=True).then_inc(weights[s], 16)
                    sp.dma_start(sb2[s][:, :], b2(e).partition_broadcast(P)).then_inc(weights[s], 16)

                def load_rows(g, i, s):
                    wait_past(sp, turned, g)
                    n = width // P
                    sp.dma_start(x[:, 0:n, :], rows_in[bass.ds(g * width, n * P), :].rearrange("(m p) d -> p m d", p=P)).then_inc(x_in, 16)
                    if width % P:
                        sp.dma_start(x[0:width % P, n, :], rows_in[bass.ds(g * width + n * P, width % P), :]).then_inc(x_in, 16)

                loop(sp, load_rows, load_weights)

            @block.gpsimd
            def _(pool):
                def store(g, i, s):
                    pool.wait_ge(y_ok, g * NT + NT)
                    n = width // P
                    pool.dma_start(rows_out[bass.ds(g * width, n * P), :].rearrange("(m p) d -> p m d", p=P), y[:, 0:n, :]).then_inc(y_out, 16)
                    if width % P:
                        pool.dma_start(rows_out[bass.ds(g * width + n * P, width % P), :], y[0:width % P, n, :]).then_inc(y_out, 16)

                loop(pool, store)
                pool.wait_ge(y_out, turns * GI * LOADS)

            @block.tensor
            def _(pe):
                def group(g, i, s):
                    pe.wait_ge(x_in, g * LOADS + LOADS)
                    wait_past(pe, xT_ok, g)
                    for c in range(DC):
                        for m, (at, n) in enumerate(TOKS):
                            last = nc.tensor.transpose(ps_x[c][:, at:at + n], x[0:n, m, c * P:(c + 1) * P], k.ident[0:n, 0:n])
                    last.then_inc(turned, 1)
                    pe.wait_ge(weights[s], i * 64 + 64)
                    pe.wait_ge(xT_ok, g + 1)
                    for f in range(FC):
                        wait_past(pe, relu_ok, g * FC + (f - 1))
                        for c in range(DC):
                            last = nc.tensor.matmul(ps_h[f % 2][:, 0:width], sw1[s][:, c, f * P:(f + 1) * P], xT[:, c, :],
                                                    start=(c == 0), stop=(c == DC - 1))
                        last.then_inc(hid, 1)
                    pe.wait_ge(relu_ok, g * FC + FC)
                    for m, (at, n) in enumerate(TOKS):
                        wait_past(pe, y_ok, g * NT + (m - 1))
                        for f in range(FC):
                            last = nc.tensor.matmul(ps_y[m % 2][0:n, 0:D], hT[:, f, at:at + n], sw2[s][:, f, :],
                                                    start=(f == 0), stop=(f == FC - 1))
                        last.then_inc(y_ps, 1)

                loop(pe, group)

            @block.scalar
            def _(act):
                def group(g, i, s):
                    act.wait_ge(weights[s], i * 64 + 64)
                    wait_past(act, y_ps, g * NT)
                    for f in range(FC):
                        act.wait_ge(hid, g * FC + f + 1)
                        nc.scalar.activation(hT[:, f, :], ps_h[f % 2][:, 0:width], func, bias=sb1[s][:, f:f + 1]).then_inc(relu_ok, 1)

                loop(act, group)

            @block.vector
            def _(dve):
                def group(g, i, s):
                    dve.wait_ge(turned, g + 1)
                    wait_past(dve, hid, g * FC)
                    for c in range(DC):
                        last = nc.vector.tensor_copy(xT[:, c, :], ps_x[c][:, 0:width])
                    last.then_inc(xT_ok, 1)
                    wait_past(dve, y_out, g * LOADS)
                    for m, (at, n) in enumerate(TOKS):
                        dve.wait_ge(y_ps, g * NT + m + 1)
                        nc.vector.tensor_tensor(y[0:n, m, :], ps_y[m % 2][0:n, 0:D], sb2[s][0:n, :], ALU.add).then_inc(y_ok, 1)

                loop(dve, group)


def graph_tables(nc, k):
    k.own = k.keep_own()
    KW = 128
    FMAX = 3.4028234663852886e38
    with Phase(nc, "l1") as ph:
        wcat = ph.sb("wcat", [P, DC, KW + GH])
        wq, wv = ph.sb("wq", [P, DC, KW]), ph.sb("wv", [P, DC, KW])
        wout = ph.sb("wout", [P, D])
        keys = ph.sb("keys", [P, NB, KW])
        kmax = ph.sb("kmax", [P, KW])
        slot = [ph.sb(f"slot{b}", [P, 1], I32) for b in range(2)]
        got = [ph.sb(f"got{b}", [P, D]) for b in range(2)]
        fin, ind = ph.sb("fin", [P, D]), ph.sb("ind", [P, 3, D])
        tok = Tokens(nc, k, ph)
        ps_k = [ph.ps(f"ps_k{b}", [P, 512]) for b in range(2)]
        ps_m, ps_g = ph.ps("ps_m", [P, 512]), ph.ps("ps_g", [P, 512])
        ps_d = ph.ps("ps_d", [P, 512])
        loaded, root, deg = ph.sem("loaded"), ph.sem("root"), ph.sem("deg")
        slot_ok = ph.sem("slot_ok")
        got_ok, got_used, stored = ([ph.sem(f"{s}{b}") for b in range(2)] for s in ("got_ok", "got_used", "stored"))
        adding, pool_going = ph.sem("adding"), ph.sem("pool_going")

        with nc.Block() as block:

            @block.sync
            def _(sp):
                load_matrix(sp, loaded, wcat[:, :, 0:KW], k.W_qkv[:, KW:2 * KW])
                load_matrix(sp, loaded, wcat[:, :, KW:KW + GH], k.gcn_W1)
                load_matrix(sp, loaded, wq[:, :, :], k.W_qkv[:, 0:KW])
                load_matrix(sp, loaded, wv[:, :, :], k.W_qkv[:, 2 * KW:3 * KW])
                sp.dma_start(wout[:, :], k.W_out).then_inc(loaded, 16)
                sp.dma_start(k.mixb[:, :], k.b_out.rearrange("(a n) -> a n", a=1)).then_inc(loaded, 16)

                def store(i, t, b, rows):
                    sp.wait_ge(tok.dve_done[b], i + 1)
                    sp.dma_start(k.gcn_table[0][bass.ds(t * P, rows), :],
                                 flat(k.own[0:rows, bass.ds(t, 1), :])).then_inc(stored[b], 16)

                tok.blocks(sp, store)
                sp.wait_ge(stored[0], 16 * (PAIRS + 1))
                sp.wait_ge(stored[1], 16 * PAIRS)

            @block.gpsimd
            def _(pool):
                def fetch(i, t, b, rows):
                    pool.wait_ge(got_used[b], i)
                    pool.sem_inc(pool_going, 1)
                    pool.tensor_copy(slot[b][:, :], k.source[:, bass.ds(t, 1)]).then_inc(slot_ok, 1)
                    pool.wait_ge(slot_ok, t + 1)
                    pool.sem_inc(pool_going, 1)
                    pool.indirect_dma_start(out=got[b][:, :], out_offset=None, in_=k.expert_out,
                                            in_offset=bass.IndirectOffsetOnAxis(ap=slot[b][:, :], axis=0)).then_inc(got_ok[b], 16)

                tok.blocks(pool, fetch)

            @block.vector
            def _(dve):
                v = nc.vector
                v.memset(kmax[:, :], -BIG)
                v.tensor_scalar(k.dinv[:, :], k.graph[1].count[:, :], 1.0, None, ALU.add).then_inc(deg, 1)
                dve.wait_ge(root, 1)
                v.reciprocal(k.dinv[:, :], k.dinv[:, :]).then_inc(deg, 1)
                dve.wait_ge(deg, 2)

                def mixed(i, t, b, rows):
                    dve.wait_ge(got_ok[b], i * 16 + 16)
                    link = Chain(dve, adding, t * 7)
                    x = flat(k.X[:, bass.ds(t, 1), :])
                    link(v.tensor_scalar(got[b][:, :], got[b][:, :], k.weight[:, bass.ds(t, 1)], None, ALU.mult))
                    link(v.tensor_scalar(fin[:, :], got[b][:, :], -FMAX, FMAX, ALU.max, ALU.min))
                    v.tensor_tensor(ind[:, 0, :], got[b][:, :], fin[:, :], ALU.is_equal)
                    v.tensor_tensor(ind[:, 1, :], got[b][:, :], fin[:, :], ALU.is_gt)
                    link(v.tensor_tensor(ind[:, 2, :], got[b][:, :], fin[:, :], ALU.is_lt))
                    link(v.tensor_tensor(fin[:, :], fin[:, :], ind[:, 0, :], ALU.mult))
                    link(v.tensor_tensor(ind[:, 1, :], ind[:, 1, :], ind[:, 2, :], ALU.subtract))
                    link(v.scalar_tensor_tensor(out=fin[:, :], in0=ind[:, 1, :], scalar=1.0e4, in1=fin[:, :], op0=ALU.mult, op1=ALU.add))
                    link(v.tensor_tensor(x, x, fin[:, :], ALU.add))
                    v.tensor_copy(ind[:, 0, 0:1], k.ones[:, 0:1]).then_inc(got_used[b], 1)

                def post(i, t, b, rows):
                    v.tensor_scalar(flat(k.own[:, bass.ds(t, 1), :]), ps_k[b][:, KW:KW + GH], k.dinv[:, bass.ds(t, 1)], None, ALU.mult)
                    v.tensor_copy(flat(keys[:, bass.ds(t, 1), :]), ps_k[b][:, 0:KW])
                    dve.wait_ge(tok.dve_done[1 - b], i + b)
                    return v.tensor_tensor(kmax[0:rows, :], kmax[0:rows, :], ps_k[b][0:rows, 0:KW], ALU.max)

                tok.vector(dve, post, mixed)

            @block.scalar
            def _(act):
                act.wait_ge(deg, 1)
                nc.scalar.activation(k.dinv[:, :], k.dinv[:, :], ACT.Sqrt).then_inc(root, 1)
                tok.scalar(act)

            @block.tensor
            def _(pe):
                pe.wait_ge(loaded, 16 * 6)

                def project(i, t, b, rows):
                    for c in range(DC):
                        last = nc.tensor.matmul(ps_k[b][:, 0:KW + GH], tok.xnT[b][:, c, :], wcat[:, c, :],
                                                start=(c == 0), stop=(c == DC - 1))
                    return last

                tok.tensor(pe, project)

        chain, pe_step, diag_ok, exp_ok, exp_used, shifted, copied = (
            ph.sem(s) for s in ("chain", "pe_step", "diag_ok", "exp_ok", "exp_used", "shifted", "copied"))
        kd, ek = [tok.xn[b][:, 0:KW] for b in range(2)], [got[b][:, 0:KW] for b in range(2)]
        peak, diag, rden = ph.sb("peak", [P, 1]), ph.sb("diag", [P, P]), ph.sb("rden", [P, 1])
        gram, gramT, ctxT, wqT, folded = ind[:, 0, :], ph.sb("gramT", [P, DC, KW]), ph.sb("ctxT", [P, KW]), ph.sb("wqT", [P, DC, P]), fin
        HW = 32
        with nc.Block() as block:

            @block.tensor
            def _(pe):
                nc.tensor.transpose(ps_m[:, 0:P], kmax[:, :], k.ident[:, :]).then_inc(pe_step, 1)
                pe.wait_ge(diag_ok, 1)
                nc.tensor.matmul(ps_m[:, 0:KW], k.ones[:, :], diag[:, :], start=True, stop=True).then_inc(pe_step, 1)

                def product(n, b, t, rows, start):
                    pe.wait_ge(exp_ok, n + 1)
                    nc.tensor.matmul(ps_g[:, 0:D], ek[b][0:rows, :], flat(k.XN[0:rows, bass.ds(t, 1), :]),
                                     start=start, stop=False, skip_group_check=True)
                    nc.tensor.matmul(ps_d[:, 0:1], ek[b][0:rows, :], k.ones[0:rows, 0:1],
                                     start=start, stop=False, skip_group_check=True).then_inc(exp_used, 1)

                product(0, 0, NB - 1, LAST, True)
                with pe.Fori(0, PAIRS, 1) as i:
                    product(i * 2 + 1, 1, i * 2, P, False)
                    product(i * 2 + 2, 0, i * 2 + 1, P, False)
                pe.wait_ge(copied, 1)
                for c in range(DC):
                    nc.tensor.transpose(ps_m[:, c * P:(c + 1) * P], gram[:, c * P:(c + 1) * P], k.ident[:, :])
                for c in range(DC):
                    last = nc.tensor.transpose(ps_m[:, (DC + c) * P:(DC + c + 1) * P], wq[:, c, :], k.ident[:, :])
                last.then_inc(pe_step, 1)
                pe.wait_ge(copied, 2)
                for c in range(DC):
                    last = nc.tensor.matmul(ps_k[0][:, 0:KW], wv[:, c, :], gramT[:, c, :], start=(c == 0), stop=(c == DC - 1))
                last.then_inc(pe_step, 1)
                pe.wait_ge(copied, 3)
                nc.tensor.matmul(ps_k[1][:, 0:D], ctxT[:, :], wout[:, :], start=True, stop=True).then_inc(pe_step, 1)
                pe.wait_ge(copied, 4)
                for c in range(DC):
                    last = nc.tensor.matmul(ps_m[:, c * D:(c + 1) * D], wqT[:, c, :], folded[:, :], start=True, stop=True)
                last.then_inc(pe_step, 1)

            @block.vector
            def _(dve):
                v = nc.vector
                link = Chain(dve, chain)
                dve.wait_ge(pe_step, 1)
                link(v.tensor_reduce(peak[:, :], ps_m[:, 0:P], AX.X, ALU.max))
                v.tensor_scalar(diag[:, :], k.ident[:, :], peak[:, :], None, ALU.mult).then_inc(diag_ok, 1)
                dve.wait_ge(pe_step, 2)
                link(v.tensor_copy(kmax[:, :], ps_m[:, 0:KW]))

                def shift(n, b, t, rows):
                    wait_past(dve, exp_ok, n - 1)
                    v.tensor_tensor(kd[b][0:rows, :], flat(keys[0:rows, bass.ds(t, 1), :]), kmax[0:rows, :],
                                    ALU.subtract).then_inc(shifted, 1)

                shift(0, 0, NB - 1, LAST)
                with dve.Fori(0, PAIRS, 1) as i:
                    shift(i * 2 + 1, 1, i * 2, P)
                    shift(i * 2 + 2, 0, i * 2 + 1, P)
                dve.wait_ge(exp_used, NB)
                link(v.reciprocal(rden[:, :], ps_d[:, 0:1]))
                v.tensor_scalar(gram[:, :], ps_g[:, 0:D], rden[:, :], None, ALU.mult).then_inc(copied, 1)
                link(v.memset(ctxT[:, :], 0.0))
                dve.wait_ge(pe_step, 3)
                v.tensor_copy(gramT[:, :, :].rearrange("p c n -> p (c n)"), ps_m[:, 0:D])
                v.tensor_copy(wqT[:, :, :].rearrange("p c n -> p (c n)"), ps_m[:, D:2 * D]).then_inc(copied, 1)
                dve.wait_ge(pe_step, 4)
                for h in range(KW // HW):
                    r = slice(h * HW, (h + 1) * HW)
                    last = v.tensor_copy(ctxT[r, r], ps_k[0][r, r])
                last.then_inc(copied, 1)
                dve.wait_ge(pe_step, 5)
                v.tensor_scalar(folded[:, :], ps_k[1][:, 0:D], HW ** -0.5, None, ALU.mult).then_inc(copied, 1)
                dve.wait_ge(pe_step, 6)
                v.tensor_copy(k.mixw[:, :, :].rearrange("p c n -> p (c n)"), ps_m[:, :])

            @block.scalar
            def _(act):
                def exps(n, b, rows):
                    act.wait_ge(shifted, n + 1)
                    wait_past(act, exp_used, n - 1)
                    nc.scalar.activation(ek[b][0:rows, :], kd[b][0:rows, :], ACT.Exp).then_inc(exp_ok, 1)

                exps(0, 0, LAST)
                with act.Fori(0, PAIRS, 1) as i:
                    exps(i * 2 + 1, 1, P)
                    exps(i * 2 + 2, 0, P)

    add_mix(nc, k, "l1mix")


def convolve(nc, k, n):
    graph = k.graph[1]
    with Phase(nc, f"conv{n}") as ph:
        io = Gather(nc, k, ph, graph, k.gcn_table[n], GH)
        ps_sum = [ph.ps(f"ps_sum{j}", [P, 512]) for j in range(TGRP)]
        cleared = ph.sem("cleared")

        with nc.Block() as block:

            @block.gpsimd
            def _(pool):
                io.fetch(pool)

            @block.scalar
            def _(act):
                ring_steps(act, lambda g, b, i: io.indices(act, g, b, i))

            @block.tensor
            def _(pe):
                def group(g, b, i):
                    io.arrived(pe, b, i)
                    pe.wait_ge(io.members_ok, g + 1)
                    io.total(g, b, ps_sum)

                ring_steps(pe, group)

            @block.vector
            def _(dve):
                nc.vector.memset(k.sums64[:, :, :], 0.0).then_inc(cleared, 1)
                dve.wait_ge(cleared, 1)

                def group(g, b, i):
                    adds = has(g - 1, TGROUPS)
                    if adds:
                        blocks = io.blocks(dve, g - 1)
                        dve.wait_ge(io.summed, g)
                    for j in range(TGRP):
                        if adds:
                            io.add(dve, g - 1, j, k.sums64, blocks, ps_sum)
                        if j == 0 and has(g + 2, TGROUPS):
                            io.members(g + 2, (b + 2) % TRING).then_inc(io.members_ok, 1)

                for g in range(2):
                    io.members(g, g).then_inc(io.members_ok, 1)
                ring_steps(dve, group, drain=1)


def hidden(nc, k):
    with Phase(nc, "hidden") as ph:
        bias = ph.sb("bias", [P, GH])
        loaded, chain, stored = ph.sem("loaded"), ph.sem("chain"), ph.sem("stored")
        W3 = [P, NB, GH]
        with nc.Block() as block:

            @block.vector
            def _(dve):
                v, link = nc.vector, Chain(dve, chain)
                s, scale = k.sums64[:, 0:NB, :], k.dinv[:, :].unsqueeze(2).to_broadcast(W3)
                dve.wait_ge(loaded, 16)
                link(v.tensor_tensor(s, s, k.own[:, :, :], ALU.add))
                link(v.tensor_tensor(s, s, scale, ALU.mult))
                link(v.tensor_tensor(s, s, bias[:, :].unsqueeze(1).to_broadcast(W3), ALU.add))
                link(v.tensor_scalar(s, s, 0.0, None, ALU.max))
                link(v.tensor_tensor(k.own[:, :, :], s, scale, ALU.mult))

            @block.sync
            def _(sp):
                sp.dma_start(bias[:, :], k.gcn_b1.partition_broadcast(P)).then_inc(loaded, 16)
                sp.wait_ge(chain, 5)
                table = k.gcn_table[1]
                sp.dma_start(table[0:(NB - 1) * P, :].rearrange("(t p) d -> p t d", p=P), k.own[:, 0:NB - 1, :]).then_inc(stored, 16)
                sp.dma_start(table[(NB - 1) * P:N, :], k.own[0:LAST, NB - 1, :]).then_inc(stored, 16)
                sp.wait_ge(stored, 32)


def convolved(nc, k):
    with Phase(nc, "tanh") as ph:
        w2, b2 = ph.sb("w2", [GH, D]), ph.sb("b2", [1, D])
        aT = [ph.sb(f"aT{b}", [GH, P]) for b in range(2)]
        a = [ph.sb(f"a{b}", [P, GH]) for b in range(2)]
        th = [ph.sb(f"th{b}", [P, D]) for b in range(2)]
        ps_t = [ph.ps(f"ps_t{b}", [P, 512]) for b in range(2)]
        ps_y = [ph.ps(f"ps_y{b}", [P, 512]) for b in range(2)]
        loaded, chain, pe_going = ph.sem("loaded"), ph.sem("chain"), ph.sem("pe_going")
        a_ok, turned, aT_ok, y_ok, th_ok, done = (ph.sem(s) for s in ("a_ok", "turned", "aT_ok", "y_ok", "th_ok", "done"))

        def blocks(eng, step):
            step(0, 0)
            step(1, 1)
            with eng.Fori(1, PAIRS, 1) as i:
                for b in range(2):
                    step(i * 2 + b, b)
            step(NB - 1, 0)

        with nc.Block() as block:

            @block.sync
            def _(sp):
                sp.dma_start(w2[:, :], k.gcn_W2).then_inc(loaded, 16)
                sp.dma_start(b2[:, :], k.gcn_b2.rearrange("(a n) -> a n", a=1)).then_inc(loaded, 16)

            @block.vector
            def _(dve):
                v = nc.vector

                def first(t, b):
                    link = Chain(dve, chain, t * 1)
                    wait_past(dve, turned, t - 1)
                    link(v.tensor_tensor(a[b][:, :], flat(k.sums64[:, bass.ds(t, 1), :]), flat(k.own[:, bass.ds(t, 1), :]), ALU.add))
                    v.tensor_scalar(a[b][:, :], a[b][:, :], k.dinv[:, bass.ds(t, 1)], None, ALU.mult).then_inc(a_ok, 1)

                def last(t, b):
                    dve.wait_ge(th_ok, t + 1)
                    x = flat(k.X[:, bass.ds(t, 1), :])
                    v.tensor_tensor(x, x, th[b][:, :], ALU.add).then_inc(done, 1)

                first(0, 0)
                first(1, 1)
                last(0, 0)
                with dve.Fori(1, PAIRS, 1) as i:
                    first(i * 2, 0)
                    last(i * 2 - 1, 1)
                    first(i * 2 + 1, 1)
                    last(i * 2, 0)
                first(NB - 1, 0)
                last(NB - 2, 1)
                last(NB - 1, 0)

            @block.scalar
            def _(act):
                def step(t, b):
                    act.wait_ge(turned, t + 1)
                    wait_past(act, y_ok, t - 1)
                    nc.scalar.copy(aT[b][:, :], ps_t[b][0:GH, 0:P]).then_inc(aT_ok, 1)
                    act.wait_ge(y_ok, t + 1)
                    wait_past(act, done, t - 1)
                    nc.scalar.activation(th[b][:, :], ps_y[b][:, 0:D], ACT.Tanh).then_inc(th_ok, 1)

                blocks(act, step)

            @block.tensor
            def _(pe):
                pe.wait_ge(loaded, 32)

                def step(t, b):
                    pe.wait_ge(a_ok, t + 1)
                    wait_past(pe, aT_ok, t - 1)
                    pe.sem_inc(pe_going, 1)
                    nc.tensor.transpose(ps_t[b][0:GH, 0:P], a[b][:, :], k.ident[:, :]).then_inc(turned, 1)
                    pe.wait_ge(aT_ok, t + 1)
                    wait_past(pe, th_ok, t - 1)
                    nc.tensor.matmul(ps_y[b][:, 0:D], aT[b][:, :], w2[:, :], start=True, stop=False)
                    nc.tensor.matmul(ps_y[b][:, 0:D], k.ones[0:1, :], b2[:, :], start=False, stop=True).then_inc(y_ok, 1)

                blocks(pe, step)


def choose(nc, k):
    with Phase(nc, "choose") as ph:
        wr, br = ph.sb("wr", [P, DC, 1]), ph.sb("br", [1, 1])
        zero = ph.sb("zero", [P, D])
        score = ph.sb("score", [P, NB])
        tok = Tokens(nc, k, ph)
        ps_w = [ph.ps(f"ps_w{b}", [P, 512]) for b in range(2)]
        loaded, zeroed, cleared, summed = ph.sem("loaded"), ph.sem("zeroed"), ph.sem("cleared"), ph.sem("summed")
        with nc.Block() as block:

            @block.sync
            def _(sp):
                load_columns(sp, loaded, wr[:, :, 0], k.wr.rearrange("d a -> (d a)"))
                sp.dma_start(br[:, :], k.br.rearrange("(a n) -> a n", a=1)).then_inc(loaded, 16)
                sp.wait_ge(zeroed, 1)
                sp.dma_start(k.chosen_rows[TOPK:CROWS, :], zero[0:CROWS - TOPK, :]).then_inc(cleared, 16)
                sp.wait_ge(cleared, 16)

            @block.vector
            def _(dve):
                nc.vector.memset(zero[:, :], 0.0).then_inc(zeroed, 1)

                def post(i, t, b, rows):
                    x = flat(k.X[:, bass.ds(t, 1), :])
                    nc.vector.tensor_tensor(x, x, tok.xn[b][:, :], ALU.add)
                    return nc.vector.tensor_copy(score[:, bass.ds(t, 1)], ps_w[b][:, 0:1])

                tok.vector(dve, post)

            @block.scalar
            def _(act):
                tok.scalar(act)

            @block.tensor
            def _(pe):
                pe.wait_ge(loaded, 16 * (DC + 1))

                def project(i, t, b, rows):
                    for c in range(DC):
                        nc.tensor.matmul(ps_w[b][:, 0:1], tok.xnT[b][:, c, :], wr[:, c, :], start=(c == 0), stop=False)
                    return nc.tensor.matmul(ps_w[b][:, 0:1], k.ones[0:1, :], br[:, :], start=False, stop=True)

                tok.tensor(pe, project)

        BITS = 32
        chain, counted, ready, places_ok, spread = (ph.sem(s) for s in ("chain", "counted", "ready", "places_ok", "spread"))
        u, bit, cand, flip, least, many, take = (ph.sb(s, [P, 1], I32) for s in ("u", "bit", "cand", "flip", "least", "many", "take"))
        part = ph.sb("part", [P, 1])
        least_f = least[:, :].bitcast(F32)
        hit, above, equal, before, tot, scan, chosen, a, c = (
            ph.sb(s, [P, NB]) for s in ("hit", "above", "equal", "before", "tot", "scan", "chosen", "a", "c"))
        room = ph.sb("room", [P, 1])
        place = ph.sb("place", [P, NB], I32)
        ps_c, ps_p, ps_t = tok.ps_turn[0], ps_w[0], ps_w[1]
        STEPS = 8
        with nc.Block() as block:

            @block.tensor
            def _(pe):
                with pe.Fori(0, BITS, 1) as i:
                    pe.wait_ge(ready, i + 1)
                    nc.tensor.matmul(ps_c[:, 0:1], k.ones[:, :], part[:, :], start=True, stop=True).then_inc(counted, 1)
                pe.wait_ge(ready, BITS + 1)
                nc.tensor.matmul(ps_c[:, 0:1], k.ones[:, :], part[:, :], start=True, stop=True)
                nc.tensor.matmul(ps_p[:, 0:NB], k.upper[:, :], equal[:, :], start=True, stop=True)
                nc.tensor.matmul(ps_t[:, 0:NB], k.ones[:, :], equal[:, :], start=True, stop=True).then_inc(counted, 1)
                pe.wait_ge(ready, BITS + 2)
                nc.tensor.matmul(ps_p[:, 0:NB], k.upper[:, :], chosen[:, :], start=True, stop=True)
                nc.tensor.matmul(ps_t[:, 0:NB], k.ones[:, :], chosen[:, :], start=True, stop=True).then_inc(counted, 1)

            @block.vector
            def _(dve):
                v = nc.vector
                link = Chain(dve, chain)

                def to_float(link, src):
                    link(v.tensor_scalar(flip[:, :], src[:, :], 31, -1, ALU.arith_shift_right, ALU.bitwise_xor))
                    link(v.scalar_tensor_tensor(out=least[:, :], in0=flip[:, :], scalar=-2147483648, in1=src[:, :],
                                                op0=ALU.bitwise_or, op1=ALU.bitwise_xor))

                link(v.tensor_tensor(score[:, :], score[:, :], k.valid[:, :], ALU.mult))
                link(v.tensor_scalar(a[:, :], k.valid[:, :], -1.0, 3.0e38, ALU.add, ALU.mult))
                link(v.tensor_tensor(score[:, :], score[:, :], a[:, :], ALU.add))
                link(v.memset(u[:, :], 0))
                link(v.memset(bit[:, :], -2147483648))
                with dve.Fori(0, BITS, 1) as i:
                    loop_link = Chain(dve, chain, i * STEPS + 5)
                    loop_link(v.tensor_tensor(cand[:, :], u[:, :], bit[:, :], ALU.bitwise_or))
                    to_float(loop_link, cand)
                    v.tensor_scalar(hit[:, :], score[:, :], least_f, 0.0, ALU.is_ge, ALU.add, accum_out=part[:, :]).then_inc(ready, 1)
                    dve.wait_ge(counted, i + 1)
                    loop_link(v.tensor_scalar(many[:, :], ps_c[:, 0:1], float(TOPK), None, ALU.is_ge))
                    loop_link(v.tensor_scalar(take[:, :], many[:, :], 31, 31, ALU.logical_shift_left, ALU.arith_shift_right))
                    loop_link(v.tensor_tensor(take[:, :], take[:, :], bit[:, :], ALU.bitwise_and))
                    loop_link(v.tensor_tensor(u[:, :], u[:, :], take[:, :], ALU.bitwise_or))
                    loop_link(v.tensor_single_scalar(bit[:, :], bit[:, :], 1, ALU.logical_shift_right))
                    assert loop_link.n == STEPS
                link = Chain(dve, chain, BITS * STEPS + 5)
                to_float(link, u)
                link(v.tensor_scalar(above[:, :], score[:, :], least_f, 0.0, ALU.is_gt, ALU.add, accum_out=part[:, :]))
                v.scalar_tensor_tensor(out=equal[:, :], in0=score[:, :], scalar=least_f, in1=k.valid[:, :],
                                       op0=ALU.is_equal, op1=ALU.mult).then_inc(ready, 1)

                def ahead(n, marks):
                    dve.wait_ge(counted, n)
                    link(v.tensor_copy(tot[:, :], ps_t[:, 0:NB]))
                    link(v.tensor_tensor_scan(scan[:, :], k.ones[:, 0:NB], tot[:, :], 0.0, ALU.mult, ALU.add))
                    link(v.tensor_tensor(scan[:, :], scan[:, :], tot[:, :], ALU.subtract))
                    link(v.tensor_tensor(before[:, :], scan[:, :], ps_p[:, 0:NB], ALU.add))

                ahead(BITS + 1, equal)
                link(v.tensor_scalar(room[:, :], ps_c[:, 0:1], -1.0, float(TOPK), ALU.mult, ALU.add))
                link(v.scalar_tensor_tensor(out=a[:, :], in0=before[:, :], scalar=room[:, 0:1], in1=equal[:, :], op0=ALU.is_lt, op1=ALU.mult))
                v.tensor_tensor(chosen[:, :], above[:, :], a[:, :], ALU.add).then_inc(ready, 1)
                ahead(BITS + 2, chosen)
                link(v.tensor_tensor(k.weight[:, :], score[:, :], chosen[:, :], ALU.mult))
                link(v.tensor_tensor(a[:, :], before[:, :], chosen[:, :], ALU.mult))
                v.tensor_copy(k.source[:, :], a[:, :])
                link(v.tensor_scalar(c[:, :], k.token[:, :], float(CROWS), None, ALU.add))
                link(v.tensor_tensor(before[:, :], before[:, :], c[:, :], ALU.subtract))
                link(v.tensor_tensor(before[:, :], before[:, :], chosen[:, :], ALU.mult))
                link(v.tensor_tensor(before[:, :], before[:, :], c[:, :], ALU.add))
                v.tensor_copy(place[:, :], before[:, :]).then_inc(places_ok, 1)

            @block.gpsimd
            def _(pool):
                pool.wait_ge(places_ok, 1)
                spread_rows(pool, k, k.chosen_rows, place, spread)


def finish(nc, k):
    with Phase(nc, "finish") as ph:
        slot = [ph.sb(f"slot{b}", [P, 1], I32) for b in range(2)]
        got = [ph.sb(f"got{b}", [P, D]) for b in range(2)]
        slot_ok, pool_going = ph.sem("slot_ok"), ph.sem("pool_going")
        got_ok, used, stored = [ph.sem(f"got_ok{b}") for b in range(2)], [ph.sem(f"used{b}") for b in range(2)], ph.sem("stored")

        def blocks(eng, step):
            with eng.Fori(0, PAIRS, 1) as i:
                for b in range(2):
                    step(i, i * 2 + b, b, P)
            step(PAIRS, NB - 1, 0, LAST)

        with nc.Block() as block:

            @block.gpsimd
            def _(pool):
                def fetch(i, t, b, rows):
                    pool.wait_ge(used[b], i)
                    pool.sem_inc(pool_going, 1)
                    pool.tensor_copy(slot[b][:, :], k.source[:, bass.ds(t, 1)]).then_inc(slot_ok, 1)
                    pool.wait_ge(slot_ok, t + 1)
                    pool.sem_inc(pool_going, 1)
                    pool.indirect_dma_start(out=got[b][:, :], out_offset=None, in_=k.chosen_out,
                                            in_offset=bass.IndirectOffsetOnAxis(ap=slot[b][:, :], axis=0)).then_inc(got_ok[b], 16)

                blocks(pool, fetch)

            @block.vector
            def _(dve):
                def add(i, t, b, rows):
                    dve.wait_ge(got_ok[b], i * 16 + 16)
                    x = flat(k.X[:, bass.ds(t, 1), :])
                    nc.vector.scalar_tensor_tensor(out=x, in0=got[b][:, :], scalar=k.weight[:, bass.ds(t, 1)], in1=x,
                                                   op0=ALU.mult, op1=ALU.add).then_inc(used[b], 1)

                blocks(dve, add)

            @block.sync
            def _(sp):
                def store(i, t, b, rows):
                    sp.wait_ge(used[b], i + 1)
                    sp.dma_start(k.out[bass.ds(t * P, rows), :], flat(k.X[0:rows, bass.ds(t, 1), :])).then_inc(stored, 16)

                blocks(sp, store)
                sp.wait_ge(stored, 16 * NB)


def gps_block_kernel(
    nc, x, src, dst, gnn_W, gnn_a, W_qk, b_qk, W_v, b_v, gamma, beta, gate_w, gate_b, w1, b1, w2, b2, gcn_W1,
    gcn_b1, gcn_W2, gcn_b2, W_qkv, W_out, b_out, wr, br, mw1, mb1, mw2, mb2, out,
):
    k = Buffers()
    k.x = x
    k.src = src
    k.dst = dst
    k.gnn_W = gnn_W
    k.gnn_a = gnn_a
    k.W_qk = W_qk
    k.b_qk = b_qk
    k.W_v = W_v
    k.b_v = b_v
    k.gamma = gamma
    k.beta = beta
    k.gate_w = gate_w
    k.gate_b = gate_b
    k.w1 = w1
    k.b1 = b1
    k.w2 = w2
    k.b2 = b2
    k.gcn_W1 = gcn_W1
    k.gcn_b1 = gcn_b1
    k.gcn_W2 = gcn_W2
    k.gcn_b2 = gcn_b2
    k.W_qkv = W_qkv
    k.W_out = W_out
    k.b_out = b_out
    k.wr = wr
    k.br = br
    k.mw1 = mw1
    k.mb1 = mb1
    k.mw2 = mw2
    k.mb2 = mb2
    k.out = out
    with ExitStack() as keep:
        def sb(name, shape, dt=F32):
            return keep.enter_context(nc.sbuf_tensor(name, shape, dt))

        def dram(name, shape, dt=F32):
            return nc.dram_tensor(name, shape, dt).ap()

        k.ident = sb("ident", [P, P])
        k.upper = sb("upper", [P, P])
        k.ones = sb("ones", [P, P])
        k.ident_b = sb("ident_b", [P, P], BF16)
        k.ramp = sb("ramp", [P, TILES])
        k.eps = sb("eps", [P, 1])
        k.eps16 = sb("eps16", [P, 1])
        k.valid = sb("valid", [P, NB])
        k.token = sb("token", [P, NB])
        k.weight = sb("weight", [P, NB])
        k.dinv = sb("dinv", [P, NB])
        k.keep_own = lambda: sb("own", [P, NB, GH])
        k.spare = sb("spare", [P, 1])
        k.source = sb("source", [P, NB], I32)
        k.sdm = sb("sdm", [P, NB + 1, 2 * HEADS])
        k.mixw = sb("mixw", [P, DC, D])
        k.mixb = sb("mixb", [1, D])
        k.zeros_b = sb("zeros_b", [P, P], BF16)
        k.graph = []
        for n in range(2):
            k.graph.append(Graph(
                table=dram(f"sorted{n}", [SLOTS, 2]), other=sb(f"other{n}", [P, TILES], I32),
                local=sb(f"local{n}", [P, TILES + TGRP]), block=sb(f"block{n}", [1, TILES], I32),
                count=sb(f"count{n}", [P, NB]), last=sb(f"last{n}", [P, NB], I32)))
        k.peak_table = dram("peak_table", [SLOTS, HEADS])
        k.expert_rows = dram("expert_rows", [EXPERTS * EROWS + NB * P, D])
        k.expert_out = dram("expert_out", [EXPERTS * EROWS, D])
        k.chosen_rows = dram("chosen_rows", [CROWS + NB * P, D])
        k.chosen_out = dram("chosen_out", [CROWS, D])
        k.gcn_table = [dram(f"gcn_table{n}", [N, GH]) for n in range(2)]
        k.scores_table = dram("scores_table", [N, HEADS])
        k.hs = dram("hs", [N, ROW])
        constants(nc, k)
        sort_edges(nc, k, "by_source", k.src, k.dst, k.graph[0])
        sort_edges(nc, k, "by_destination", k.dst, k.src, k.graph[1])
        k.X = sb("X", [P, NB, D])
        work = sb("work", [P, (NB + 1) * ROW])
        k.XN = work[:, 0:NB * D].rearrange("p (t d) -> p t d", d=D)
        k.sums64 = work[:, 0:(NB + 1) * GH].rearrange("p (t d) -> p t d", d=GH)
        k.sums = work[:, :].rearrange("p (t d) -> p t d", d=ROW)
        load_x(nc, k)
        attention_tables(nc, k)
        segment_peaks(nc, k)
        attend(nc, k)
        route(nc, k)
        feed_forward(nc, k, "experts", k.expert_rows, k.expert_out, EGROUP, EXPERTS, 2, ACT.Relu,
                     lambda e: k.w1[bass.ds(e, 1)].rearrange("a d f -> (a d) f"),
                     lambda e: k.b1[bass.ds(e, 1)].rearrange("a f -> (a f)"),
                     lambda e: k.w2[bass.ds(e, 1)].rearrange("a f d -> (a f) d"),
                     lambda e: k.b2[bass.ds(e, 1)].rearrange("a d -> (a d)"))
        graph_tables(nc, k)
        convolve(nc, k, 0)
        hidden(nc, k)
        convolve(nc, k, 1)
        convolved(nc, k)
        choose(nc, k)
        feed_forward(nc, k, "chosen", k.chosen_rows, k.chosen_out, CGROUP, 1, CROWS // CGROUP, ACT.Gelu_apprx_tanh,
                     lambda e: k.mw1, lambda e: k.mb1, lambda e: k.mw2, lambda e: k.mb2)
        finish(nc, k)


_ARGS = [
    "x", "src", "dst", "L0_gnn_W", "L0_gnn_a", "L0_mix_W_qk", "L0_mix_b_qk", "L0_mix_W_v", "L0_mix_b_v",
    "L0_mix_gamma", "L0_mix_beta", "L0_ffn_gate_w", "L0_ffn_gate_b", "L0_ffn_w1", "L0_ffn_b1", "L0_ffn_w2",
    "L0_ffn_b2", "L1_gnn_W1", "L1_gnn_b1", "L1_gnn_W2", "L1_gnn_b2", "L1_mix_W_qkv", "L1_mix_W_out",
    "L1_mix_b_out", "L1_ffn_wr", "L1_ffn_br", "L1_ffn_w1", "L1_ffn_b1", "L1_ffn_w2", "L1_ffn_b2",
]


def kernel(**inputs):
    import numpy as _np
    import concourse.bacc as _bacc
    from concourse import mybir as _mybir
    from concourse.bass_utils import run_bass_kernel_spmd as _run

    nc = _bacc.Bacc("TRN2", target_bir_lowering=False, num_devices=1)
    arrays, args = {}, []
    for name in _ARGS:
        a = _np.ascontiguousarray(inputs[name])
        arrays[f"in_{name}"] = a
        args.append(nc.dram_tensor(f"in_{name}", a.shape, _mybir.dt.from_np(a.dtype), kind="ExternalInput").ap())
    args.append(nc.dram_tensor("out_0", (N, D), F32, kind="ExternalOutput").ap())
    gps_block_kernel(nc, *args)
    return _run(nc, [arrays], core_ids=[0]).results[0]["out_0"]
```

```python
from contextlib import ExitStack

import concourse.bass as bass
from concourse import mybir

ALU = mybir.AluOpType
ACT = mybir.ActivationFunctionType
AX = mybir.AxisListType
F32 = mybir.dt.float32
BF16 = mybir.dt.bfloat16
I32 = mybir.dt.int32

P = 128
N, D = 6250, 256
NB = -(-N // P)
LAST = N - (NB - 1) * P
PAIRS = (NB - 1) // 2
DC = D // P
E_ALL = 106250
EP, ET = 125, 850
GRP = 5
LOOPS = ET // (2 * GRP)
RING = 5
GROUPS = ET // GRP
TILES = 880
SLOTS = TILES * P
TGRP = 4
TRING = 5
TGROUPS = TILES // TGRP
PGRP = 5
PGROUPS = TILES // PGRP
assert 0 <= PGROUPS - GROUPS < 9 and PGROUPS * PGRP == TILES
assert TGROUPS % TRING == 0 and GROUPS % RING == 0
HEADS, HD = 8, 32
ROW = D + HEADS
GH = 64
EXPERTS, FF = 8, 1024
SENT = ((14, 10), (26, 2 * EXPERTS), (3, 2 * NB))
SENT_FROM = (0, 14 * 10, 14 * 10 + 26 * 2 * EXPERTS)
assert SENT_FROM[2] + 3 * 2 * NB == ET
FC = FF // P
CAP = 977
EGROUP = 489
EROWS = 2 * EGROUP
TOPK = N // 2 - 1
CGROUP = 448
CROWS = 7 * CGROUP
BIG = 1.0e30
LN_EPS = 1e-05


class Buffers:
    pass


class Graph:

    def __init__(self, table, other, local, block, count, last):
        self.table, self.other, self.local = table, other, local
        self.block, self.count, self.last = block, count, last


class Chain:

    def __init__(self, eng, sem, base=0):
        self.eng, self.sem, self.base, self.n = eng, sem, base, 0

    def __call__(self, ins):
        self.n += 1
        ins.then_inc(self.sem, 1)
        self.eng.wait_ge(self.sem, self.base + self.n)


def rounds(eng, groups, width, step):
    for j in range(width):
        step(j, j)
    with eng.Fori(1, groups // width, 1) as i:
        for j in range(width):
            step(i * width + j, j)


def each_pair(eng, step):
    step(0)
    with eng.Fori(1, PAIRS, 1) as i:
        step(i)


def has(g, groups):
    return not isinstance(g, int) or 0 <= g < groups


def staged(eng, groups, width, step, drain=0):
    for b in range(width):
        step(b, b, 0)
    with eng.Fori(1, groups // width - 1, 1) as i:
        for b in range(width):
            step(i * width + b, b, i)
    for b in range(width + drain):
        step(groups - width + b, b % width, groups // width - 1 + b // width)




def wait_past(eng, sem, value):
    if not isinstance(value, int) or value > 0:
        eng.wait_ge(sem, value)


class Phase:

    def __init__(self, nc, name):
        self.nc, self.name, self.stack, self.sems = nc, name, ExitStack(), []

    def sb(self, name, shape, dt=F32):
        return self.stack.enter_context(self.nc.sbuf_tensor(f"{self.name}_{name}", shape, dt))

    def ps(self, name, shape, dt=F32):
        return self.stack.enter_context(self.nc.psum_tensor(f"{self.name}_{name}", shape, dt))

    def sem(self, name):
        s = self.nc.alloc_semaphore(f"{self.name}_{name}")
        self.sems.append(s)
        return s

    def __enter__(self):
        return self

    def __exit__(self, *error):
        if error[0] is None:
            self.nc.clear_and_free_semaphores(self.sems)
            self.nc.all_engine_barrier()
        self.stack.close()


def constants(nc, k):
    with Phase(nc, "const") as ph:
        made, ramp = ph.sem("made"), ph.sem("ramp")
        valid_set = ph.sem("valid_set")
        token_i = ph.sb("token_i", [P, NB], I32)
        ramp_i = ph.sb("ramp_i", [P, TILES], I32)
        with nc.Block() as block:

            @block.gpsimd
            def _(pool):
                pool.memset(k.ident[:, :], 0.0).then_inc(made, 1)
                pool.memset(k.upper[:, :], 1.0).then_inc(made, 1)
                pool.memset(k.ones[:, :], 1.0).then_inc(made, 1)
                pool.memset(k.valid[:, :], 1.0).then_inc(valid_set, 1)
                pool.wait_ge(valid_set, 1)
                pool.affine_select(out=k.valid[:, NB - 1:NB], in_=k.valid[:, NB - 1:NB], compare_op=ALU.is_ge, fill=0.0,
                                   base=LAST - 1, pattern=[[0, 1]], channel_multiplier=-1).then_inc(valid_set, 1)
                pool.iota(token_i[:, :], [[P, NB]], base=0, channel_multiplier=1).then_inc(valid_set, 1)
                pool.iota(ramp_i[:, :], [[1, TILES]], base=0, channel_multiplier=0).then_inc(ramp, 1)
                pool.wait_ge(made, 3)
                pool.affine_select(out=k.ident[:, :], in_=k.ident[:, :], compare_op=ALU.not_equal, fill=1.0,
                                   base=0, pattern=[[-1, P]], channel_multiplier=1).then_inc(made, 1)
                pool.affine_select(out=k.upper[:, :], in_=k.upper[:, :], compare_op=ALU.is_gt, fill=0.0,
                                   base=0, pattern=[[1, P]], channel_multiplier=-1).then_inc(made, 1)

            @block.vector
            def _(dve):
                dve.wait_ge(ramp, 1)
                nc.vector.tensor_copy(k.ramp[:, :], ramp_i[:, :])
                nc.vector.tensor_copy(k.ramp_b[:, :], ramp_i[:, 0:P])
                dve.wait_ge(valid_set, 3)
                nc.vector.tensor_copy(k.token[:, :], token_i[:, :])
                nc.vector.memset(k.eps[:, :], LN_EPS)
                dve.wait_ge(made, 5)
                nc.vector.tensor_copy(k.ident_b[:, :], k.ident[:, :])


def load_x(nc, k):
    with Phase(nc, "load") as ph:
        zeroed, loaded = ph.sem("zeroed"), ph.sem("loaded")
        with nc.Block() as block:

            @block.vector
            def _(dve):
                nc.vector.memset(k.X[:, NB - 1, :], 0.0).then_inc(zeroed, 1)

            @block.sync
            def _(sp):
                sp.dma_start(k.X[:, 0:NB - 1, :],
                             k.x[0:(NB - 1) * P, :].rearrange("(t p) d -> p t d", p=P)).then_inc(loaded, 16)
                sp.wait_ge(zeroed, 1)
                sp.dma_start(k.X[0:LAST, NB - 1, :], k.x[(NB - 1) * P:N, :]).then_inc(loaded, 16)
                sp.wait_ge(loaded, 32)


def flat(ap):
    return ap.rearrange("p a d -> p (a d)")


class Tokens:

    def __init__(self, nc, k, ph, norm=True):
        self.nc, self.k, self.norm = nc, k, norm
        self.xn = [ph.sb(f"xn{b}", [P, D]) for b in range(2)]
        self.xnT = [ph.sb(f"xnT{b}", [P, DC, P]) for b in range(2)]
        self.stats = [ph.sb(f"stats{b}", [P, 6]) for b in range(2)]
        self.mv = [ph.sb(f"mv{b}", [P, 2]) for b in range(2)]
        self.meanvar = ph.sb("meanvar", [P, NB, 2])
        self.scale = ph.sb("scale", [P, NB])
        self.ps_turn = [ph.ps(f"ps_turn{b}", [P, 512]) for b in range(2)]
        self.stats_ok = [ph.sem(f"stats_ok{b}") for b in range(2)]
        self.var_ok = [ph.sem(f"var_ok{b}") for b in range(2)]
        self.mv_kept = [ph.sem(f"mv_kept{b}") for b in range(2)]
        self.std_ok, self.scale_ok = ph.sem("std_ok"), ph.sem("scale_ok")
        self.xn_ok = [ph.sem(f"xn_ok{b}") for b in range(2)]
        self.xn_saved = [ph.sem(f"xn_saved{b}") for b in range(2)]
        self.turned = [ph.sem(f"turned{b}") for b in range(2)]
        self.xnT_ok = [ph.sem(f"xnT_ok{b}") for b in range(2)]
        self.projected = [ph.sem(f"projected{b}") for b in range(2)]
        self.dve_done = [ph.sem(f"dve_done{b}") for b in range(2)]
        self.act_done = [ph.sem(f"act_done{b}") for b in range(2)]
        self.dve_going = ph.sem("dve_going")

    def blocks(self, eng, step):
        step(0, 0, 0, P)
        step(0, 1, 1, P)
        with eng.Fori(1, PAIRS, 1) as i:
            for b in range(2):
                step(i, i * 2 + b, b, P)
        step(PAIRS, NB - 1, 0, LAST)

    def skewed(self, eng, first, second):
        first(0, 0, 0, P)

        def pair(i):
            first(i, i * 2 + 1, 1, P)
            second(i, i * 2, 0, P)
            first(i + 1, i * 2 + 2, 0, P)
            second(i, i * 2 + 1, 1, P)

        each_pair(eng, pair)
        second(PAIRS, NB - 1, 0, LAST)

    def skewed_by_two(self, first, second, eng):
        first(0, 0, 0, P)
        first(0, 1, 1, P)

        def pair(i):
            for b in range(2):
                first(i + 1, i * 2 + b + 2, b, P)
                second(i, i * 2 + b, b, P)

        pair(0)
        with eng.Fori(1, PAIRS - 1, 1) as i:
            pair(i)
        first(PAIRS, NB - 1, 0, P)
        second(PAIRS - 1, NB - 3, 0, P)
        second(PAIRS - 1, NB - 2, 1, P)
        second(PAIRS, NB - 1, 0, LAST)

    def vector(self, dve, post, before=None):
        nc, k = self.nc, self.k

        def statistics(i, t, b, rows):
            if before:
                before(i, t, b, rows)
            wait_past(dve, self.var_ok[b], i)
            dve.sem_inc(self.dve_going, 1)
            nc.vector.bn_stats(self.stats[b][:, :], flat(k.X[:, bass.ds(t, 1), :])).then_inc(self.stats_ok[b], 1)

        def aggregate(i, t, b, rows):
            dve.wait_ge(self.stats_ok[b], i + 1)
            wait_past(dve, self.mv_kept[b], i)
            dve.sem_inc(self.dve_going, 1)
            nc.vector.bn_aggr(self.mv[b][:, :], self.stats[b][:, :]).then_inc(self.var_ok[b], 1)

        def normalise(i, t, b, rows):
            if not self.norm:
                return
            wait_past(dve, self.xn_saved[b], i)
            wait_past(dve, self.turned[b], i)
            nc.vector.tensor_scalar(self.xn[b][:, :], flat(k.X[:, bass.ds(t, 1), :]), self.meanvar[:, bass.ds(t, 1), 0],
                                    self.scale[:, bass.ds(t, 1)], ALU.subtract, ALU.mult).then_inc(self.xn_ok[b], 1)

        def after(i, t, b, rows):
            dve.wait_ge(self.projected[b], i + 1)
            post(i, t, b, rows).then_inc(self.dve_done[b], 1)

        if self.norm:
            self.skewed(dve, statistics, aggregate)
            dve.wait_ge(self.std_ok, 1)
            nc.vector.reciprocal(self.scale[:, :], self.scale[:, :]).then_inc(self.scale_ok, 1)
            dve.wait_ge(self.scale_ok, 1)
        self.skewed_by_two(normalise, after, dve)

    def scalar(self, act, post=None):
        nc, k = self.nc, self.k

        def copies(i, t, b, rows):
            saved = flat(k.XN[:, bass.ds(t, 1), :])
            if self.norm:
                act.wait_ge(self.xn_ok[b], i + 1)
                nc.scalar.copy(saved, self.xn[b][:, :]).then_inc(self.xn_saved[b], 1)
            else:
                wait_past(act, self.turned[b], i)
                nc.scalar.copy(self.xn[b][:, :], saved).then_inc(self.xn_ok[b], 1)
            act.wait_ge(self.turned[b], i + 1)
            wait_past(act, self.projected[b], i)
            nc.scalar.copy(self.xnT[b][:, :, :].rearrange("p c n -> p (c n)"),
                           self.ps_turn[b][:, 0:D]).then_inc(self.xnT_ok[b], 1)

        def keep(i, t, b, rows):
            act.wait_ge(self.var_ok[b], i + 1)
            nc.scalar.copy(flat(self.meanvar[:, bass.ds(t, 1), :]), self.mv[b][:, :]).then_inc(self.mv_kept[b], 1)

        def after(i, t, b, rows):
            act.wait_ge(self.projected[b], i + 1)
            post(i, t, b, rows).then_inc(self.act_done[b], 1)

        if self.norm:
            self.blocks(act, keep)
            act.wait_ge(self.mv_kept[0], PAIRS + 1)
            act.wait_ge(self.mv_kept[1], PAIRS)
            nc.scalar.activation(self.scale[:, :], self.meanvar[:, :, 1], ACT.Sqrt, bias=k.eps[:, 0:1]).then_inc(self.std_ok, 1)
        if post:
            self.skewed(act, copies, after)
        else:
            self.blocks(act, copies)

    def tensor(self, pe, project, act_posts=False):
        nc, k = self.nc, self.k

        def turn(i, t, b, rows):
            pe.wait_ge(self.xn_ok[b], i + 1)
            wait_past(pe, self.xnT_ok[b], i)
            for c in range(DC):
                last = nc.tensor.transpose(self.ps_turn[b][:, c * P:(c + 1) * P],
                                           self.xn[b][:, c * P:(c + 1) * P], k.ident[:, :])
            last.then_inc(self.turned[b], 1)

        def products(i, t, b, rows):
            pe.wait_ge(self.xnT_ok[b], i + 1)
            wait_past(pe, self.dve_done[b], i)
            if act_posts:
                wait_past(pe, self.act_done[b], i)
            project(i, t, b, rows).then_inc(self.projected[b], 1)

        self.skewed(pe, turn, products)


def load_columns(sp, sem, dst, src):
    for c in range(DC):
        sp.dma_start(dst[:, c:c + 1], src[c * P:(c + 1) * P].rearrange("(p a) -> p a", a=1)).then_inc(sem, 16)


def load_matrix(sp, sem, dst, src):
    sp.dma_start(dst, src.rearrange("(c p) n -> p c n", p=P)).then_inc(sem, 16)


class OneHots:

    def __init__(self, nc, k, ph, name, hi, lo, key_i, part_i):
        self.nc, self.k, self.hi, self.lo, self.key_i, self.part_i = nc, k, hi, lo, key_i, part_i
        self.is_hi = [ph.sb(f"{name}_is_hi{b}", [EP, GRP, NB], BF16) for b in range(RING)]
        self.is_lo = [ph.sb(f"{name}_is_lo{b}", [EP, GRP, P], BF16) for b in range(RING)]
        self.chain = ph.sem(f"{name}_chain")

    def split(self, dve):
        v, link = self.nc.vector, Chain(dve, self.chain)
        link(v.tensor_single_scalar(self.part_i, self.key_i, 7, ALU.arith_shift_right))
        link(v.tensor_copy(self.hi, self.part_i))
        link(v.tensor_single_scalar(self.part_i, self.key_i, P - 1, ALU.bitwise_and))
        link(v.tensor_copy(self.lo, self.part_i))

    def make(self, g, b):
        cols = bass.ds(g * GRP, GRP)
        self.nc.vector.tensor_tensor(self.is_hi[b][:, :, :], self.k.ramp_b[0:EP, 0:NB].unsqueeze(1).to_broadcast([EP, GRP, NB]),
                                     self.hi[:, cols].unsqueeze(2).to_broadcast([EP, GRP, NB]), ALU.is_equal)
        return self.nc.vector.tensor_tensor(self.is_lo[b][:, :, :], self.k.ramp_b[0:EP, 0:P].unsqueeze(1).to_broadcast([EP, GRP, P]),
                                            self.lo[:, cols].unsqueeze(2).to_broadcast([EP, GRP, P]), ALU.is_equal)


def clear_counts(nc, k, bank, zeros):
    return nc.tensor.matmul(bank[0:NB, 0:P], zeros[:, 0:NB], k.ident_b[:, :], start=True, stop=False,
                            skip_group_check=True)


def count_tile(nc, hots, bank, b, j):
    return nc.tensor.matmul(bank[0:NB, 0:P], hots.is_hi[b][:, j, :], hots.is_lo[b][:, j, :], start=False, stop=False,
                            skip_group_check=True)


class Starts:

    def __init__(self, nc, k, ph, name, out, starts, bank, wide, narrow):
        self.nc, self.k, self.out, self.starts, self.bank, self.wide, self.narrow = nc, k, out, starts, bank, wide, narrow
        self.counts = ph.sb(f"{name}_counts", [NB, P])
        self.upto = ph.sb(f"{name}_upto", [NB, P])
        self.ones_row = ph.sb(f"{name}_ones_row", [NB, P])
        self.tiles_i = ph.sb(f"{name}_tiles_i", [NB, 1], I32)
        self.tiles = ph.sb(f"{name}_tiles", [NB, 4])
        self.past = ph.sb(f"{name}_past", [NB, TILES])
        self.chain, self.mid_pe, self.mid_dve = (ph.sem(f"{name}_{s}") for s in ("starts_chain", "mid_pe", "mid_dve"))

    def vector(self, dve):
        v, link, tiles, upto, counts = self.nc.vector, Chain(dve, self.chain), self.tiles, self.upto, self.counts
        link(v.memset(self.ones_row[:, :], 1.0))
        link(v.tensor_copy(counts[:, :], self.bank[0:NB, 0:P]))
        link(v.tensor_tensor_scan(upto[:, :], self.ones_row[:, :], counts[:, :], 0.0, ALU.mult, ALU.add))
        link(v.tensor_scalar(self.tiles_i[:, :], upto[:, P - 1:P], 127.0, None, ALU.add))
        link(v.tensor_single_scalar(self.tiles_i[:, :], self.tiles_i[:, :], 7, ALU.arith_shift_right))
        v.tensor_copy(tiles[:, 0:1], self.tiles_i[:, :]).then_inc(self.mid_dve, 1)
        dve.wait_ge(self.mid_dve, 1)
        dve.wait_ge(self.mid_pe, 1)
        link(v.tensor_tensor(tiles[:, 1:2], self.bank[0:NB, 256:257], tiles[:, 0:1], ALU.add))
        link(v.tensor_scalar(tiles[:, 2:3], self.bank[0:NB, 256:257], float(P), None, ALU.mult))
        v.tensor_scalar(self.past[:, :], self.k.ramp[0:NB, :], tiles[:, 1:2], None, ALU.is_ge).then_inc(self.mid_dve, 1)
        link(v.tensor_scalar(upto[:, :], upto[:, :], tiles[:, 2:3], None, ALU.add))
        link(v.tensor_tensor(self.starts[:, :], upto[:, :], counts[:, :], ALU.subtract))
        link(v.tensor_scalar(upto[:, :], upto[:, :], -1.0, 0.0, ALU.add, ALU.max))
        v.tensor_copy(tiles[:, 3:4], tiles[:, 2:3]).then_inc(self.mid_dve, 1)
        dve.wait_ge(self.mid_pe, 2)
        for q in range(2):
            w = min(512, TILES - 512 * q)
            v.tensor_scalar(self.out.local[:, 512 * q:512 * q + w], self.wide[q][:, 0:w], float(P), None, ALU.mult)
            v.tensor_copy(self.out.block[0:1, 512 * q:512 * q + w], self.wide[q][0:1, 0:w])
        v.tensor_copy(self.out.count[:, :], self.narrow[:, 0:NB])
        v.tensor_copy(self.out.last[:, :], self.narrow[:, 64:64 + NB])

    def tensor(self, pe):
        mm, k = self.nc.tensor.matmul, self.k
        pe.wait_ge(self.mid_dve, 1)
        mm(self.bank[0:NB, 256:257], k.upper[0:NB, 0:NB], self.tiles[:, 0:1], start=True, stop=True,
           skip_group_check=True).then_inc(self.mid_pe, 1)
        pe.wait_ge(self.mid_dve, 3)
        for q in range(2):
            w = min(512, TILES - 512 * q)
            mm(self.wide[q][:, 0:w], k.ones[0:NB, :], self.past[:, 512 * q:512 * q + w], start=True, stop=True)
        self.nc.tensor.transpose(self.narrow[:, 0:NB], self.counts[:, :], k.ident[0:NB, 0:NB])
        self.nc.tensor.transpose(self.narrow[:, 64:64 + NB], self.upto[:, :], k.ident[0:NB, 0:NB]).then_inc(self.mid_pe, 1)


class Places:

    HALF = 4

    def __init__(self, nc, k, ph, hots, starts, hiT, state, picked):
        self.nc, self.k, self.one, self.starts = nc, k, hots, starts
        self.hiT, self.state, self.picked = hiT, state, picked
        self.hots, self.turned, self.turn_ok = ph.sem("hots"), ph.sem("turned"), ph.sem("turn_ok")
        self.same_ok, self.earlier_ok = ph.sem("same_ok"), ph.sem("earlier_ok")
        self.state_new, self.state_ok = ph.sem("state_new"), ph.sem("state_ok")
        self.looked, self.placed, self.step = ph.sem("looked"), ph.sem("placed"), ph.sem("step")
        self.picked_ok, self.pe_going = ph.sem("picked_ok"), ph.sem("pe_going")
        self.hiT_b = [ph.sb(f"hiT_b{b}", [NB, GRP, EP], BF16) for b in range(RING)]
        self.earlier = [ph.sb(f"earlier{b}", [EP, GRP, EP], BF16) for b in range(RING)]
        self.place_f = ph.sb("place_f", [EP, GRP])
        self.ps_h = ph.ps("ps_h", [P, 512])
        self.ps_a = [ph.ps(f"ps_a{q}", [P, 512]) for q in range(2)]
        self.ps_p = [ph.ps(f"ps_p{q}", [P, 512]) for q in range(2)]
        self.ps_t = ph.ps("ps_t", [P, 1024], BF16)
        self.split = ((0, self.HALF), (1, GRP - self.HALF))


    def compare(self, dve, g, b):
        dve.wait_ge(self.same_ok, g + 1)
        for q, n in self.split:
            last = self.nc.vector.tensor_tensor(
                self.earlier[b][:, q * self.HALF:q * self.HALF + n, :],
                self.ps_a[q][0:EP, 0:n * P].rearrange("p (n e) -> p n e", n=n)[:, :, 0:EP],
                self.k.upper[0:EP, 0:EP].unsqueeze(1).to_broadcast([EP, n, EP]), ALU.mult)
        last.then_inc(self.earlier_ok, 1)

    def pick(self, dve, g, b):
        dve.wait_ge(self.looked, g + 1)
        wait_past(dve, self.step, g)
        for q, n in self.split:
            last = self.nc.vector.tensor_tensor(
                self.picked[:, q * self.HALF:q * self.HALF + n, :],
                self.ps_p[q][0:EP, 0:n * P].rearrange("p (n e) -> p n e", n=n),
                self.one.is_lo[b][:, q * self.HALF:q * self.HALF + n, :], ALU.mult)
        last.then_inc(self.picked_ok, 1)

    def vector_step(self, dve, g, b, i, write):
        if has(g - 2, GROUPS):
            self.pick(dve, g - 2, (b - 2) % RING)
        if has(g, GROUPS):
            self.compare(dve, g, b)
        if has(g - 2, GROUPS):
            dve.wait_ge(self.picked_ok, g - 1)
            wait_past(dve, self.placed, g - 2)
            self.nc.vector.tensor_reduce(self.place_f[:, :], self.picked[:, :, :], AX.X, ALU.add).then_inc(self.step, 1)
            write(g - 2, (b - 2) % RING, i + (b - 2) // RING)
        if has(g + 2, GROUPS):
            self.one.make(g + 2, (b + 2) % RING).then_inc(self.hots, 1)


    def scalar_turn(self, act, g, b):
        act.wait_ge(self.turned, g + 1)
        hot = self.ps_t[0:NB, 0:GRP * P].rearrange("p (n e) -> p n e", n=GRP)[:, :, 0:EP]
        self.nc.scalar.copy(self.hiT_b[b][:, :, :], hot)
        self.nc.scalar.copy(self.hiT[b], hot).then_inc(self.turn_ok, 1)

    def scalar_step(self, act, g, b):
        for j in range(GRP):
            act.wait_ge(self.state_new, g * GRP + j + 1)
            self.nc.scalar.copy(self.state[b][:, j, :], self.ps_h[0:NB, 0:P]).then_inc(self.state_ok, 1)
            if j == 0 and has(g + 1, GROUPS):
                self.scalar_turn(act, g + 1, (b + 1) % RING)


    def turn(self, pe, g, b):
        pe.wait_ge(self.hots, g + 1)
        wait_past(pe, self.turn_ok, g)
        pe.sem_inc(self.pe_going, 1)
        for j in range(GRP):
            last = self.nc.tensor.transpose(self.ps_t[0:NB, j * P:j * P + EP], self.one.is_hi[b][:, j, :],
                                            self.k.ident_b[0:EP, 0:EP])
        last.then_inc(self.turned, 1)

    def same(self, pe, g, b, tiles):
        if tiles[0] == 0:
            pe.wait_ge(self.turn_ok, g + 1)
            wait_past(pe, self.earlier_ok, g)
        for j in tiles:
            q, r = j // self.HALF, j % self.HALF
            last = self.nc.tensor.matmul(self.ps_a[q][0:EP, r * P:r * P + EP], self.hiT_b[b][:, j, :],
                                         self.hiT_b[b][:, j, :], start=True, stop=True)
        if tiles[-1] == GRP - 1:
            last.then_inc(self.same_ok, 1)

    def count(self, pe, g, b, j):
        pe.wait_ge(self.state_ok, g * GRP + j + 1)
        count_tile(self.nc, self.one, self.ps_h, b, j).then_inc(self.state_new, 1)

    def lookup(self, pe, g, b, tiles):
        if tiles[0] == 0:
            pe.wait_ge(self.earlier_ok, g + 1)
            wait_past(pe, self.picked_ok, g)
        for j in tiles:
            q, r = j // self.HALF, j % self.HALF
            cols = self.ps_p[q][0:EP, r * P:(r + 1) * P]
            self.nc.tensor.matmul(cols, self.hiT[b][:, j, :], self.state[b][:, j, :], start=True, stop=False)
            last = self.nc.tensor.matmul(cols, self.earlier[b][:, j, :], self.one.is_lo[b][:, j, :], start=False, stop=True)
        if tiles[-1] == GRP - 1:
            last.then_inc(self.looked, 1)

    def tensor_first(self, pe):
        self.nc.tensor.matmul(self.ps_h[0:NB, 0:P], self.k.ident[0:NB, 0:NB], self.starts[:, :], start=True, stop=False,
                              skip_group_check=True).then_inc(self.state_new, 1)
        self.turn(pe, 0, 0)
        self.same(pe, 0, 0, list(range(GRP)))

    def tensor_step(self, pe, g, b):
        here, ahead, behind = has(g, GROUPS), has(g + 1, GROUPS), has(g - 1, GROUPS)
        after, prev = (b + 1) % RING, (b - 1) % RING
        if ahead:
            self.turn(pe, g + 1, after)
        if here:
            self.count(pe, g, b, 0)
        if behind:
            self.lookup(pe, g - 1, prev, [0, 1])
        if here:
            self.count(pe, g, b, 1)
        if behind:
            self.lookup(pe, g - 1, prev, [2, 3, 4])
        if here:
            self.count(pe, g, b, 2)
        if ahead:
            self.same(pe, g + 1, after, [0, 1, 2])
        if here:
            self.count(pe, g, b, 3)
        if ahead:
            self.same(pe, g + 1, after, [3, 4])
        if here:
            self.count(pe, g, b, 4)


def sort_edges(nc, k):
    out = k.graph[0]
    with Phase(nc, "sort") as ph:
        key_i = [ph.sb(f"key_i{n}", [EP, ET], I32) for n in range(2)]
        part_i = ph.sb("part_i", [EP, ET], I32)
        hi, lo = ([ph.sb(f"{s}{n}", [EP, ET], BF16) for n in range(2)] for s in ("hi", "lo"))
        pairs = [ph.sb(f"pairs{n}", [EP, ET, 2]) for n in range(2)]
        zeros = ph.sb("zeros", [P, NB], BF16)
        free = ph.sb("free", [P, TILES // 4, 2])
        hots = [OneHots(nc, k, ph, f"by{n}", hi[n][:, :], lo[n][:, :], key_i[n][:, :], part_i[:, :]) for n in range(2)]
        starts, next_starts = ph.sb("starts", [NB, P]), ph.sb("next_starts", [NB, P])
        hiT = [ph.sb(f"hiT{b}", [NB, GRP, EP]) for b in range(RING)]
        state = [ph.sb(f"state{b}", [NB, GRP, P]) for b in range(RING)]
        picked = ph.sb("picked", [EP, GRP, P])
        place = [ph.sb(f"place{b}", [EP, GRP], I32) for b in range(RING)]
        row = [ph.sb(f"row{b}", [EP, GRP, 2]) for b in range(RING)]
        pl = Places(nc, k, ph, hots[0], starts, [t[:, :, :] for t in hiT], [t[:, :, :] for t in state], picked)
        ps_next = ph.ps("ps_next", [P, 512])

        loaded, filled, free_set, paired = (ph.sem(s) for s in ("loaded", "filled", "free_set", "paired"))
        onehot = [ph.sem(f"onehot{b}") for b in range(2)]
        counted = [ph.sem(f"counted{b}") for b in range(2)]
        first = Starts(nc, k, ph, "first", out, starts, pl.ps_h, pl.ps_a, pl.ps_p[0])

        with nc.Block() as block:

            @block.sync
            def _(sp):
                for n in range(2):
                    keys = k.dst if n else k.src
                    sp.dma_start(key_i[n][:, :], keys.rearrange("(p t) -> p t", p=EP)).then_inc(loaded, 16)
                sp.wait_ge(free_set, 2)
                for n in range(2):
                    for q in range(4):
                        sp.dma_start(k.graph[n].table.rearrange("(q p t) a -> q p t a", q=4, p=P)[q], free[:, :, :]).then_inc(filled, 16)
                sp.wait_ge(paired, 4)
                sp.dma_start(k.pairs, pairs[1][:, :, :]).then_inc(filled, 16)
                sp.wait_ge(filled, 144)

            @block.vector
            def _(dve):
                nc.vector.memset(free[:, :, 0], 0.0).then_inc(free_set, 1)
                nc.vector.memset(free[:, :, 1], -1.0).then_inc(free_set, 1)
                nc.vector.memset(zeros[:, :], 0.0).then_inc(free_set, 1)
                dve.wait_ge(loaded, 32)
                hots[0].split(dve)
                for b in range(2):
                    hots[0].make(b, b).then_inc(onehot[b], 1)
                with dve.Fori(1, LOOPS, 1) as i:
                    for b in range(2):
                        dve.wait_ge(counted[b], i)
                        hots[0].make(i * 2 + b, b).then_inc(onehot[b], 1)
                for b in range(2):
                    dve.wait_ge(counted[b], LOOPS)
                first.vector(dve)
                hots[1].split(dve)

            @block.scalar
            def _(act):
                act.wait_ge(loaded, 32)
                for n in range(2):
                    nc.scalar.copy(pairs[n][:, :, 0], key_i[1 - n][:, :]).then_inc(paired, 1)
                    nc.scalar.copy(pairs[n][:, :, 1], key_i[n][:, :]).then_inc(paired, 1)

            @block.tensor
            def _(pe):
                pe.wait_ge(free_set, 3)
                clear_counts(nc, k, pl.ps_h, zeros)
                with pe.Fori(0, LOOPS, 1) as i:
                    for b in range(2):
                        pe.wait_ge(onehot[b], i + 1)
                        for j in range(GRP):
                            last = count_tile(nc, hots[0], pl.ps_h, b, j)
                        last.then_inc(counted[b], 1)
                first.tensor(pe)

        scattered = [[ph.sem(f"scattered{b}_{j}") for j in range(GRP)] for b in range(RING)]
        starts_out = ph.sem("starts_out")
        next_hot, next_counted, pool_going = ph.sem("next_hot"), ph.sem("next_counted"), ph.sem("pool_going")
        second = Starts(nc, k, ph, "second", k.graph[1], next_starts, ps_next, pl.ps_a, pl.ps_p[0])

        with nc.Block() as block:

            @block.vector
            def _(dve):
                def write(g, b, i):
                    if not isinstance(g, int) or g >= RING:
                        for j in range(GRP):
                            dve.wait_ge(scattered[b][j], i * 16)
                    nc.vector.tensor_copy(row[b][:, :, :], pairs[0][:, bass.ds(g * GRP, GRP), :])
                    dve.wait_ge(pl.step, g + 1)
                    nc.vector.tensor_copy(place[b][:, :], pl.place_f[:, :]).then_inc(pl.placed, 1)

                def group(g, b, i):
                    pl.vector_step(dve, g, b, i, write)
                    if has(g, GROUPS):
                        wait_past(dve, next_counted, g - (RING - 1))
                        hots[1].make(g, b).then_inc(next_hot, 1)

                for g in range(2):
                    hots[0].make(g, g).then_inc(pl.hots, 1)
                staged(dve, GROUPS, RING, group, drain=2)
                dve.wait_ge(next_counted, GROUPS)
                second.vector(dve)

            @block.sync
            def _(sp):
                sp.wait_ge(second.mid_dve, 3)
                sp.dma_start(k.starts, next_starts[:, :]).then_inc(starts_out, 16)
                sp.wait_ge(starts_out, 16)

            @block.scalar
            def _(act):
                pl.scalar_turn(act, 0, 0)
                staged(act, GROUPS, RING, lambda g, b, i: pl.scalar_step(act, g, b))

            @block.tensor
            def _(pe):
                def group(g, b, i):
                    pl.tensor_step(pe, g, b)
                    if has(g - 1, GROUPS):
                        pe.wait_ge(next_hot, g)
                        for j in range(GRP):
                            last = count_tile(nc, hots[1], ps_next, (b - 1) % RING, j)
                        last.then_inc(next_counted, 1)

                clear_counts(nc, k, ps_next, zeros)
                pl.tensor_first(pe)
                staged(pe, GROUPS, RING, group, drain=1)
                second.tensor(pe)

            @block.gpsimd
            def _(pool):
                def group(g, b):
                    pool.wait_ge(pl.placed, g + 1)
                    pool.sem_inc(pool_going, 1)
                    for j in range(GRP):
                        pool.indirect_dma_start(out=out.table, out_offset=bass.IndirectOffsetOnAxis(ap=place[b][:, j:j + 1], axis=0),
                                                in_=row[b][:, j, :], in_offset=None).then_inc(scattered[b][j], 16)

                rounds(pool, GROUPS, RING, group)
                for b in range(RING):
                    for j in range(GRP):
                        pool.wait_ge(scattered[b][j], GROUPS // RING * 16)

    tile_order(nc, k, "order0", out)


def tile_order(nc, k, name, out):
    CH = -(-TILES // P)
    with Phase(nc, name) as ph:
        tab = ph.sb("tab", [P, CH, 2 * P])
        ps = [ph.ps(f"ps{q}", [P, 512]) for q in range(2)]
        reloaded, turned, moved = [ph.sem(f"reloaded{c}") for c in range(CH)], ph.sem("turned"), ph.sem("moved")
        with nc.Block() as block:

            @block.sync
            def _(sp):
                t = out.table.rearrange("(t p) a -> t (p a)", p=P)
                for c in range(CH):
                    n = min(P, TILES - c * P)
                    sp.dma_start(tab[0:n, c, :], t[c * P:c * P + n, :]).then_inc(reloaded[c], 16)

            @block.tensor
            def _(pe):
                for c in range(CH):
                    n = min(P, TILES - c * P)
                    pe.wait_ge(reloaded[c], 16)
                    wait_past(pe, moved, c - 1)
                    for a in range(2):
                        last = nc.tensor.transpose(ps[c % 2][:, a * P:a * P + n],
                                                   tab[0:n, c, :].rearrange("t (p a) -> t a p", a=2)[:, a, :], k.ident[0:n, 0:n])
                    last.then_inc(turned, 1)

            @block.vector
            def _(dve):
                for c in range(CH):
                    n = min(P, TILES - c * P)
                    cols = out.local[:, c * P:c * P + n]
                    dve.wait_ge(turned, c + 1)
                    nc.vector.tensor_copy(out.other[:, c * P:c * P + n], ps[c % 2][:, 0:n])
                    nc.vector.tensor_tensor(cols, ps[c % 2][:, P:P + n], cols, ALU.subtract).then_inc(moved, 1)


class Scatter:

    def __init__(self, nc, k, ph, first, chunk, chunks):
        assert chunks % 2 == 0
        self.k, self.first, self.chunk, self.chunks = k, first, chunk, chunks
        self.place = [ph.sb(f"place{b}", [EP, chunk], I32) for b in range(2)]
        self.row = [ph.sb(f"row{b}", [EP, chunk, 2]) for b in range(2)]
        self.in_ok = [ph.sem(f"pairs_in{b}") for b in range(2)]
        self.out_ok = [[ph.sem(f"scattered{b}_{j}") for j in range(chunk)] for b in range(2)]
        self.going = ph.sem("scatter_going")

    def load(self, eng, c, b, i):
        if not isinstance(i, int) or i > 0:
            for j in range(self.chunk):
                eng.wait_ge(self.out_ok[b][j], i * 16)
        cols = bass.ds(self.first + c * self.chunk, self.chunk)
        eng.dma_start(self.place[b][:, :], self.k.places[:, cols]).then_inc(self.in_ok[b], 16)
        eng.dma_start(self.row[b][:, :, :], self.k.pairs[:, cols, :]).then_inc(self.in_ok[b], 16)

    def send(self, pool, c, b, i):
        pool.wait_ge(self.in_ok[b], i * 32 + 32)
        pool.sem_inc(self.going, 1)
        for j in range(self.chunk):
            pool.indirect_dma_start(out=self.k.graph[1].table,
                                    out_offset=bass.IndirectOffsetOnAxis(ap=self.place[b][:, j:j + 1], axis=0),
                                    in_=self.row[b][:, j, :], in_offset=None).then_inc(self.out_ok[b][j], 16)

    def feed(self, eng):
        staged(eng, self.chunks, 2, lambda c, b, i: self.load(eng, c, b, i))

    def run(self, pool):
        staged(pool, self.chunks, 2, lambda c, b, i: self.send(pool, c, b, i))
        self.left(pool)

    def left(self, pool):
        for b in range(2):
            for j in range(self.chunk):
                pool.wait_ge(self.out_ok[b][j], 16 * (self.chunks // 2))


def attention_tables(nc, k):
    with Phase(nc, "l0") as ph:
        wcat = ph.sb("wcat", [P, DC, D + 16])
        wh = ph.sb("wh", [P, DC, D])
        whT = ph.sb("whT", [P, DC, D])
        amat = ph.sb("amat", [P, DC, 16])
        bias_k = ph.sb("bias_k", [P, D])
        bias_q = ph.sb("bias_q", [P, DC])
        bias_v = ph.sb("bias_v", [1, D])
        gamma = ph.sb("gamma", [P, DC])
        beta = ph.sb("beta", [P, DC])
        wq = ph.sb("wq", [P, DC, D])
        wqT = ph.sb("wqT", [P, DC, D])
        wv = ph.sb("wv", [P, DC, D])
        keys = ph.sb("keys", [P, NB, D])
        kmax = ph.sb("kmax", [P, D])
        rows_out = [ph.sb(f"rows{b}", [P, ROW]) for b in range(2)]
        ps_k = [ph.ps(f"ps_k{b}", [P, 512]) for b in range(2)]
        ps_h = [ph.ps(f"ps_h{b}", [P, 512]) for b in range(2)]
        ps_m = ph.ps("ps_m", [P, 2, 512])
        tok = Tokens(nc, k, ph)

        loaded, cleared = ph.sem("loaded"), ph.sem("cleared")
        w_products, w_copied, score_w = ph.sem("w_products"), ph.sem("w_copied"), ph.sem("score_w")
        key_ok = ph.sem("key_ok")
        row_out = [ph.sem(f"row_out{b}") for b in range(2)]
        n_loads = 3 + DC + 2 + 3 * DC + 2 * HEADS

        with nc.Block() as block:

            @block.sync
            def _(sp):
                sp.wait_ge(cleared, 1)
                load_matrix(sp, loaded, wcat[:, :, 0:D], k.W_qk[1])
                load_matrix(sp, loaded, wq[:, :, :], k.W_qk[0])
                load_matrix(sp, loaded, wv[:, :, :], k.W_v)
                for c in range(DC):
                    sp.dma_start(wh[:, c, :].rearrange("p (h d) -> p h d", h=HEADS),
                                 k.gnn_W[:, c * P:(c + 1) * P, :].rearrange("h p d -> p h d")).then_inc(loaded, 16)
                sp.dma_start(bias_k[:, :], k.b_qk[1].partition_broadcast(P)).then_inc(loaded, 16)
                sp.dma_start(bias_v[:, :], k.b_v.rearrange("(a n) -> a n", a=1)).then_inc(loaded, 16)
                load_columns(sp, loaded, bias_q, k.b_qk[0])
                load_columns(sp, loaded, gamma, k.gamma)
                load_columns(sp, loaded, beta, k.beta)
                for h in range(HEADS):
                    for s in range(2):
                        r = (h * HD) % P
                        sp.dma_start(amat[r:r + HD, h * HD // P, s * HEADS + h:s * HEADS + h + 1],
                                     k.gnn_a[h, s * HD:(s + 1) * HD].rearrange("(p a) -> p a", a=1)).then_inc(loaded, 16)

                def store(i, t, b, rows):
                    sp.wait_ge(tok.act_done[b], i + 1)
                    sp.wait_ge(tok.dve_done[b], i + 1)
                    sp.dma_start(k.hs[bass.ds(t * P, rows), :], rows_out[b][0:rows, :]).then_inc(row_out[b], 16)
                    sp.dma_start(k.scores_table[bass.ds(t * P, rows), :], rows_out[b][0:rows, D:ROW]).then_inc(row_out[b], 16)

                tok.blocks(sp, store)
                sp.wait_ge(row_out[0], 32 * (PAIRS + 1))
                sp.wait_ge(row_out[1], 32 * PAIRS)

            @block.vector
            def _(dve):
                nc.vector.memset(kmax[:, :], -BIG)
                nc.vector.memset(amat[:, :, :], 0.0).then_inc(cleared, 1)
                dve.wait_ge(w_products, 1)
                nc.vector.tensor_copy(whT[:, :, :].rearrange("p c n -> p (c n)"), ps_m[:, 0, :]).then_inc(w_copied, 1)
                dve.wait_ge(w_products, 2)
                dve.wait_ge(loaded, 16 * n_loads)
                for c in range(DC):
                    nc.vector.tensor_copy(wcat[:, c, D:D + 16], ps_m[:, 1, c * 16:(c + 1) * 16]).then_inc(score_w, 1)

                def post(i, t, b, rows):
                    wait_past(dve, row_out[b], i * 32)
                    nc.vector.tensor_copy(rows_out[b][:, D:ROW], ps_k[b][:, D + 8:D + 16])
                    nc.vector.tensor_copy(flat(k.sdm[:, bass.ds(t, 1), 0:HEADS]), ps_k[b][:, D:D + 8])
                    key = flat(keys[:, bass.ds(t, 1), :])
                    nc.vector.tensor_tensor(key, ps_k[b][:, 0:D], bias_k[:, :], ALU.add).then_inc(key_ok, 1)
                    dve.wait_ge(key_ok, t + 1)
                    wait_past(dve, tok.dve_done[1 - b], i + b)
                    return nc.vector.tensor_tensor(kmax[0:rows, :], kmax[0:rows, :], key[0:rows, :], ALU.max)

                tok.vector(dve, post)

            @block.scalar
            def _(act):
                def post(i, t, b, rows):
                    wait_past(act, row_out[b], i * 32)
                    return nc.scalar.copy(rows_out[b][:, 0:D], ps_h[b][:, 0:D])

                tok.scalar(act, post)

            @block.tensor
            def _(pe):
                pe.wait_ge(loaded, 16 * n_loads)
                for c in range(DC):
                    for d in range(DC):
                        last = nc.tensor.transpose(ps_m[:, 0, d * D + c * P:d * D + (c + 1) * P],
                                                   wh[:, c, d * P:(d + 1) * P], k.ident[:, :])
                last.then_inc(w_products, 1)
                pe.wait_ge(w_copied, 1)
                for c in range(DC):
                    for d in range(DC):
                        last = nc.tensor.matmul(ps_m[:, 1, c * 16:(c + 1) * 16], whT[:, d, c * P:(c + 1) * P],
                                                amat[:, d, :], start=(d == 0), stop=(d == DC - 1))
                last.then_inc(w_products, 1)
                pe.wait_ge(score_w, DC)

                def project(i, t, b, rows):
                    for c in range(DC):
                        nc.tensor.matmul(ps_k[b][:, 0:D + 16], tok.xnT[b][:, c, :], wcat[:, c, :], start=(c == 0), stop=(c == DC - 1))
                    for c in range(DC):
                        last = nc.tensor.matmul(ps_h[b][:, 0:D], tok.xnT[b][:, c, :], wh[:, c, :],
                                                start=(c == 0), stop=(c == DC - 1))
                    return last

                tok.tensor(pe, project, act_posts=True)

        chain, pe_step, diag_ok = ph.sem("chain"), ph.sem("pe_step"), ph.sem("diag_ok")
        shifted = [ph.sem(f"shifted{b}") for b in range(2)]
        exp_ok = [ph.sem(f"exp_ok{b}") for b in range(2)]
        exp_used = [ph.sem(f"exp_used{b}") for b in range(2)]
        den_row, den_col = ph.sem("den_row"), ph.sem("den_col")
        max_ok, copied, std_done, m_ok = ph.sem("max_ok"), ph.sem("copied"), ph.sem("std_done"), ph.sem("m_ok")
        kd, ek = tok.xn, [rows_out[b][:, 0:D] for b in range(2)]
        peak, diag, peaks = ph.sb("peak", [P, DC]), tok.xnT[0], kmax
        grams, lam = whT, wh
        gramsT = whT
        rden, st6, mv2, std2 = ph.sb("rden", [P, DC]), ph.sb("st6", [P, DC, 6]), ph.sb("mv2", [P, DC, 2]), ph.sb("std2", [P, DC, 2])
        ps_g = ps_k
        ps_x = ps_h

        with nc.Block() as block:

            @block.tensor
            def _(pe):
                for c in range(DC):
                    last = nc.tensor.transpose(ps_m[:, 0, c * P:(c + 1) * P], kmax[:, c * P:(c + 1) * P], k.ident[:, :])
                last.then_inc(pe_step, 1)
                pe.wait_ge(diag_ok, DC)
                nc.tensor.matmul(ps_m[:, 1, 0:D], k.ones[:, :], diag[:, :, :].rearrange("p c n -> p (c n)"),
                                 start=True, stop=True).then_inc(pe_step, 1)

                def gram(i, t, b, rows, start, stop):
                    pe.wait_ge(exp_ok[b], i + 1)
                    for c in range(DC):
                        nc.tensor.matmul(ps_g[c][:, 0:D], ek[b][0:rows, c * P:(c + 1) * P],
                                         flat(k.XN[0:rows, bass.ds(t, 1), :]), start=start, stop=stop, skip_group_check=True)
                    nc.tensor.matmul(ps_x[0][0:1, 0:D], k.ones[0:rows, 0:1], ek[b][0:rows, :],
                                     start=start, stop=stop, skip_group_check=True).then_inc(exp_used[b], 1)

                gram(0, NB - 1, 0, LAST, True, False)

                def both(i):
                    gram(i, i * 2, 1, P, False, False)
                    gram(i + 1, i * 2 + 1, 0, P, False, False)

                each_pair(pe, both)
                pe.wait_ge(den_row, 1)
                for c in range(DC):
                    last = nc.tensor.matmul(ps_x[1][:, c:c + 1], k.mixb[:, c * P:(c + 1) * P], k.ones[0:1, 0:1],
                                            start=True, stop=True)
                last.then_inc(den_col, 1)
                pe.wait_ge(copied, 1)
                for src, q in ((grams, 0), (wq, 1)):
                    for c in range(DC):
                        for d in range(DC):
                            last = nc.tensor.transpose(ps_m[:, q, d * D + c * P:d * D + (c + 1) * P],
                                                       src[:, c, d * P:(d + 1) * P], k.ident[:, :])
                last.then_inc(pe_step, 1)
                pe.wait_ge(copied, 3)
                for m in range(DC):
                    for c in range(DC):
                        nc.tensor.matmul(tok.ps_turn[m][:, 0:D], gramsT[:, c, m * P:(m + 1) * P], wv[:, c, :],
                                         start=(c == 0), stop=False)
                    last = nc.tensor.matmul(tok.ps_turn[m][:, 0:D], k.ones[0:1, :], bias_v[:, :], start=False, stop=True)
                last.then_inc(pe_step, 1)
                pe.wait_ge(m_ok, 1)
                for m in range(DC):
                    for d in range(DC):
                        nc.tensor.matmul(ps_g[m][:, 0:D], wqT[:, d, m * P:(m + 1) * P], lam[:, d, :],
                                         start=(d == 0), stop=(d == DC - 1))
                for d in range(DC):
                    last = nc.tensor.matmul(ps_x[0][0:1, 0:D], bias_q[:, d:d + 1], lam[:, d, :],
                                            start=(d == 0), stop=(d == DC - 1))
                last.then_inc(pe_step, 1)

            @block.vector
            def _(dve):
                link = Chain(dve, chain)
                dve.wait_ge(pe_step, 1)
                for c in range(DC):
                    link(nc.vector.tensor_reduce(peak[:, c:c + 1], ps_m[:, 0, c * P:(c + 1) * P], AX.X, ALU.max))
                    nc.vector.tensor_scalar(diag[:, c, :], k.ident[:, :], peak[:, c:c + 1], None, ALU.mult).then_inc(diag_ok, 1)
                dve.wait_ge(pe_step, 2)
                link(nc.vector.tensor_copy(peaks[:, :], ps_m[:, 1, 0:D]))

                def shift(i, t, b, rows):
                    wait_past(dve, exp_ok[b], i)
                    nc.vector.tensor_tensor(kd[b][0:rows, :], flat(keys[0:rows, bass.ds(t, 1), :]),
                                            peaks[0:rows, :], ALU.subtract).then_inc(shifted[b], 1)

                shift(0, NB - 1, 0, LAST)

                def both(i):
                    shift(i, i * 2, 1, P)
                    shift(i + 1, i * 2 + 1, 0, P)

                each_pair(dve, both)
                dve.wait_ge(exp_used[0], PAIRS + 1)
                dve.wait_ge(exp_used[1], PAIRS)
                nc.vector.tensor_copy(k.mixb[:, :], ps_x[0][0:1, 0:D]).then_inc(den_row, 1)
                dve.wait_ge(den_col, 1)
                for c in range(DC):
                    link(nc.vector.reciprocal(rden[:, c:c + 1], ps_x[1][:, c:c + 1]))
                    link(nc.vector.tensor_scalar(grams[:, c, :], ps_g[c][:, 0:D], rden[:, c:c + 1], None, ALU.mult))
                nc.vector.tensor_copy(std2[:, 0, :], k.ones[:, 0:2]).then_inc(copied, 1)
                dve.wait_ge(pe_step, 3)
                nc.vector.tensor_copy(gramsT[:, :, :].rearrange("p c n -> p (c n)"), ps_m[:, 0, :]).then_inc(copied, 1)
                nc.vector.tensor_copy(wqT[:, :, :].rearrange("p c n -> p (c n)"), ps_m[:, 1, :]).then_inc(copied, 1)
                dve.wait_ge(pe_step, 4)
                for m in range(DC):
                    link(nc.vector.bn_stats(st6[:, m, :], tok.ps_turn[m][:, 0:D]))
                    last = nc.vector.bn_aggr(mv2[:, m, :], st6[:, m, :])
                    link(last)
                nc.vector.tensor_copy(std2[:, 0, 0:1], k.ones[:, 0:1]).then_inc(max_ok, 1)
                dve.wait_ge(std_done, 1)
                for m in range(DC):
                    link(nc.vector.reciprocal(std2[:, m, 1:2], std2[:, m, 0:1]))
                    link(nc.vector.tensor_scalar(lam[:, m, :], tok.ps_turn[m][:, 0:D], mv2[:, m, 0:1], std2[:, m, 1:2],
                                                 ALU.subtract, ALU.mult))
                    link(nc.vector.tensor_scalar(lam[:, m, :], lam[:, m, :], gamma[:, m:m + 1], beta[:, m:m + 1],
                                                 ALU.mult, ALU.add))
                nc.vector.tensor_copy(peak[:, 0:1], k.ones[:, 0:1]).then_inc(m_ok, 1)
                dve.wait_ge(pe_step, 5)
                for m in range(DC):
                    nc.vector.tensor_copy(k.mixw[:, m, :], ps_g[m][:, 0:D])
                nc.vector.tensor_copy(k.mixb[:, :], ps_x[0][0:1, 0:D])

            @block.scalar
            def _(act):
                def exps(i, b, rows):
                    act.wait_ge(shifted[b], i + 1)
                    wait_past(act, exp_used[b], i)
                    nc.scalar.activation(ek[b][0:rows, :], kd[b][0:rows, :], ACT.Exp).then_inc(exp_ok[b], 1)

                exps(0, 0, LAST)

                def both(i):
                    exps(i, 1, P)
                    exps(i + 1, 0, P)

                each_pair(act, both)
                act.wait_ge(max_ok, 1)
                for m in range(DC):
                    last = nc.scalar.activation(std2[:, m, 0:1], mv2[:, m, 1:2], ACT.Sqrt, bias=k.eps[:, 0:1])
                last.then_inc(std_done, 1)

    add_mix(nc, k, "l0mix")


def add_mix(nc, k, name):
    with Phase(nc, name) as ph:
        tok = Tokens(nc, k, ph, norm=False)
        ps_y = [ph.ps(f"ps_y{b}", [P, 512]) for b in range(2)]
        ps_bias = ph.ps("ps_bias", [P, 512])
        bias_ok, biased = ph.sem("bias_ok"), ph.sem("biased")
        with nc.Block() as block:

            @block.vector
            def _(dve):
                dve.wait_ge(bias_ok, 1)

                def post(i, t, b, rows):
                    x = flat(k.X[:, bass.ds(t, 1), :])
                    nc.vector.tensor_tensor(x, x, ps_bias[:, 0:D], ALU.add).then_inc(biased, 1)
                    dve.wait_ge(biased, t + 1)
                    return nc.vector.tensor_tensor(x, x, ps_y[b][:, 0:D], ALU.add)

                tok.vector(dve, post)

            @block.scalar
            def _(act):
                tok.scalar(act)

            @block.tensor
            def _(pe):
                nc.tensor.matmul(ps_bias[:, 0:D], k.ones[0:1, :], k.mixb[:, :], start=True, stop=True).then_inc(bias_ok, 1)

                def project(i, t, b, rows):
                    for c in range(DC):
                        last = nc.tensor.matmul(ps_y[b][:, 0:D], tok.xnT[b][:, c, :], k.mixw[:, c, :],
                                                start=(c == 0), stop=(c == DC - 1))
                    return last

                tok.tensor(pe, project)


class Carve:

    def __init__(self, memory):
        self.memory, self.at = memory, 0

    def take(self, rows, *dims):
        size = dims[0] * (dims[1] if len(dims) > 1 else 1)
        part = self.memory[0:rows, self.at:self.at + size]
        self.at += size
        return part.rearrange("p (a b) -> p a b", a=dims[0]) if len(dims) > 1 else part


def park(nc, k):
    with Phase(nc, "park") as ph:
        parked = ph.sem("parked")
        with nc.Block() as block:

            @block.sync
            def _(sp):
                sp.dma_start(k.parked, k.X[:, :, :]).then_inc(parked, 16)
                sp.wait_ge(parked, 16)


def segment_peaks(nc, k):
    g = k.graph[0]
    FOLD = SLOTS // P
    with Phase(nc, "peaks") as ph:
        other = ph.sb("other", [P, FOLD], I32)
        slot = [ph.sb(f"slot{b}", [P, PGRP], I32) for b in range(RING)]
        got = [ph.sb(f"got{b}", [P, PGRP, HEADS]) for b in range(RING)]
        scores = ph.sb("scores", [P, HEADS, FOLD])
        edge_keys = ph.sb("edge_keys", [P, 8])
        keyT = ph.sb("keyT", [8, P])
        tails = ph.sb("tails", [P, 16])
        tailsT = ph.sb("tailsT", [8, P])
        pen = ph.sb("pen", [8, P])
        carry = ph.sb("carry", [8, P + 1])
        carried = ph.sb("carried", [P, 8])
        in_xn, in_x = Carve(k.work), Carve(k.X[:, :, :].rearrange("p t d -> p (t d)"))
        flip = in_xn.take(P, FOLD, HEADS)
        tab = in_xn.take(P, FOLD, 2)
        fresh = in_xn.take(P, FOLD)
        first = in_xn.take(P, FOLD)
        cand = in_xn.take(P, FOLD)
        hiT = [in_x.take(NB, GRP, EP) for b in range(RING)]
        state = [in_x.take(NB, GRP, P) for b in range(RING)]
        picked = in_x.take(EP, GRP, P)
        hi, lo = (ph.sb(s, [EP, ET], BF16)[:, :] for s in ("hi", "lo"))
        z, peak = in_x.take(P, NB, HEADS), in_x.take(P, NB, HEADS)
        key_i = ph.sb("key_i", [EP, ET], I32)
        hots = OneHots(nc, k, ph, "by_destination", hi, lo, key_i[:, :], k.graph[1].other[0:EP, 0:ET])
        starts = ph.sb("starts", [NB, P])
        pl = Places(nc, k, ph, hots, starts, hiT, state, picked)
        ps = ph.ps("ps", [P, 512])

        loaded, ready, chain = ph.sem("loaded"), ph.sem("ready"), ph.sem("chain")
        slots_ok, fetched = ph.sem("slots_ok"), [[ph.sem(f"fetched{b}_{j}") for j in range(PGRP)] for b in range(RING)]
        kept, pe_ok, pe_go, stored, node_got = ph.sem("kept"), ph.sem("pe_ok"), ph.sem("pe_go"), ph.sem("stored"), ph.sem("node_got")
        pool_going, keys_in = ph.sem("pool_going"), ph.sem("keys_in")
        with nc.Block() as block:

            @block.sync
            def _(sp):
                sp.dma_start(tab, g.table.rearrange("(p t) a -> p t a", p=P)).then_inc(loaded, 16)
                sp.dma_start(key_i[:, :], k.dst.rearrange("(p t) -> p t", p=EP)).then_inc(keys_in, 16)
                sp.dma_start(starts[:, :], k.starts).then_inc(keys_in, 16)
                sp.wait_ge(ready, 2)
                sp.dma_start(k.peak_table.rearrange("(p t) a -> p t a", p=P), flip).then_inc(stored, 16)
                sp.dma_start(k.places, key_i[:, :]).then_inc(stored, 16)
                sp.wait_ge(stored, 32)

            @block.gpsimd
            def _(pool):
                def fetch(g_, b):
                    pool.wait_ge(slots_ok, g_ + 1)
                    wait_past(pool, kept, g_ - (RING - 1))
                    pool.sem_inc(pool_going, 1)
                    for j in range(PGRP):
                        pool.indirect_dma_start(out=got[b][:, j, :], out_offset=None, in_=k.scores_table,
                                                in_offset=bass.IndirectOffsetOnAxis(ap=slot[b][:, j:j + 1], axis=0)).then_inc(fetched[b][j], 16)

                rounds(pool, PGROUPS // RING * RING, RING, fetch)
                for g_ in range(PGROUPS // RING * RING, PGROUPS):
                    fetch(g_, g_ % RING)
                pool.wait_ge(stored, 32)
                for t in range(NB):
                    pool.indirect_dma_start(out=peak[:, t, :], out_offset=None, in_=k.peak_table,
                                            in_offset=bass.IndirectOffsetOnAxis(ap=g.last[:, t:t + 1], axis=0)).then_inc(node_got, 16)

            @block.scalar
            def _(act):
                act.wait_ge(ready, 1)

                def indices(g_, b, i):
                    if not isinstance(i, int) or i:
                        for j in range(PGRP):
                            act.wait_ge(fetched[b][j], i * 16)
                    nc.scalar.copy(slot[b][:, :], other[:, bass.ds(g_ * PGRP, PGRP)]).then_inc(slots_ok, 1)

                def group(g_, b, i):
                    if has(g_ + 3, PGROUPS):
                        indices(g_ + 3, (b + 3) % RING, i + (b + 3) // RING)
                    if has(g_, GROUPS):
                        pl.scalar_step(act, g_, b)

                for b in range(3):
                    indices(b, b, 0)
                pl.scalar_turn(act, 0, 0)
                staged(act, GROUPS, RING, group, drain=PGROUPS - GROUPS)

            @block.vector
            def _(dve):
                link = Chain(dve, chain)
                dve.wait_ge(loaded, 16)
                nc.vector.tensor_copy(other[:, :], tab[:, :, 0]).then_inc(ready, 1)
                dve.wait_ge(keys_in, 32)
                hots.split(dve)
                link(nc.vector.tensor_tensor(fresh[:, 1:FOLD], tab[:, 1:FOLD, 1], tab[:, 0:FOLD - 1, 1], ALU.not_equal))
                link(nc.vector.memset(fresh[:, 0:1], 1.0))
                link(nc.vector.tensor_scalar(fresh[:, :], fresh[:, :], -BIG, None, ALU.mult))
                link(nc.vector.tensor_scalar(first[:, :], tab[:, :, 1], tab[:, 0, 1:2], -BIG, ALU.not_equal, ALU.mult))
                link(nc.vector.tensor_copy(edge_keys[:, 0:1], tab[:, 0, 1:2]))
                link(nc.vector.tensor_copy(edge_keys[:, 1:2], tab[:, FOLD - 1, 1:2]))

                def keep(g_, b, i):
                    for j in range(PGRP):
                        dve.wait_ge(fetched[b][j], i * 16 + 16)
                    nc.vector.tensor_copy(scores[:, :, bass.ds(g_ * PGRP, PGRP)], got[b][:, :, :].rearrange("p t h -> p h t")).then_inc(kept, 1)

                def write(g_, b, i):
                    dve.wait_ge(pl.step, g_ + 1)
                    nc.vector.tensor_copy(key_i[:, bass.ds(g_ * GRP, GRP)], pl.place_f[:, :]).then_inc(pl.placed, 1)

                def group(g_, b, i):
                    pl.vector_step(dve, g_, b, i, write)
                    if has(g_, PGROUPS):
                        keep(g_, b, i)

                for g_ in range(2):
                    hots.make(g_, g_).then_inc(pl.hots, 1)
                staged(dve, GROUPS, RING, group, drain=PGROUPS - GROUPS)
                dve.wait_ge(kept, PGROUPS)
                for h in range(HEADS):
                    link(nc.vector.tensor_tensor_scan(cand[:, :], fresh[:, :], scores[:, h, :], -BIG, ALU.add, ALU.max))
                    link(nc.vector.tensor_copy(scores[:, h, :], cand[:, :]))
                for c in range(2):
                    link(nc.vector.tensor_copy(tails[:, c * 8:c * 8 + 8], (edge_keys[:, c:c + 1] if c else edge_keys[:, 0:1]).to_broadcast([P, 8])))
                pe_go_ins = nc.vector.tensor_copy(tails[:, 0:1], edge_keys[:, 0:1])
                link(pe_go_ins)
                nc.vector.tensor_copy(carried[:, :], scores[:, :, FOLD - 1]).then_inc(pe_go, 1)
                dve.wait_ge(pe_ok, 1)
                link(nc.vector.tensor_copy(tailsT[:, :], ps[0:8, 2 * P:3 * P]))
                link(nc.vector.tensor_copy(keyT[:, :], ps[0:8, 0:P]))
                link(nc.vector.memset(pen[:, :], 1.0))
                link(nc.vector.tensor_tensor(pen[:, 1:P], keyT[:, 1:P], ps[0:8, P:2 * P - 1], ALU.not_equal))
                link(nc.vector.tensor_scalar(pen[:, :], pen[:, :], -BIG, None, ALU.mult))
                link(nc.vector.tensor_tensor(keyT[:, :], keyT[:, :], ps[0:8, P:2 * P], ALU.not_equal))
                link(nc.vector.tensor_scalar(keyT[:, :], keyT[:, :], -BIG, None, ALU.mult))
                link(nc.vector.tensor_tensor(keyT[:, :], keyT[:, :], pen[:, :], ALU.min))
                link(nc.vector.memset(carry[:, :], -BIG))
                link(nc.vector.tensor_tensor_scan(carry[:, 1:P + 1], keyT[:, :], tailsT[:, :], -BIG, ALU.add, ALU.max))
                nc.vector.tensor_tensor(tailsT[:, :], carry[:, 0:P], pen[:, :], ALU.add).then_inc(pe_go, 1)
                dve.wait_ge(pe_ok, 2)
                link(nc.vector.tensor_copy(carried[:, :], ps[:, 0:8]))
                for h in range(HEADS):
                    link(nc.vector.tensor_scalar(cand[:, :], first[:, :], carried[:, h:h + 1], None, ALU.add))
                    last = nc.vector.tensor_tensor(flip[:, :, h], scores[:, h, :], cand[:, :], ALU.max)
                    link(last)
                nc.vector.tensor_copy(tails[:, 0:1], tails[:, 1:2]).then_inc(ready, 1)
                dve.wait_ge(node_got, 16 * NB)
                link(nc.vector.tensor_tensor(z[:, :, :], k.sdm[:, 0:NB, 0:HEADS], peak[:, :, :], ALU.add))
                link(nc.vector.scalar_tensor_tensor(out=peak[:, :, :], in0=z[:, :, :], scalar=0.2, in1=z[:, :, :],
                                                    op0=ALU.mult, op1=ALU.max))
                nc.vector.tensor_copy(k.sdm[:, 0:NB, HEADS:2 * HEADS], peak[:, :, :])
                nc.vector.memset(k.sdm[:, NB, :], 0.0)

            @block.tensor
            def _(pe):
                pe.wait_ge(keys_in, 32)
                pl.tensor_first(pe)
                staged(pe, GROUPS, RING, lambda g_, b, i: pl.tensor_step(pe, g_, b), drain=1)
                pe.wait_ge(pe_go, 1)
                nc.tensor.transpose(ps[0:8, 0:P], tails[:, 0:8], k.ident[:, :])
                nc.tensor.transpose(ps[0:8, P:2 * P], tails[:, 8:16], k.ident[:, :])
                nc.tensor.transpose(ps[0:8, 2 * P:3 * P], carried[:, :], k.ident[:, :]).then_inc(pe_ok, 1)
                pe.wait_ge(pe_go, 2)
                nc.tensor.transpose(ps[:, 0:8], tailsT[:, :], k.ident[0:8, 0:8]).then_inc(pe_ok, 1)


class Gather:

    def __init__(self, nc, k, ph, graph, table, width):
        self.nc, self.graph, self.table, self.width = nc, graph, table, width
        self.k = k
        self.slot = [ph.sb(f"slot{b}", [P, TGRP], I32) for b in range(TRING)]
        self.got = [ph.sb(f"got{b}", [P, TGRP, width]) for b in range(TRING)]
        self.member = [ph.sb(f"member{b}", [P, TGRP, P]) for b in range(TRING)]
        self.slots_ok, self.adding = ph.sem("slots_ok"), ph.sem("adding")
        self.members_ok, self.summed = ph.sem("members_ok"), ph.sem("summed")
        self.pool_going = ph.sem("pool_going")
        self.fetched = [[ph.sem(f"fetched{b}_{j}") for j in range(TGRP)] for b in range(TRING)]

    def fetch(self, pool):
        def group(g, b):
            pool.wait_ge(self.slots_ok, g + 1)
            wait_past(pool, self.summed, g - (TRING - 1))
            pool.sem_inc(self.pool_going, 1)
            for j in range(TGRP):
                pool.indirect_dma_start(out=self.got[b][:, j, :], out_offset=None, in_=self.table,
                                        in_offset=bass.IndirectOffsetOnAxis(ap=self.slot[b][:, j:j + 1], axis=0)).then_inc(self.fetched[b][j], 16)

        rounds(pool, TGROUPS, TRING, group)

    def arrived(self, eng, b, i):
        for j in range(TGRP):
            eng.wait_ge(self.fetched[b][j], i * 16 + 16)

    def indices(self, act, g, b, i):
        if not isinstance(i, int) or i:
            for j in range(TGRP):
                act.wait_ge(self.fetched[b][j], i * 16)
        self.nc.scalar.copy(self.slot[b][:, :], self.graph.other[:, bass.ds(g * TGRP, TGRP)]).then_inc(self.slots_ok, 1)

    def members(self, g, b):
        return self.nc.vector.tensor_tensor(
            self.member[b][:, :, :], self.k.ramp[:, 0:P].unsqueeze(1).to_broadcast([P, TGRP, P]),
            self.graph.local[:, bass.ds(g * TGRP, TGRP)].unsqueeze(2).to_broadcast([P, TGRP, P]), ALU.is_equal)

    def total(self, g, b, ps_sum):
        for j in range(TGRP):
            wait_past(self.nc.tensor, self.adding, (g - 1) * TGRP + j + 1)
            last = self.nc.tensor.matmul(ps_sum[j][:, 0:self.width], self.member[b][:, j, :], self.got[b][:, j, :],
                                         start=True, stop=True)
        last.then_inc(self.summed, 1)

    def blocks(self, kind, g):
        _, values = self.nc.values_load_multi_w_load_instructions(
            self.graph.block[0:1, bass.ds(g * TGRP, TGRP)], engines=[kind], min_val=0, max_val=NB,
            skip_runtime_bounds_check_because="a tile's block is the number of blocks that end before it, of NB")
        return values

    def add(self, dve, g, j, sums, blocks, ps_sum):
        wait_past(dve, self.adding, g * TGRP + j)
        into = flat(sums[:, bass.ds(blocks[j], 1), :])
        self.nc.vector.tensor_tensor(into, into, ps_sum[j][:, 0:self.width], ALU.add).then_inc(self.adding, 1)


def ring_steps(eng, step, drain=0):
    staged(eng, TGROUPS, TRING, step, drain)


def attend(nc, k):
    graph = k.graph[0]
    with Phase(nc, "attend") as ph:
        io = Gather(nc, k, ph, graph, k.hs, ROW)
        nodeT = [ph.sb(f"nodeT{b}", [P, TGRP, P]) for b in range(TRING)]
        z = [ph.sb(f"z{b}", [P, TGRP, HEADS]) for b in range(TRING)]
        ps_n = ph.ps("ps_n", [P, 512])
        ps_s = ph.ps("ps_s", [P, 512])
        ps_sum = [ph.ps(f"ps_sum{j}", [P, 512]) for j in range(TGRP)]
        turned, nodeT_ok, looked, z_ok, exp_ok, step = (ph.sem(s) for s in ("turned", "nodeT_ok", "looked", "z_ok", "exp_ok", "step"))
        weighed = ph.sem("weighed")
        cleared, returned = ph.sem("cleared"), ph.sem("returned")

        with nc.Block() as block:

            @block.sync
            def _(sp):
                sp.dma_start(k.X[:, :, :], k.parked).then_inc(returned, 16)
                sp.wait_ge(returned, 16)

            @block.gpsimd
            def _(pool):
                io.fetch(pool)

            @block.scalar
            def _(act):
                def turn(g, b):
                    act.wait_ge(turned, g + 1)
                    nc.scalar.copy(nodeT[b][:, :, :].rearrange("p t n -> p (t n)"), ps_n[:, :]).then_inc(nodeT_ok, 1)

                def group(g, b, i):
                    if has(g + 1, TGROUPS):
                        turn(g + 1, (b + 1) % TRING)
                    if has(g + 3, TGROUPS):
                        io.indices(act, g + 3, (b + 3) % TRING, i + (b + 3) // TRING)
                    act.wait_ge(z_ok, g + 1)
                    nc.scalar.activation(io.got[b][:, :, D:ROW], z[b][:, :, :], ACT.Exp).then_inc(exp_ok, 1)

                for b in range(3):
                    io.indices(act, b, b, 0)
                turn(0, 0)
                ring_steps(act, group)

            @block.tensor
            def _(pe):
                def turn(g, b):
                    pe.wait_ge(io.members_ok, g + 1)
                    wait_past(pe, nodeT_ok, g)
                    for j in range(TGRP):
                        last = nc.tensor.transpose(ps_n[:, j * P:(j + 1) * P], io.member[b][:, j, :], k.ident[:, :])
                    last.then_inc(turned, 1)

                def look(g, b):
                    blocks = io.blocks(mybir.EngineType.PE, g)
                    pe.wait_ge(nodeT_ok, g + 1)
                    wait_past(pe, z_ok, g)
                    for j in range(TGRP):
                        last = nc.tensor.matmul(ps_s[:, j * 16:(j + 1) * 16], nodeT[b][:, j, :],
                                                flat(k.sdm[:, bass.ds(blocks[j], 1), :]), start=True, stop=True)
                    last.then_inc(looked, 1)

                def group(g, b, i):
                    if has(g + 1, TGROUPS):
                        turn(g + 1, (b + 1) % TRING)
                    if has(g - 2, TGROUPS):
                        pe.wait_ge(weighed, g - 1)
                        io.total(g - 2, (b - 2) % TRING, ps_sum)
                    if has(g + 1, TGROUPS):
                        look(g + 1, (b + 1) % TRING)

                turn(0, 0)
                look(0, 0)
                ring_steps(pe, group, drain=2)

            @block.vector
            def _(dve):
                nc.vector.memset(k.sums[:, :, :], 0.0).then_inc(cleared, 1)
                dve.wait_ge(cleared, 1)

                def group(g, b, i):
                    here, before, adds = has(g, TGROUPS), has(g - 1, TGROUPS), has(g - 3, TGROUPS)
                    s = ps_s[:, 0:TGRP * 16].rearrange("p (t a h) -> p t a h", t=TGRP, a=2)
                    if adds:
                        blocks = io.blocks(mybir.EngineType.DVE, g - 3)
                        dve.wait_ge(io.summed, g - 2)
                        io.add(dve, g - 3, 0, k.sums, blocks, ps_sum)
                    if has(g + 2, TGROUPS):
                        io.members(g + 2, (b + 2) % TRING).then_inc(io.members_ok, 1)
                    if adds:
                        io.add(dve, g - 3, 1, k.sums, blocks, ps_sum)
                    if here:
                        io.arrived(dve, b, i)
                        dve.wait_ge(looked, g + 1)
                        first = nc.vector.tensor_tensor(z[b][:, :, :], s[:, :, 0, :], io.got[b][:, :, D:ROW], ALU.add)
                        first.then_inc(step, 1)
                    if adds:
                        io.add(dve, g - 3, 2, k.sums, blocks, ps_sum)
                    if here:
                        dve.wait_ge(step, g * 2 + 1)
                        second = nc.vector.scalar_tensor_tensor(out=z[b][:, :, :], in0=z[b][:, :, :], scalar=0.2, in1=z[b][:, :, :],
                                                                op0=ALU.mult, op1=ALU.max)
                        second.then_inc(step, 1)
                    if adds:
                        io.add(dve, g - 3, 3, k.sums, blocks, ps_sum)
                    if here:
                        dve.wait_ge(step, g * 2 + 2)
                        nc.vector.tensor_tensor(z[b][:, :, :], z[b][:, :, :], s[:, :, 1, :], ALU.subtract).then_inc(z_ok, 1)
                    if before:
                        c = (b - 1) % TRING
                        dve.wait_ge(exp_ok, g)
                        rows = io.got[c][:, :, 0:D].rearrange("p t (h d) -> p t h d", h=HEADS)
                        nc.vector.tensor_tensor(rows, rows, io.got[c][:, :, D:ROW].unsqueeze(3).to_broadcast([P, TGRP, HEADS, HD]),
                                                ALU.mult).then_inc(weighed, 1)

                for g in range(2):
                    io.members(g, g).then_inc(io.members_ok, 1)
                ring_steps(dve, group, drain=3)


def route(nc, k):
    with Phase(nc, "route") as ph:
        gate = ph.sb("gate", [P, DC, EXPERTS])
        gate_b = ph.sb("gate_b", [1, EXPERTS])
        inv = [ph.sb(f"inv{b}", [P, HEADS]) for b in range(2)]
        share = [ph.sb(f"share{b}", [P, D]) for b in range(2)]
        zero = ph.sb("zero", [P, D])
        logits = ph.sb("logits", [P, NB, EXPERTS])
        tok = Tokens(nc, k, ph)
        ps_l = [ph.ps(f"ps_l{b}", [P, 512]) for b in range(2)]
        pairs = Scatter(nc, k, ph, SENT_FROM[0], *SENT[0])
        loaded, attn, zeroed, cleared = ph.sem("loaded"), ph.sem("attn"), ph.sem("zeroed"), ph.sem("cleared")
        with nc.Block() as block:

            @block.sync
            def _(sp):
                load_matrix(sp, loaded, gate[:, :, :], k.gate_w)
                sp.dma_start(gate_b[:, :], k.gate_b.rearrange("(a n) -> a n", a=1)).then_inc(loaded, 16)
                sp.wait_ge(zeroed, 1)
                full = EXPERTS * EROWS // P
                sp.dma_start(k.expert_rows[0:full * P, :].rearrange("(t p) d -> p t d", p=P),
                             zero[:, :].unsqueeze(1).to_broadcast([P, full, D])).then_inc(cleared, 16)
                rest = EXPERTS * EROWS - full * P
                if rest:
                    sp.dma_start(k.expert_rows[full * P:full * P + rest, :], zero[0:rest, :]).then_inc(cleared, 16)
                pairs.feed(sp)
                sp.wait_ge(cleared, 32 if rest else 16)

            @block.gpsimd
            def _(pool):
                pairs.run(pool)

            @block.vector
            def _(dve):
                nc.vector.memset(zero[:, :], 0.0).then_inc(zeroed, 1)

                def attended(i, t, b, rows):
                    link = Chain(dve, attn, t * 4)
                    s = flat(k.sums[:, bass.ds(t, 1), :])
                    x = flat(k.X[:, bass.ds(t, 1), :])
                    link(nc.vector.tensor_scalar(inv[b][:, :], s[:, D:ROW], 1e-16, None, ALU.add))
                    link(nc.vector.reciprocal(inv[b][:, :], inv[b][:, :]))
                    link(nc.vector.tensor_tensor(share[b][:, :].rearrange("p (h d) -> p h d", h=HEADS),
                                                 s[:, 0:D].rearrange("p (h d) -> p h d", h=HEADS),
                                                 inv[b][:, :].unsqueeze(2).to_broadcast([P, HEADS, HD]), ALU.mult))
                    link(nc.vector.tensor_tensor(x, x, share[b][:, :], ALU.add))

                def post(i, t, b, rows):
                    return nc.vector.tensor_copy(flat(logits[:, bass.ds(t, 1), :]), ps_l[b][:, 0:EXPERTS])

                tok.vector(dve, post, attended)

            @block.scalar
            def _(act):
                tok.scalar(act)

            @block.tensor
            def _(pe):
                pe.wait_ge(loaded, 32)

                def project(i, t, b, rows):
                    for c in range(DC):
                        nc.tensor.matmul(ps_l[b][:, 0:EXPERTS], tok.xnT[b][:, c, :], gate[:, c, :], start=(c == 0), stop=False)
                    return nc.tensor.matmul(ps_l[b][:, 0:EXPERTS], k.ones[0:1, :], gate_b[:, :], start=False, stop=True)

                tok.tensor(pe, project)

        chain, shifted, exp_ok, marks_ok, counted = (ph.sem(s) for s in ("chain", "shifted", "exp_ok", "marks_ok", "counted"))
        places_ok, spread = ph.sem("places_ok"), ph.sem("spread")
        E3 = [P, NB, EXPERTS]
        top, total, expert, pos, kept, a, c = (ph.sb(s, [P, NB]) for s in ("top", "total", "expert", "pos", "kept", "a", "c"))
        prob, marks, tot, scan = (ph.sb(s, E3) for s in ("prob", "marks", "tot", "scan"))
        place = ph.sb("place", [P, NB], I32)
        ramp8 = k.ramp[:, 0:EXPERTS].unsqueeze(1).to_broadcast(E3)

        def wide(v):
            return v[:, :].unsqueeze(2).to_broadcast(E3)

        with nc.Block() as block:

            @block.scalar
            def _(act):
                act.wait_ge(shifted, 1)
                nc.scalar.activation(prob[:, :, :], logits[:, :, :], ACT.Exp).then_inc(exp_ok, 1)

            @block.tensor
            def _(pe):
                pe.wait_ge(marks_ok, 1)
                m = marks[:, :, :].rearrange("p t e -> p (t e)")
                nc.tensor.matmul(ps_l[0][:, 0:NB * EXPERTS], k.upper[:, :], m, start=True, stop=True)
                nc.tensor.matmul(ps_l[1][:, 0:NB * EXPERTS], k.ones[:, :], m, start=True, stop=True).then_inc(counted, 1)

            @block.vector
            def _(dve):
                link = Chain(dve, chain)
                v = nc.vector
                link(v.tensor_reduce(top[:, :], logits[:, :, :], AX.X, ALU.max))
                v.tensor_tensor(logits[:, :, :], logits[:, :, :], wide(top), ALU.subtract).then_inc(shifted, 1)
                dve.wait_ge(exp_ok, 1)
                link(v.tensor_reduce(total[:, :], prob[:, :, :], AX.X, ALU.add))
                link(v.tensor_reduce(top[:, :], prob[:, :, :], AX.X, ALU.max))
                link(v.tensor_tensor(marks[:, :, :], prob[:, :, :], wide(top), ALU.is_equal))
                link(v.scalar_tensor_tensor(out=marks[:, :, :], in0=marks[:, :, :], scalar=-float(EXPERTS), in1=ramp8,
                                            op0=ALU.mult, op1=ALU.add))
                link(v.tensor_reduce(expert[:, :], marks[:, :, :], AX.X, ALU.min))
                link(v.tensor_scalar(expert[:, :], expert[:, :], float(EXPERTS), None, ALU.add))
                link(v.tensor_tensor(marks[:, :, :], ramp8, wide(expert), ALU.is_equal))
                v.tensor_tensor(marks[:, :, :], marks[:, :, :], wide(k.valid), ALU.mult).then_inc(marks_ok, 1)
                link(v.reciprocal(total[:, :], total[:, :]))
                link(v.tensor_tensor(top[:, :], top[:, :], total[:, :], ALU.mult))
                dve.wait_ge(counted, 1)
                link(v.tensor_copy(tot[:, :, :].rearrange("p t e -> p (t e)"), ps_l[1][:, 0:NB * EXPERTS]))
                for e in range(EXPERTS):
                    v.tensor_tensor_scan(scan[:, :, e], k.ones[:, 0:NB], tot[:, :, e], 0.0, ALU.mult, ALU.add)
                link(v.tensor_copy(a[:, :], k.ones[:, 0:NB]))
                link(v.tensor_tensor(scan[:, :, :], scan[:, :, :], tot[:, :, :], ALU.subtract))
                link(v.tensor_tensor(scan[:, :, :].rearrange("p t e -> p (t e)"), scan[:, :, :].rearrange("p t e -> p (t e)"),
                                     ps_l[0][:, 0:NB * EXPERTS], ALU.add))
                link(v.tensor_tensor(scan[:, :, :], scan[:, :, :], marks[:, :, :], ALU.mult))
                link(v.tensor_reduce(pos[:, :], scan[:, :, :], AX.X, ALU.add))
                link(v.tensor_scalar(kept[:, :], pos[:, :], float(CAP), None, ALU.is_lt))
                link(v.tensor_tensor(k.weight[:, :], top[:, :], kept[:, :], ALU.mult))
                link(v.scalar_tensor_tensor(out=a[:, :], in0=expert[:, :], scalar=float(EROWS), in1=pos[:, :], op0=ALU.mult, op1=ALU.add))
                link(v.tensor_scalar(c[:, :], k.token[:, :], float(EXPERTS * EROWS), None, ALU.add))
                link(v.tensor_tensor(a[:, :], a[:, :], c[:, :], ALU.subtract))
                link(v.tensor_tensor(a[:, :], a[:, :], kept[:, :], ALU.mult))
                link(v.tensor_tensor(a[:, :], a[:, :], c[:, :], ALU.add))
                v.tensor_copy(place[:, :], a[:, :]).then_inc(places_ok, 1)
                link(v.tensor_scalar(pos[:, :], pos[:, :], float(CAP - 1), None, ALU.min))
                link(v.scalar_tensor_tensor(out=pos[:, :], in0=expert[:, :], scalar=float(EROWS), in1=pos[:, :], op0=ALU.mult, op1=ALU.add))
                v.tensor_copy(k.source[:, :], pos[:, :])

            @block.gpsimd
            def _(pool):
                pool.wait_ge(places_ok, 1)
                spread_rows(pool, k, k.expert_rows, place, spread)


def spread_rows(pool, k, table, place, sem):
    for t in range(NB):
        rows = P if t < NB - 1 else LAST
        pool.indirect_dma_start(out=table, out_offset=bass.IndirectOffsetOnAxis(ap=place[0:rows, t:t + 1], axis=0),
                                in_=k.XN[0:rows, t, :], in_offset=None).then_inc(sem, 16)
    pool.wait_ge(sem, 16 * NB)


def feed_forward(nc, k, name, rows_in, rows_out, width, experts, per_expert, func, w1, b1, w2, b2, edges=False):
    TOKS = [(m * P, min(P, width - m * P)) for m in range(-(-width // P))]
    NT = len(TOKS)
    sets = min(2, experts)
    turns = experts // sets
    LOADS = 32 if width % P else 16
    GI = sets * per_expert
    with Phase(nc, name) as ph:
        sw1 = [ph.sb(f"w1_{s}", [P, DC, FF]) for s in range(sets)]
        sw2 = [ph.sb(f"w2_{s}", [P, FC, D]) for s in range(sets)]
        sb1 = [ph.sb(f"b1_{s}", [P, FC]) for s in range(sets)]
        sb2 = [ph.sb(f"b2_{s}", [P, D]) for s in range(sets)]
        x = ph.sb("x", [P, NT, D])
        xT = ph.sb("xT", [P, DC, width])
        hT = ph.sb("hT", [P, FC, width])
        y = ph.sb("y", [P, NT, D])
        ps_x = [ph.ps(f"ps_x{c}", [P, 512]) for c in range(DC)]
        ps_h = [ph.ps(f"ps_h{q}", [P, 512]) for q in range(2)]
        ps_y = [ph.ps(f"ps_y{q}", [P, 512]) for q in range(2)]
        weights = [ph.sem(f"weights{s}") for s in range(sets)]
        x_in, turned, xT_ok, hid, relu_ok, y_ps, y_ok, y_out = (
            ph.sem(s) for s in ("x_in", "turned", "xT_ok", "hid", "relu_ok", "y_ps", "y_ok", "y_out"))

        def turn_of(eng, step, head, i):
            for s in range(sets):
                if head:
                    head(i, s)
                for h in range(per_expert):
                    q = s * per_expert + h
                    step(i * GI + q, i, s, q)

        def loop(eng, step, head=None):
            turn_of(eng, step, head, 0)
            if turns > 2:
                with eng.Fori(1, turns - 1, 1) as i:
                    turn_of(eng, step, head, i)
            if turns > 1:
                turn_of(eng, step, head, turns - 1)

        if edges:
            pairs = Scatter(nc, k, ph, SENT_FROM[1], *SENT[1])

        with nc.Block() as block:

            @block.sync
            def _(sp):
                def load_weights(i, s):
                    if not isinstance(i, int) or i:
                        sp.wait_ge(y_ok, (i - 1) * (GI * NT) + (s + 1) * per_expert * NT)
                    e = i * sets + s
                    sp.dma_start(sw1[s][:, :, :], w1(e).rearrange("(c p) n -> p c n", p=P)).then_inc(weights[s], 16)
                    sp.dma_start(sw2[s][:, :, :], w2(e).rearrange("(c p) n -> p c n", p=P)).then_inc(weights[s], 16)
                    sp.dma_start(sb1[s][:, :], b1(e).rearrange("(f p) -> p f", p=P), allow_slow_non_contiguous=True).then_inc(weights[s], 16)
                    sp.dma_start(sb2[s][:, :], b2(e).partition_broadcast(P)).then_inc(weights[s], 16)

                def load_rows(g):
                    wait_past(sp, turned, g)
                    n = width // P
                    sp.dma_start(x[:, 0:n, :], rows_in[bass.ds(g * width, n * P), :].rearrange("(m p) d -> p m d", p=P)).then_inc(x_in, 16)
                    if width % P:
                        sp.dma_start(x[0:width % P, n, :], rows_in[bass.ds(g * width + n * P, width % P), :]).then_inc(x_in, 16)

                def store(g):
                    sp.wait_ge(y_ok, g * NT + NT)
                    n = width // P
                    sp.dma_start(rows_out[bass.ds(g * width, n * P), :].rearrange("(m p) d -> p m d", p=P), y[:, 0:n, :]).then_inc(y_out, 16)
                    if width % P:
                        sp.dma_start(rows_out[bass.ds(g * width + n * P, width % P), :], y[0:width % P, n, :]).then_inc(y_out, 16)

                def group(g, i, s, q):
                    load_rows(g)
                    if edges:
                        pairs.load(sp, g, q % 2, i * (GI // 2) + q // 2)
                    if not isinstance(g, int) or g:
                        store(g - 1)

                loop(sp, group, load_weights)
                store(turns * GI - 1)
                sp.wait_ge(y_out, turns * GI * LOADS)

            if edges:
                @block.gpsimd
                def _(pool):
                    pairs.run(pool)

            @block.tensor
            def _(pe):
                def turn(g):
                    pe.wait_ge(x_in, g * LOADS + LOADS)
                    wait_past(pe, xT_ok, g)
                    for c in range(DC):
                        for m, (at, n) in enumerate(TOKS):
                            last = nc.tensor.transpose(ps_x[c][:, at:at + n], x[0:n, m, c * P:(c + 1) * P], k.ident[0:n, 0:n])
                    last.then_inc(turned, 1)

                def group(g, i, s, q):
                    pe.wait_ge(weights[s], i * 64 + 64)
                    pe.wait_ge(xT_ok, g + 1)
                    for f in range(FC):
                        wait_past(pe, relu_ok, g * FC + (f - 1))
                        for c in range(DC):
                            last = nc.tensor.matmul(ps_h[f % 2][:, 0:width], sw1[s][:, c, f * P:(f + 1) * P], xT[:, c, :],
                                                    start=(c == 0), stop=(c == DC - 1))
                        last.then_inc(hid, 1)
                    if has(g + 1, turns * GI):
                        turn(g + 1)
                    pe.wait_ge(relu_ok, g * FC + FC)
                    for m, (at, n) in enumerate(TOKS):
                        wait_past(pe, y_ok, g * NT + (m - 1))
                        for f in range(FC):
                            last = nc.tensor.matmul(ps_y[m % 2][0:n, 0:D], hT[:, f, at:at + n], sw2[s][:, f, :],
                                                    start=(f == 0), stop=(f == FC - 1))
                        last.then_inc(y_ps, 1)

                turn(0)
                loop(pe, group)

            @block.scalar
            def _(act):
                def group(g, i, s, q):
                    act.wait_ge(weights[s], i * 64 + 64)
                    wait_past(act, y_ps, g * NT)
                    for f in range(FC):
                        act.wait_ge(hid, g * FC + f + 1)
                        nc.scalar.activation(hT[:, f, :], ps_h[f % 2][:, 0:width], func, bias=sb1[s][:, f:f + 1]).then_inc(relu_ok, 1)

                loop(act, group)

            @block.vector
            def _(dve):
                def take(g):
                    dve.wait_ge(turned, g + 1)
                    wait_past(dve, hid, g * FC)
                    for c in range(DC):
                        last = nc.vector.tensor_copy(xT[:, c, :], ps_x[c][:, 0:width])
                    last.then_inc(xT_ok, 1)

                def group(g, i, s, q):
                    if has(g + 1, turns * GI):
                        take(g + 1)
                    wait_past(dve, y_out, g * LOADS)
                    for m, (at, n) in enumerate(TOKS):
                        dve.wait_ge(y_ps, g * NT + m + 1)
                        nc.vector.tensor_tensor(y[0:n, m, :], ps_y[m % 2][0:n, 0:D], sb2[s][0:n, :], ALU.add).then_inc(y_ok, 1)

                take(0)
                loop(dve, group)


def graph_tables(nc, k):
    k.own = k.keep_own()
    KW = 128
    FMAX = 3.4028234663852886e38
    with Phase(nc, "l1") as ph:
        wcat = ph.sb("wcat", [P, DC, KW + GH])
        wq, wv = ph.sb("wq", [P, DC, KW]), ph.sb("wv", [P, DC, KW])
        wout = ph.sb("wout", [P, D])
        keys = ph.sb("keys", [P, NB, KW])
        kmax = ph.sb("kmax", [P, KW])
        slot = [ph.sb(f"slot{b}", [P, 1], I32) for b in range(2)]
        got = [ph.sb(f"got{b}", [P, D]) for b in range(2)]
        fin, ind = ph.sb("fin", [P, D]), ph.sb("ind", [P, 3, D])
        tok = Tokens(nc, k, ph)
        ps_k = [ph.ps(f"ps_k{b}", [P, 512]) for b in range(2)]
        ps_m, ps_g = ph.ps("ps_m", [P, 512]), ph.ps("ps_g", [P, 512])
        ps_d = ph.ps("ps_d", [P, 512])
        loaded, root, deg = ph.sem("loaded"), ph.sem("root"), ph.sem("deg")
        slot_ok = ph.sem("slot_ok")
        got_ok, got_used = ([ph.sem(f"{s}{b}") for b in range(2)] for s in ("got_ok", "got_used"))
        stored = ph.sem("stored")
        adding, pool_going = ph.sem("adding"), ph.sem("pool_going")
        pairs = Scatter(nc, k, ph, SENT_FROM[2], *SENT[2])

        with nc.Block() as block:

            @block.sync
            def _(sp):
                load_matrix(sp, loaded, wcat[:, :, 0:KW], k.W_qkv[:, KW:2 * KW])
                load_matrix(sp, loaded, wcat[:, :, KW:KW + GH], k.gcn_W1)
                load_matrix(sp, loaded, wq[:, :, :], k.W_qkv[:, 0:KW])
                load_matrix(sp, loaded, wv[:, :, :], k.W_qkv[:, 2 * KW:3 * KW])
                sp.dma_start(wout[:, :], k.W_out).then_inc(loaded, 16)
                sp.dma_start(k.mixb[:, :], k.b_out.rearrange("(a n) -> a n", a=1)).then_inc(loaded, 16)

                pairs.feed(sp)
                sp.wait_ge(tok.dve_done[0], PAIRS + 1)
                sp.wait_ge(tok.dve_done[1], PAIRS)
                table = k.gcn_table[0]
                sp.dma_start(table[0:(NB - 1) * P, :].rearrange("(t p) d -> p t d", p=P), k.own[:, 0:NB - 1, :]).then_inc(stored, 16)
                sp.dma_start(table[(NB - 1) * P:N, :], k.own[0:LAST, NB - 1, :]).then_inc(stored, 16)
                sp.wait_ge(stored, 32)

            @block.gpsimd
            def _(pool):
                def fetch(i, t, b, rows):
                    wait_past(pool, got_used[b], i)
                    pool.sem_inc(pool_going, 1)
                    pool.tensor_copy(slot[b][:, :], k.source[:, bass.ds(t, 1)]).then_inc(slot_ok, 1)
                    pool.wait_ge(slot_ok, t + 1)
                    pool.sem_inc(pool_going, 1)
                    pool.indirect_dma_start(out=got[b][:, :], out_offset=None, in_=k.expert_out,
                                            in_offset=bass.IndirectOffsetOnAxis(ap=slot[b][:, :], axis=0)).then_inc(got_ok[b], 16)
                    pairs.send(pool, t, b, i)

                tok.blocks(pool, fetch)
                pairs.send(pool, NB, 1, PAIRS)
                with pool.Fori(PAIRS + 1, NB, 1) as i:
                    for b in range(2):
                        pairs.send(pool, i * 2 + b, b, i)
                pairs.left(pool)

            @block.vector
            def _(dve):
                v = nc.vector
                v.memset(kmax[:, :], -BIG)
                v.tensor_scalar(k.dinv[:, :], k.graph[1].count[:, :], 1.0, None, ALU.add).then_inc(deg, 1)
                dve.wait_ge(root, 1)
                v.reciprocal(k.dinv[:, :], k.dinv[:, :]).then_inc(deg, 1)
                dve.wait_ge(deg, 2)

                def mixed(i, t, b, rows):
                    dve.wait_ge(got_ok[b], i * 16 + 16)
                    link = Chain(dve, adding, t * 7)
                    x = flat(k.X[:, bass.ds(t, 1), :])
                    link(v.tensor_scalar(got[b][:, :], got[b][:, :], k.weight[:, bass.ds(t, 1)], None, ALU.mult))
                    link(v.tensor_scalar(fin[:, :], got[b][:, :], -FMAX, FMAX, ALU.max, ALU.min))
                    v.tensor_tensor(ind[:, 0, :], got[b][:, :], fin[:, :], ALU.is_equal)
                    v.tensor_tensor(ind[:, 1, :], got[b][:, :], fin[:, :], ALU.is_gt)
                    link(v.tensor_tensor(ind[:, 2, :], got[b][:, :], fin[:, :], ALU.is_lt))
                    link(v.tensor_tensor(fin[:, :], fin[:, :], ind[:, 0, :], ALU.mult))
                    link(v.tensor_tensor(ind[:, 1, :], ind[:, 1, :], ind[:, 2, :], ALU.subtract))
                    link(v.scalar_tensor_tensor(out=fin[:, :], in0=ind[:, 1, :], scalar=1.0e4, in1=fin[:, :], op0=ALU.mult, op1=ALU.add))
                    link(v.tensor_tensor(x, x, fin[:, :], ALU.add))
                    v.tensor_copy(ind[:, 0, 0:1], k.ones[:, 0:1]).then_inc(got_used[b], 1)

                def post(i, t, b, rows):
                    v.tensor_scalar(flat(k.own[:, bass.ds(t, 1), :]), ps_k[b][:, KW:KW + GH], k.dinv[:, bass.ds(t, 1)], None, ALU.mult)
                    v.tensor_copy(flat(keys[:, bass.ds(t, 1), :]), ps_k[b][:, 0:KW])
                    wait_past(dve, tok.dve_done[1 - b], i + b)
                    return v.tensor_tensor(kmax[0:rows, :], kmax[0:rows, :], ps_k[b][0:rows, 0:KW], ALU.max)

                tok.vector(dve, post, mixed)

            @block.scalar
            def _(act):
                act.wait_ge(deg, 1)
                nc.scalar.activation(k.dinv[:, :], k.dinv[:, :], ACT.Sqrt).then_inc(root, 1)
                tok.scalar(act)

            @block.tensor
            def _(pe):
                pe.wait_ge(loaded, 16 * 6)

                def project(i, t, b, rows):
                    for c in range(DC):
                        last = nc.tensor.matmul(ps_k[b][:, 0:KW + GH], tok.xnT[b][:, c, :], wcat[:, c, :],
                                                start=(c == 0), stop=(c == DC - 1))
                    return last

                tok.tensor(pe, project)

        chain, pe_step, diag_ok, exp_ok, exp_used, shifted, copied = (
            ph.sem(s) for s in ("chain", "pe_step", "diag_ok", "exp_ok", "exp_used", "shifted", "copied"))
        kd, ek = [tok.xn[b][:, 0:KW] for b in range(2)], [got[b][:, 0:KW] for b in range(2)]
        peak, diag, rden = ph.sb("peak", [P, 1]), ph.sb("diag", [P, P]), ph.sb("rden", [P, 1])
        gram, gramT, ctxT, wqT, folded = ind[:, 0, :], ph.sb("gramT", [P, DC, KW]), ph.sb("ctxT", [P, KW]), ph.sb("wqT", [P, DC, P]), fin
        HW = 32
        den_row, den_col = ph.sem("den_row"), ph.sem("den_col")
        with nc.Block() as block:

            @block.tensor
            def _(pe):
                nc.tensor.transpose(ps_m[:, 0:P], kmax[:, :], k.ident[:, :]).then_inc(pe_step, 1)
                pe.wait_ge(diag_ok, 1)
                nc.tensor.matmul(ps_m[:, 0:KW], k.ones[:, :], diag[:, :], start=True, stop=True).then_inc(pe_step, 1)

                def product(n, b, t, rows, start):
                    pe.wait_ge(exp_ok, n + 1)
                    nc.tensor.matmul(ps_g[:, 0:D], ek[b][0:rows, :], flat(k.XN[0:rows, bass.ds(t, 1), :]),
                                     start=start, stop=False, skip_group_check=True)
                    nc.tensor.matmul(ps_d[0:1, 0:KW], k.ones[0:rows, 0:1], ek[b][0:rows, :],
                                     start=start, stop=False, skip_group_check=True).then_inc(exp_used, 1)

                product(0, 0, NB - 1, LAST, True)

                def both(i):
                    product(i * 2 + 1, 1, i * 2, P, False)
                    product(i * 2 + 2, 0, i * 2 + 1, P, False)

                each_pair(pe, both)
                pe.wait_ge(den_row, 1)
                nc.tensor.matmul(ps_m[:, 0:1], ctxT[0:1, 0:KW], k.ones[0:1, 0:1], start=True, stop=True).then_inc(den_col, 1)
                pe.wait_ge(copied, 1)
                for c in range(DC):
                    nc.tensor.transpose(ps_m[:, c * P:(c + 1) * P], gram[:, c * P:(c + 1) * P], k.ident[:, :])
                for c in range(DC):
                    last = nc.tensor.transpose(ps_m[:, (DC + c) * P:(DC + c + 1) * P], wq[:, c, :], k.ident[:, :])
                last.then_inc(pe_step, 1)
                pe.wait_ge(copied, 2)
                for c in range(DC):
                    last = nc.tensor.matmul(ps_k[0][:, 0:KW], wv[:, c, :], gramT[:, c, :], start=(c == 0), stop=(c == DC - 1))
                last.then_inc(pe_step, 1)
                pe.wait_ge(copied, 3)
                nc.tensor.matmul(ps_k[1][:, 0:D], ctxT[:, :], wout[:, :], start=True, stop=True).then_inc(pe_step, 1)
                pe.wait_ge(copied, 4)
                for c in range(DC):
                    last = nc.tensor.matmul(ps_m[:, c * D:(c + 1) * D], wqT[:, c, :], folded[:, :], start=True, stop=True)
                last.then_inc(pe_step, 1)

            @block.vector
            def _(dve):
                v = nc.vector
                link = Chain(dve, chain)
                dve.wait_ge(pe_step, 1)
                link(v.tensor_reduce(peak[:, :], ps_m[:, 0:P], AX.X, ALU.max))
                v.tensor_scalar(diag[:, :], k.ident[:, :], peak[:, :], None, ALU.mult).then_inc(diag_ok, 1)
                dve.wait_ge(pe_step, 2)
                link(v.tensor_copy(kmax[:, :], ps_m[:, 0:KW]))

                def shift(n, b, t, rows):
                    wait_past(dve, exp_ok, n - 1)
                    v.tensor_tensor(kd[b][0:rows, :], flat(keys[0:rows, bass.ds(t, 1), :]), kmax[0:rows, :],
                                    ALU.subtract).then_inc(shifted, 1)

                shift(0, 0, NB - 1, LAST)

                def both(i):
                    shift(i * 2 + 1, 1, i * 2, P)
                    shift(i * 2 + 2, 0, i * 2 + 1, P)

                each_pair(dve, both)
                dve.wait_ge(exp_used, NB)
                v.tensor_copy(ctxT[0:1, 0:KW], ps_d[0:1, 0:KW]).then_inc(den_row, 1)
                dve.wait_ge(den_col, 1)
                link(v.reciprocal(rden[:, :], ps_m[:, 0:1]))
                v.tensor_scalar(gram[:, :], ps_g[:, 0:D], rden[:, :], None, ALU.mult).then_inc(copied, 1)
                link(v.memset(ctxT[:, :], 0.0))
                dve.wait_ge(pe_step, 3)
                v.tensor_copy(gramT[:, :, :].rearrange("p c n -> p (c n)"), ps_m[:, 0:D])
                v.tensor_copy(wqT[:, :, :].rearrange("p c n -> p (c n)"), ps_m[:, D:2 * D]).then_inc(copied, 1)
                dve.wait_ge(pe_step, 4)
                for h in range(KW // HW):
                    r = slice(h * HW, (h + 1) * HW)
                    last = v.tensor_copy(ctxT[r, r], ps_k[0][r, r])
                last.then_inc(copied, 1)
                dve.wait_ge(pe_step, 5)
                v.tensor_scalar(folded[:, :], ps_k[1][:, 0:D], HW ** -0.5, None, ALU.mult).then_inc(copied, 1)
                dve.wait_ge(pe_step, 6)
                v.tensor_copy(k.mixw[:, :, :].rearrange("p c n -> p (c n)"), ps_m[:, :])

            @block.scalar
            def _(act):
                def exps(n, b, rows):
                    act.wait_ge(shifted, n + 1)
                    wait_past(act, exp_used, n - 1)
                    nc.scalar.activation(ek[b][0:rows, :], kd[b][0:rows, :], ACT.Exp).then_inc(exp_ok, 1)

                exps(0, 0, LAST)

                def both(i):
                    exps(i * 2 + 1, 1, P)
                    exps(i * 2 + 2, 0, P)

                each_pair(act, both)

    add_mix(nc, k, "l1mix")


def convolve(nc, k, n):
    graph = k.graph[1]
    with Phase(nc, f"conv{n}") as ph:
        io = Gather(nc, k, ph, graph, k.gcn_table[n], GH)
        ps_sum = [ph.ps(f"ps_sum{j}", [P, 512]) for j in range(TGRP)]
        cleared = ph.sem("cleared")

        with nc.Block() as block:

            @block.gpsimd
            def _(pool):
                io.fetch(pool)

            @block.scalar
            def _(act):
                ring_steps(act, lambda g, b, i: io.indices(act, g, b, i))

            @block.tensor
            def _(pe):
                def group(g, b, i):
                    io.arrived(pe, b, i)
                    pe.wait_ge(io.members_ok, g + 1)
                    io.total(g, b, ps_sum)

                ring_steps(pe, group)

            @block.vector
            def _(dve):
                nc.vector.memset(k.sums64[:, :, :], 0.0).then_inc(cleared, 1)
                dve.wait_ge(cleared, 1)

                def group(g, b, i):
                    adds = has(g - 1, TGROUPS)
                    if adds:
                        blocks = io.blocks(mybir.EngineType.DVE, g - 1)
                        dve.wait_ge(io.summed, g)
                    for j in range(TGRP):
                        if adds:
                            io.add(dve, g - 1, j, k.sums64, blocks, ps_sum)
                        if j == 0 and has(g + 2, TGROUPS):
                            io.members(g + 2, (b + 2) % TRING).then_inc(io.members_ok, 1)

                for g in range(2):
                    io.members(g, g).then_inc(io.members_ok, 1)
                ring_steps(dve, group, drain=1)


def hidden(nc, k):
    with Phase(nc, "hidden") as ph:
        bias = ph.sb("bias", [P, GH])
        loaded, chain, stored = ph.sem("loaded"), ph.sem("chain"), ph.sem("stored")
        W3 = [P, NB, GH]
        with nc.Block() as block:

            @block.vector
            def _(dve):
                v, link = nc.vector, Chain(dve, chain)
                s, scale = k.sums64[:, 0:NB, :], k.dinv[:, :].unsqueeze(2).to_broadcast(W3)
                dve.wait_ge(loaded, 16)
                link(v.tensor_tensor(s, s, k.own[:, :, :], ALU.add))
                link(v.tensor_tensor(s, s, scale, ALU.mult))
                link(v.tensor_tensor(s, s, bias[:, :].unsqueeze(1).to_broadcast(W3), ALU.add))
                link(v.tensor_scalar(s, s, 0.0, None, ALU.max))
                link(v.tensor_tensor(k.own[:, :, :], s, scale, ALU.mult))

            @block.sync
            def _(sp):
                sp.dma_start(bias[:, :], k.gcn_b1.partition_broadcast(P)).then_inc(loaded, 16)
                sp.wait_ge(chain, 5)
                table = k.gcn_table[1]
                sp.dma_start(table[0:(NB - 1) * P, :].rearrange("(t p) d -> p t d", p=P), k.own[:, 0:NB - 1, :]).then_inc(stored, 16)
                sp.dma_start(table[(NB - 1) * P:N, :], k.own[0:LAST, NB - 1, :]).then_inc(stored, 16)
                sp.wait_ge(stored, 32)


def convolved(nc, k):
    with Phase(nc, "tanh") as ph:
        w2 = ph.sb("w2", [GH + 1, D])
        aT = [ph.sb(f"aT{b}", [GH + 1, P]) for b in range(2)]
        a = [ph.sb(f"a{b}", [P, GH]) for b in range(2)]
        th = [ph.sb(f"th{b}", [P, D]) for b in range(2)]
        ps_t = [ph.ps(f"ps_t{b}", [P, 512]) for b in range(2)]
        ps_y = [ph.ps(f"ps_y{b}", [P, 512]) for b in range(2)]
        loaded, chain, pe_going, ones_ok = (ph.sem(s) for s in ("loaded", "chain", "pe_going", "ones_ok"))
        a_ok, turned, aT_ok, y_ok, th_ok, done = (ph.sem(s) for s in ("a_ok", "turned", "aT_ok", "y_ok", "th_ok", "done"))

        def blocks(eng, step):
            step(0, 0)
            step(1, 1)
            with eng.Fori(1, PAIRS, 1) as i:
                for b in range(2):
                    step(i * 2 + b, b)
            step(NB - 1, 0)

        with nc.Block() as block:

            @block.sync
            def _(sp):
                sp.dma_start(w2[0:GH, :], k.gcn_W2).then_inc(loaded, 16)
                sp.dma_start(w2[GH:GH + 1, :], k.gcn_b2.rearrange("(a n) -> a n", a=1)).then_inc(loaded, 16)

            @block.vector
            def _(dve):
                v = nc.vector
                for b in range(2):
                    v.memset(aT[b][GH:GH + 1, :], 1.0).then_inc(ones_ok, 1)

                def first(t, b):
                    link = Chain(dve, chain, t * 1)
                    wait_past(dve, turned, t - 1)
                    link(v.tensor_tensor(a[b][:, :], flat(k.sums64[:, bass.ds(t, 1), :]), flat(k.own[:, bass.ds(t, 1), :]), ALU.add))
                    v.tensor_scalar(a[b][:, :], a[b][:, :], k.dinv[:, bass.ds(t, 1)], None, ALU.mult).then_inc(a_ok, 1)

                def last(t, b):
                    dve.wait_ge(th_ok, t + 1)
                    x = flat(k.X[:, bass.ds(t, 1), :])
                    v.tensor_tensor(x, x, th[b][:, :], ALU.add).then_inc(done, 1)

                first(0, 0)
                first(1, 1)
                last(0, 0)
                with dve.Fori(1, PAIRS, 1) as i:
                    first(i * 2, 0)
                    last(i * 2 - 1, 1)
                    first(i * 2 + 1, 1)
                    last(i * 2, 0)
                first(NB - 1, 0)
                last(NB - 2, 1)
                last(NB - 1, 0)

            @block.scalar
            def _(act):
                def step(t, b):
                    act.wait_ge(turned, t + 1)
                    wait_past(act, y_ok, t - 1)
                    nc.scalar.copy(aT[b][0:GH, :], ps_t[b][0:GH, 0:P]).then_inc(aT_ok, 1)
                    act.wait_ge(y_ok, t + 1)
                    wait_past(act, done, t - 1)
                    nc.scalar.activation(th[b][:, :], ps_y[b][:, 0:D], ACT.Tanh).then_inc(th_ok, 1)

                blocks(act, step)

            @block.tensor
            def _(pe):
                pe.wait_ge(loaded, 32)
                pe.wait_ge(ones_ok, 2)

                def step(t, b):
                    pe.wait_ge(a_ok, t + 1)
                    wait_past(pe, aT_ok, t - 1)
                    pe.sem_inc(pe_going, 1)
                    nc.tensor.transpose(ps_t[b][0:GH, 0:P], a[b][:, :], k.ident[:, :]).then_inc(turned, 1)
                    pe.wait_ge(aT_ok, t + 1)
                    wait_past(pe, th_ok, t - 1)
                    nc.tensor.matmul(ps_y[b][:, 0:D], aT[b][:, :], w2[:, :], start=True, stop=True).then_inc(y_ok, 1)

                blocks(pe, step)


def choose(nc, k):
    with Phase(nc, "choose") as ph:
        wr, br = ph.sb("wr", [P, DC, 1]), ph.sb("br", [1, 1])
        zero = ph.sb("zero", [P, D])
        score = ph.sb("score", [P, NB])
        tok = Tokens(nc, k, ph)
        ps_w = [ph.ps(f"ps_w{b}", [P, 512]) for b in range(2)]
        loaded, zeroed, cleared, summed = ph.sem("loaded"), ph.sem("zeroed"), ph.sem("cleared"), ph.sem("summed")
        with nc.Block() as block:

            @block.sync
            def _(sp):
                load_columns(sp, loaded, wr[:, :, 0], k.wr.rearrange("d a -> (d a)"))
                sp.dma_start(br[:, :], k.br.rearrange("(a n) -> a n", a=1)).then_inc(loaded, 16)
                sp.wait_ge(zeroed, 1)
                sp.dma_start(k.chosen_rows[TOPK:CROWS, :], zero[0:CROWS - TOPK, :]).then_inc(cleared, 16)
                sp.wait_ge(cleared, 16)

            @block.vector
            def _(dve):
                nc.vector.memset(zero[:, :], 0.0).then_inc(zeroed, 1)

                def post(i, t, b, rows):
                    x = flat(k.X[:, bass.ds(t, 1), :])
                    dve.wait_ge(tok.xn_saved[b], i + 1)
                    nc.vector.tensor_tensor(x, x, flat(k.XN[:, bass.ds(t, 1), :]), ALU.add)
                    return nc.vector.tensor_copy(score[:, bass.ds(t, 1)], ps_w[b][:, 0:1])

                tok.vector(dve, post)

            @block.scalar
            def _(act):
                tok.scalar(act)

            @block.tensor
            def _(pe):
                pe.wait_ge(loaded, 16 * (DC + 1))

                def project(i, t, b, rows):
                    for c in range(DC):
                        nc.tensor.matmul(ps_w[b][:, 0:1], tok.xnT[b][:, c, :], wr[:, c, :], start=(c == 0), stop=False)
                    return nc.tensor.matmul(ps_w[b][:, 0:1], k.ones[0:1, :], br[:, :], start=False, stop=True)

                tok.tensor(pe, project)

        BITS = 32
        chain, counted, ready, places_ok, spread = (ph.sem(s) for s in ("chain", "counted", "ready", "places_ok", "spread"))
        u, bit, cand, flip, least, many, take = (ph.sb(s, [P, 1], I32) for s in ("u", "bit", "cand", "flip", "least", "many", "take"))
        part = ph.sb("part", [P, 1])
        least_f = least[:, :].bitcast(F32)
        hit, above, equal, before, tot, scan, chosen, a, c = (
            ph.sb(s, [P, NB]) for s in ("hit", "above", "equal", "before", "tot", "scan", "chosen", "a", "c"))
        room = ph.sb("room", [P, 1])
        place = ph.sb("place", [P, NB], I32)
        ps_c, ps_p, ps_t = tok.ps_turn[0], ps_w[0], ps_w[1]
        STEPS = 8
        with nc.Block() as block:

            @block.tensor
            def _(pe):
                with pe.Fori(0, BITS, 1) as i:
                    pe.wait_ge(ready, i + 1)
                    nc.tensor.matmul(ps_c[:, 0:1], k.ones[:, :], part[:, :], start=True, stop=True).then_inc(counted, 1)
                pe.wait_ge(ready, BITS + 1)
                nc.tensor.matmul(ps_c[:, 0:1], k.ones[:, :], part[:, :], start=True, stop=True)
                nc.tensor.matmul(ps_p[:, 0:NB], k.upper[:, :], equal[:, :], start=True, stop=True)
                nc.tensor.matmul(ps_t[:, 0:NB], k.ones[:, :], equal[:, :], start=True, stop=True).then_inc(counted, 1)
                pe.wait_ge(ready, BITS + 2)
                nc.tensor.matmul(ps_p[:, 0:NB], k.upper[:, :], chosen[:, :], start=True, stop=True)
                nc.tensor.matmul(ps_t[:, 0:NB], k.ones[:, :], chosen[:, :], start=True, stop=True).then_inc(counted, 1)

            @block.vector
            def _(dve):
                v = nc.vector
                link = Chain(dve, chain)

                def to_float(link, src):
                    link(v.tensor_scalar(flip[:, :], src[:, :], 31, -1, ALU.arith_shift_right, ALU.bitwise_xor))
                    link(v.scalar_tensor_tensor(out=least[:, :], in0=flip[:, :], scalar=-2147483648, in1=src[:, :],
                                                op0=ALU.bitwise_or, op1=ALU.bitwise_xor))

                link(v.tensor_tensor(score[:, :], score[:, :], k.valid[:, :], ALU.mult))
                link(v.tensor_scalar(a[:, :], k.valid[:, :], -1.0, 3.0e38, ALU.add, ALU.mult))
                link(v.tensor_tensor(score[:, :], score[:, :], a[:, :], ALU.add))
                link(v.memset(u[:, :], 0))
                link(v.memset(bit[:, :], -2147483648))
                with dve.Fori(0, BITS, 1) as i:
                    loop_link = Chain(dve, chain, i * STEPS + 5)
                    loop_link(v.tensor_tensor(cand[:, :], u[:, :], bit[:, :], ALU.bitwise_or))
                    to_float(loop_link, cand)
                    v.tensor_scalar(hit[:, :], score[:, :], least_f, 0.0, ALU.is_ge, ALU.add, accum_out=part[:, :]).then_inc(ready, 1)
                    dve.wait_ge(counted, i + 1)
                    loop_link(v.tensor_scalar(many[:, :], ps_c[:, 0:1], float(TOPK), None, ALU.is_ge))
                    loop_link(v.tensor_scalar(take[:, :], many[:, :], 31, 31, ALU.logical_shift_left, ALU.arith_shift_right))
                    loop_link(v.tensor_tensor(take[:, :], take[:, :], bit[:, :], ALU.bitwise_and))
                    loop_link(v.tensor_tensor(u[:, :], u[:, :], take[:, :], ALU.bitwise_or))
                    loop_link(v.tensor_single_scalar(bit[:, :], bit[:, :], 1, ALU.logical_shift_right))
                    assert loop_link.n == STEPS
                link = Chain(dve, chain, BITS * STEPS + 5)
                to_float(link, u)
                link(v.tensor_scalar(above[:, :], score[:, :], least_f, 0.0, ALU.is_gt, ALU.add, accum_out=part[:, :]))
                v.scalar_tensor_tensor(out=equal[:, :], in0=score[:, :], scalar=least_f, in1=k.valid[:, :],
                                       op0=ALU.is_equal, op1=ALU.mult).then_inc(ready, 1)

                def ahead(n, marks):
                    dve.wait_ge(counted, n)
                    link(v.tensor_copy(tot[:, :], ps_t[:, 0:NB]))
                    link(v.tensor_tensor_scan(scan[:, :], k.ones[:, 0:NB], tot[:, :], 0.0, ALU.mult, ALU.add))
                    link(v.tensor_tensor(scan[:, :], scan[:, :], tot[:, :], ALU.subtract))
                    link(v.tensor_tensor(before[:, :], scan[:, :], ps_p[:, 0:NB], ALU.add))

                ahead(BITS + 1, equal)
                link(v.tensor_scalar(room[:, :], ps_c[:, 0:1], -1.0, float(TOPK), ALU.mult, ALU.add))
                link(v.scalar_tensor_tensor(out=a[:, :], in0=before[:, :], scalar=room[:, 0:1], in1=equal[:, :], op0=ALU.is_lt, op1=ALU.mult))
                v.tensor_tensor(chosen[:, :], above[:, :], a[:, :], ALU.add).then_inc(ready, 1)
                ahead(BITS + 2, chosen)
                link(v.tensor_tensor(k.weight[:, :], score[:, :], chosen[:, :], ALU.mult))
                link(v.tensor_tensor(a[:, :], before[:, :], chosen[:, :], ALU.mult))
                v.tensor_copy(k.source[:, :], a[:, :])
                link(v.tensor_scalar(c[:, :], k.token[:, :], float(CROWS), None, ALU.add))
                link(v.tensor_tensor(before[:, :], before[:, :], c[:, :], ALU.subtract))
                link(v.tensor_tensor(before[:, :], before[:, :], chosen[:, :], ALU.mult))
                link(v.tensor_tensor(before[:, :], before[:, :], c[:, :], ALU.add))
                v.tensor_copy(place[:, :], before[:, :]).then_inc(places_ok, 1)

            @block.gpsimd
            def _(pool):
                pool.wait_ge(places_ok, 1)
                spread_rows(pool, k, k.chosen_rows, place, spread)


def finish(nc, k):
    with Phase(nc, "finish") as ph:
        ROUND = 7
        assert NB % ROUND == 0
        got = [ph.sb(f"got{b}", [P, D]) for b in range(ROUND)]
        got_ok, used, stored = [ph.sem(f"got_ok{b}") for b in range(ROUND)], ph.sem("used"), ph.sem("stored")

        with nc.Block() as block:

            @block.gpsimd
            def _(pool):
                for t in range(NB):
                    if t >= ROUND:
                        pool.wait_ge(used, t - ROUND + 1)
                    pool.indirect_dma_start(out=got[t % ROUND][:, :], out_offset=None, in_=k.chosen_out,
                                            in_offset=bass.IndirectOffsetOnAxis(ap=k.source[:, t:t + 1], axis=0)).then_inc(got_ok[t % ROUND], 16)

            @block.vector
            def _(dve):
                with dve.Fori(0, NB // ROUND, 1) as i:
                    for b in range(ROUND):
                        dve.wait_ge(got_ok[b], i * 16 + 16)
                        x = flat(k.X[:, bass.ds(i * ROUND + b, 1), :])
                        nc.vector.scalar_tensor_tensor(out=x, in0=got[b][:, :], scalar=k.weight[:, bass.ds(i * ROUND + b, 1)],
                                                       in1=x, op0=ALU.mult, op1=ALU.add).then_inc(used, 1)

            @block.sync
            def _(sp):
                def store(t, blocks):
                    sp.dma_start(k.out[bass.ds(t * P, blocks * P), :].rearrange("(t p) d -> p t d", p=P),
                                 k.X[:, bass.ds(t, blocks), :]).then_inc(stored, 16)

                with sp.Fori(0, NB // ROUND - 1, 1) as i:
                    sp.wait_ge(used, i * ROUND + ROUND)
                    store(i * ROUND, ROUND)
                sp.wait_ge(used, NB)
                store(NB - ROUND, ROUND - 1)
                sp.dma_start(k.out[(NB - 1) * P:N, :], k.X[0:LAST, NB - 1, :]).then_inc(stored, 16)
                sp.wait_ge(stored, 16 * (NB // ROUND + 1))


def gps_block_kernel(
    nc, x, src, dst, gnn_W, gnn_a, W_qk, b_qk, W_v, b_v, gamma, beta, gate_w, gate_b, w1, b1, w2, b2, gcn_W1,
    gcn_b1, gcn_W2, gcn_b2, W_qkv, W_out, b_out, wr, br, mw1, mb1, mw2, mb2, out,
):
    k = Buffers()
    k.x = x
    k.src = src
    k.dst = dst
    k.gnn_W = gnn_W
    k.gnn_a = gnn_a
    k.W_qk = W_qk
    k.b_qk = b_qk
    k.W_v = W_v
    k.b_v = b_v
    k.gamma = gamma
    k.beta = beta
    k.gate_w = gate_w
    k.gate_b = gate_b
    k.w1 = w1
    k.b1 = b1
    k.w2 = w2
    k.b2 = b2
    k.gcn_W1 = gcn_W1
    k.gcn_b1 = gcn_b1
    k.gcn_W2 = gcn_W2
    k.gcn_b2 = gcn_b2
    k.W_qkv = W_qkv
    k.W_out = W_out
    k.b_out = b_out
    k.wr = wr
    k.br = br
    k.mw1 = mw1
    k.mb1 = mb1
    k.mw2 = mw2
    k.mb2 = mb2
    k.out = out
    with ExitStack() as keep:
        def sb(name, shape, dt=F32):
            return keep.enter_context(nc.sbuf_tensor(name, shape, dt))

        def dram(name, shape, dt=F32):
            return nc.dram_tensor(name, shape, dt).ap()

        k.ident = sb("ident", [P, P])
        k.upper = sb("upper", [P, P])
        k.ones = sb("ones", [P, P])
        k.ident_b = sb("ident_b", [P, P], BF16)
        k.ramp = sb("ramp", [P, TILES])
        k.ramp_b = sb("ramp_b", [P, P], BF16)
        k.eps = sb("eps", [P, 1])
        k.valid = sb("valid", [P, NB])
        k.token = sb("token", [P, NB])
        k.weight = sb("weight", [P, NB])
        k.dinv = sb("dinv", [P, NB])
        k.keep_own = lambda: sb("own", [P, NB, GH])
        k.source = sb("source", [P, NB], I32)
        k.sdm = sb("sdm", [P, NB + 1, 2 * HEADS])
        k.mixw = sb("mixw", [P, DC, D])
        k.mixb = sb("mixb", [1, D])
        k.graph = []
        for n in range(2):
            k.graph.append(Graph(
                table=dram(f"sorted{n}", [SLOTS, 2]), other=sb(f"other{n}", [P, TILES], I32),
                local=sb(f"local{n}", [P, TILES]), block=sb(f"block{n}", [1, TILES], I32),
                count=sb(f"count{n}", [P, NB]), last=sb(f"last{n}", [P, NB], I32)))
        k.starts = dram("starts", [NB, P])
        k.pairs = dram("pairs", [EP, ET, 2])
        k.places = dram("places", [EP, ET], I32)
        k.parked = dram("parked", [P, NB, D])
        k.peak_table = dram("peak_table", [SLOTS, HEADS])
        k.expert_rows = dram("expert_rows", [EXPERTS * EROWS + NB * P, D])
        k.expert_out = dram("expert_out", [EXPERTS * EROWS, D])
        k.chosen_rows = dram("chosen_rows", [CROWS + NB * P, D])
        k.chosen_out = dram("chosen_out", [CROWS, D])
        k.gcn_table = [dram(f"gcn_table{n}", [N, GH]) for n in range(2)]
        k.scores_table = dram("scores_table", [N, HEADS])
        k.hs = dram("hs", [N, ROW])
        constants(nc, k)
        sort_edges(nc, k)
        k.X = sb("X", [P, NB, D])
        k.work = work = sb("work", [P, (NB + 1) * ROW])
        k.XN = work[:, 0:NB * D].rearrange("p (t d) -> p t d", d=D)
        k.sums64 = work[:, 0:(NB + 1) * GH].rearrange("p (t d) -> p t d", d=GH)
        k.sums = work[:, :].rearrange("p (t d) -> p t d", d=ROW)
        load_x(nc, k)
        attention_tables(nc, k)
        park(nc, k)
        segment_peaks(nc, k)
        attend(nc, k)
        route(nc, k)
        feed_forward(nc, k, "experts", k.expert_rows, k.expert_out, EGROUP, EXPERTS, 2, ACT.Relu,
                     lambda e: k.w1[bass.ds(e, 1)].rearrange("a d f -> (a d) f"),
                     lambda e: k.b1[bass.ds(e, 1)].rearrange("a f -> (a f)"),
                     lambda e: k.w2[bass.ds(e, 1)].rearrange("a f d -> (a f) d"),
                     lambda e: k.b2[bass.ds(e, 1)].rearrange("a d -> (a d)"), edges=True)
        graph_tables(nc, k)
        tile_order(nc, k, "order1", k.graph[1])
        convolve(nc, k, 0)
        hidden(nc, k)
        convolve(nc, k, 1)
        convolved(nc, k)
        choose(nc, k)
        feed_forward(nc, k, "chosen", k.chosen_rows, k.chosen_out, CGROUP, 1, CROWS // CGROUP, ACT.Gelu_apprx_tanh,
                     lambda e: k.mw1, lambda e: k.mb1, lambda e: k.mw2, lambda e: k.mb2)
        finish(nc, k)


_ARGS = [
    "x", "src", "dst", "L0_gnn_W", "L0_gnn_a", "L0_mix_W_qk", "L0_mix_b_qk", "L0_mix_W_v", "L0_mix_b_v",
    "L0_mix_gamma", "L0_mix_beta", "L0_ffn_gate_w", "L0_ffn_gate_b", "L0_ffn_w1", "L0_ffn_b1", "L0_ffn_w2",
    "L0_ffn_b2", "L1_gnn_W1", "L1_gnn_b1", "L1_gnn_W2", "L1_gnn_b2", "L1_mix_W_qkv", "L1_mix_W_out",
    "L1_mix_b_out", "L1_ffn_wr", "L1_ffn_br", "L1_ffn_w1", "L1_ffn_b1", "L1_ffn_w2", "L1_ffn_b2",
]


def kernel(**inputs):
    import numpy as _np
    import concourse.bacc as _bacc
    from concourse import mybir as _mybir
    from concourse.bass_utils import run_bass_kernel_spmd as _run

    nc = _bacc.Bacc("TRN2", target_bir_lowering=False, num_devices=1)
    arrays, args = {}, []
    for name in _ARGS:
        a = _np.ascontiguousarray(inputs[name])
        arrays[f"in_{name}"] = a
        args.append(nc.dram_tensor(f"in_{name}", a.shape, _mybir.dt.from_np(a.dtype), kind="ExternalInput").ap())
    args.append(nc.dram_tensor("out_0", (N, D), F32, kind="ExternalOutput").ap())
    gps_block_kernel(nc, *args)
    return _run(nc, [arrays], core_ids=[0]).results[0]["out_0"]
```
